# Optimizing a Trainium2 kernel written in Bass

```python
import numpy as np
import jax
import jax.numpy as jnp

def _softmax(x, axis=-1):
    return jax.nn.softmax(x, axis=axis)

def _gelu(x):
    return jax.nn.gelu(x, approximate=True)

def _silu(x):
    return jax.nn.silu(x)

def _sigmoid(x):
    return jax.nn.sigmoid(x)

def _layernorm(x, axis=-1, eps=1e-05):
    m = jnp.mean(x, axis=axis, keepdims=True)
    v = jnp.var(x, axis=axis, keepdims=True)
    return (x - m) / jnp.sqrt(v + eps)

def _scatter_add(tgt, idx, src, axis=0):
    return tgt.at[idx].add(src)

def _segment_sum(src, seg, n):
    return jax.ops.segment_sum(src, seg, n)
kernel_name = 'mk_seq_preln_d2_jaxref_r8_210d5b'

def setup_inputs(seed: int=0):
    np.random.seed(seed)
    _w = jnp.asarray

    def _L0_attn_setup():
        import jax, jax.numpy as jnp
        import numpy as np
        key = jax.random.key(seed)
        ks = jax.random.split(key, 5)
        B, S, D = (1, 512, 256)
        H, Dh = (16, 128)
        scale = 1.0 / np.sqrt(D).astype(np.float32)
        return {'x': jax.random.normal(ks[0], (B, S, D), dtype=jnp.float32), 'W_K': jax.random.normal(ks[1], (H, Dh, D), dtype=jnp.float32) * scale, 'W_Q': jax.random.normal(ks[2], (H, Dh, D), dtype=jnp.float32) * scale, 'W_V': jax.random.normal(ks[3], (H, Dh, D), dtype=jnp.float32) * scale, 'W_O': jax.random.normal(ks[4], (D, H * Dh), dtype=jnp.float32) * scale}
    _L0_attn_in = _L0_attn_setup()

    def _L0_ffn_setup():
        import jax, jax.numpy as jnp
        import numpy as np
        B, S, H, I = (1, 64, 256, 768)

        def _quantized_matmul(x, w, scale):
            wq = w.astype(jnp.float8_e4m3fn).astype(x.dtype)
            y = jnp.einsum('bsi,io->bso', x, wq)
            return y * scale
        key = jax.random.key(seed)
        ks = jax.random.split(key, 7)
        return {'x': jax.random.normal(ks[0], (B, S, H), dtype=jnp.float32), 'gate_w': jax.random.normal(ks[1], (H, I), dtype=jnp.float32) * 0.02, 'up_w': jax.random.normal(ks[2], (H, I), dtype=jnp.float32) * 0.02, 'down_w': jax.random.normal(ks[3], (I, H), dtype=jnp.float32) * 0.02, 'gate_scale': jax.random.uniform(ks[4], (I,), dtype=jnp.float32, minval=0.5, maxval=1.5), 'up_scale': jax.random.uniform(ks[5], (I,), dtype=jnp.float32, minval=0.5, maxval=1.5), 'down_scale': jax.random.uniform(ks[6], (H,), dtype=jnp.float32, minval=0.5, maxval=1.5)}
    _L0_ffn_in = _L0_ffn_setup()

    def _L1_attn_setup():
        import jax, jax.numpy as jnp
        import numpy as np
        EMBED_DIM = 256
        NUM_HEADS = 16
        HEAD_DIM = EMBED_DIM // NUM_HEADS
        D_K = 128
        SCALE = 1.0 / float(np.sqrt(HEAD_DIM))
        LAYER_DEPTH = 6 / 12
        BATCH, SEQ = (2, 256)
        key = jax.random.key(seed)
        ks = jax.random.split(key, 8)
        return {'hidden_states': jax.random.normal(ks[0], (BATCH, SEQ, EMBED_DIM), jnp.float32), 'c_attn_w': jax.random.normal(ks[1], (EMBED_DIM, 3 * EMBED_DIM), jnp.float32) * 0.02, 'c_attn_b': jax.random.normal(ks[2], (3 * EMBED_DIM,), jnp.float32) * 0.02, 'c_proj_w': jax.random.normal(ks[3], (EMBED_DIM, EMBED_DIM), jnp.float32) * 0.02, 'c_proj_b': jax.random.normal(ks[4], (EMBED_DIM,), jnp.float32) * 0.02, 'cam_gate': jax.random.normal(ks[5], (D_K,), jnp.float32) * 0.1, 'cam_w0': jax.random.normal(ks[6], (1,), jnp.float32), 'cam_w1': jax.random.normal(ks[7], (1,), jnp.float32)}
    _L1_attn_in = _L1_attn_setup()

    def _L1_ffn_setup():
        import jax, jax.numpy as jnp
        import numpy as np
        HIDDEN = 256
        INTER = 1024
        SCALE = 64.0

        def fwht(x):
            orig_shape = x.shape
            n = orig_shape[-1]
            x = x.reshape(-1, n)
            h = 1
            while h < n:
                x = x.reshape(-1, n // (2 * h), 2, h)
                a, b = (x[:, :, 0, :], x[:, :, 1, :])
                x = jnp.stack([a + b, a - b], axis=2).reshape(-1, n)
                h *= 2
            return (x / jnp.sqrt(jnp.asarray(n, x.dtype))).reshape(orig_shape)
        key = jax.random.key(seed)
        ks = jax.random.split(key, 8)
        inp = jax.random.normal(ks[0], (4, 256, HIDDEN), dtype=jnp.float32)
        SU_ug = jnp.where(jax.random.bernoulli(ks[1], 0.5, (HIDDEN,)), 1.0, -1.0).astype(jnp.float32)
        SU_dp = jnp.where(jax.random.bernoulli(ks[2], 0.5, (INTER,)), 1.0, -1.0).astype(jnp.float32)
        Wscale_ug = jax.random.uniform(ks[3], (2 * INTER,), jnp.float32, 0.5, 1.5)
        Wscale_dp = jax.random.uniform(ks[4], (HIDDEN,), jnp.float32, 0.5, 1.5)
        W_up = jax.random.normal(ks[5], (INTER, HIDDEN), dtype=jnp.float32) * 0.02
        W_gate = jax.random.normal(ks[6], (INTER, HIDDEN), dtype=jnp.float32) * 0.02
        W_down = jax.random.normal(ks[7], (HIDDEN, INTER), dtype=jnp.float32) * 0.02
        return {'input': inp, 'SU_ug': SU_ug, 'SU_dp': SU_dp, 'Wscale_ug': Wscale_ug, 'Wscale_dp': Wscale_dp, 'W_up': W_up, 'W_gate': W_gate, 'W_down': W_down}
    _L1_ffn_in = _L1_ffn_setup()
    _d = {'L0_attn_x': _L0_attn_in['x'], 'L0_attn_W_K': _L0_attn_in['W_K'], 'L0_attn_W_Q': _L0_attn_in['W_Q'], 'L0_attn_W_V': _L0_attn_in['W_V'], 'L0_attn_W_O': _L0_attn_in['W_O'], 'L0_ffn_gate_w': _L0_ffn_in['gate_w'], 'L0_ffn_up_w': _L0_ffn_in['up_w'], 'L0_ffn_down_w': _L0_ffn_in['down_w'], 'L0_ffn_gate_scale': _L0_ffn_in['gate_scale'], 'L0_ffn_up_scale': _L0_ffn_in['up_scale'], 'L0_ffn_down_scale': _L0_ffn_in['down_scale'], 'L1_attn_c_attn_w': _L1_attn_in['c_attn_w'], 'L1_attn_c_attn_b': _L1_attn_in['c_attn_b'], 'L1_attn_c_proj_w': _L1_attn_in['c_proj_w'], 'L1_attn_c_proj_b': _L1_attn_in['c_proj_b'], 'L1_attn_cam_gate': _L1_attn_in['cam_gate'], 'L1_attn_cam_w0': _L1_attn_in['cam_w0'], 'L1_attn_cam_w1': _L1_attn_in['cam_w1'], 'L1_ffn_SU_ug': _L1_ffn_in['SU_ug'], 'L1_ffn_SU_dp': _L1_ffn_in['SU_dp'], 'L1_ffn_Wscale_ug': _L1_ffn_in['Wscale_ug'], 'L1_ffn_Wscale_dp': _L1_ffn_in['Wscale_dp'], 'L1_ffn_W_up': _L1_ffn_in['W_up'], 'L1_ffn_W_gate': _L1_ffn_in['W_gate'], 'L1_ffn_W_down': _L1_ffn_in['W_down']}
    _x0 = _d['L0_attn_x']
    _d['L0_attn_x'] = jax.random.normal(jax.random.fold_in(jax.random.key(seed), 1), (4, 256, 256), dtype=_x0.dtype)
    del _x0
    return _d

def reference(L0_attn_x, L0_attn_W_K, L0_attn_W_Q, L0_attn_W_V, L0_attn_W_O, L0_ffn_gate_w, L0_ffn_up_w, L0_ffn_down_w, L0_ffn_gate_scale, L0_ffn_up_scale, L0_ffn_down_scale, L1_attn_c_attn_w, L1_attn_c_attn_b, L1_attn_c_proj_w, L1_attn_c_proj_b, L1_attn_cam_gate, L1_attn_cam_w0, L1_attn_cam_w1, L1_ffn_SU_ug, L1_ffn_SU_dp, L1_ffn_Wscale_ug, L1_ffn_Wscale_dp, L1_ffn_W_up, L1_ffn_W_gate, L1_ffn_W_down):

    def _L0_attn_ref(x, W_K, W_Q, W_V, W_O):
        import jax, jax.numpy as jnp
        import numpy as np
        b, pos, d_model = x.shape
        d_head = W_K.shape[1]
        k = jnp.einsum('ihd,bpd->biph', W_K, x)
        q = jnp.einsum('ihd,bpd->biph', W_Q, x)
        v = jnp.einsum('ihd,bpd->biph', W_V, x)
        scores = jnp.einsum('biph,biqh->biqp', k, q)
        mask = jnp.tril(jnp.ones((pos, pos), dtype=x.dtype))
        masked = scores * mask - jnp.float32(10000000000.0) * (1.0 - mask)
        attn = jax.nn.softmax(masked / jnp.sqrt(jnp.float32(d_head)), axis=-1)
        z = jnp.einsum('biqp,biph->biqh', attn, v)
        z_flat = jnp.transpose(z, (0, 2, 1, 3)).reshape(b, pos, -1)
        out = jnp.einsum('df,bqf->bqd', W_O, z_flat)
        return out

    def _L0_ffn_ref(x, gate_w, up_w, down_w, gate_scale, up_scale, down_scale):
        import jax, jax.numpy as jnp
        import numpy as np
        B, S, H, I = (1, 64, 256, 768)

        def _quantized_matmul(x, w, scale):
            wq = w.astype(jnp.float8_e4m3fn).astype(x.dtype)
            y = jnp.einsum('bsi,io->bso', x, wq)
            return y * scale
        gate = jax.nn.silu(_quantized_matmul(x, gate_w, gate_scale))
        up = _quantized_matmul(x, up_w, up_scale)
        fuse = gate * up
        return _quantized_matmul(fuse, down_w, down_scale)

    def _L1_attn_ref(hidden_states, c_attn_w, c_attn_b, c_proj_w, c_proj_b, cam_gate, cam_w0, cam_w1):
        import jax, jax.numpy as jnp
        import numpy as np
        EMBED_DIM = 256
        NUM_HEADS = 16
        HEAD_DIM = EMBED_DIM // NUM_HEADS
        D_K = 128
        SCALE = 1.0 / float(np.sqrt(HEAD_DIM))
        LAYER_DEPTH = 6 / 12
        BATCH, SEQ = (2, 256)
        qkv = hidden_states @ c_attn_w + c_attn_b
        Q, K, V = jnp.split(qkv, 3, axis=2)
        attn_scores = jnp.einsum('bse,bte->bst', Q, K) * SCALE
        Q_cam, K_cam, V_cam = (Q[:, :, :D_K], K[:, :, :D_K], V[:, :, :D_K])
        base_A = jax.lax.stop_gradient(jax.nn.softmax(jnp.einsum('bsd,btd->bst', Q_cam, K_cam) * SCALE, axis=-1))
        layer_weight = jax.nn.sigmoid(cam_w0[0] + cam_w1[0] * LAYER_DEPTH)
        cam_ctx = jnp.einsum('bst,btd->bsd', base_A, V_cam)
        cam_bias = jnp.einsum('bsd,btd->bst', jnp.tanh(cam_ctx * cam_gate), K_cam)
        cam_bias = cam_bias * (SCALE * layer_weight)
        final_attn = jax.nn.softmax(attn_scores + cam_bias, axis=-1)
        context = jnp.einsum('bst,bte->bse', final_attn, V)
        output = context @ c_proj_w + c_proj_b
        return output

    def _L1_ffn_ref(input, SU_ug, SU_dp, Wscale_ug, Wscale_dp, W_up, W_gate, W_down):
        import jax, jax.numpy as jnp
        import numpy as np
        HIDDEN = 256
        INTER = 1024
        SCALE = 64.0

        def fwht(x):
            orig_shape = x.shape
            n = orig_shape[-1]
            x = x.reshape(-1, n)
            h = 1
            while h < n:
                x = x.reshape(-1, n // (2 * h), 2, h)
                a, b = (x[:, :, 0, :], x[:, :, 1, :])
                x = jnp.stack([a + b, a - b], axis=2).reshape(-1, n)
                h *= 2
            return (x / jnp.sqrt(jnp.asarray(n, x.dtype))).reshape(orig_shape)
        n = SU_ug.shape[0]
        x = input.reshape(-1, n)
        x = fwht(x * SU_ug) / SCALE
        x_up = x @ W_up.T * (Wscale_ug[:INTER] * SCALE)
        x_gate = x @ W_gate.T * (Wscale_ug[INTER:] * SCALE)
        x = jax.nn.silu(x_gate) * x_up
        x = fwht(x * SU_dp) / SCALE
        x = x @ W_down.T * (Wscale_dp * SCALE)
        return x.reshape(input.shape)
    x = L0_attn_x
    x = x + _L0_attn_ref(_layernorm(x, axis=-1), L0_attn_W_K, L0_attn_W_Q, L0_attn_W_V, L0_attn_W_O)
    x = x + _L0_ffn_ref(_layernorm(x, axis=-1), L0_ffn_gate_w, L0_ffn_up_w, L0_ffn_down_w, L0_ffn_gate_scale, L0_ffn_up_scale, L0_ffn_down_scale)
    x = x + _L1_attn_ref(_layernorm(x, axis=-1), L1_attn_c_attn_w, L1_attn_c_attn_b, L1_attn_c_proj_w, L1_attn_c_proj_b, L1_attn_cam_gate, L1_attn_cam_w0, L1_attn_cam_w1)
    x = x + _L1_ffn_ref(_layernorm(x, axis=-1), L1_ffn_SU_ug, L1_ffn_SU_dp, L1_ffn_Wscale_ug, L1_ffn_Wscale_dp, L1_ffn_W_up, L1_ffn_W_gate, L1_ffn_W_down)
    return x

_drawn_inputs = setup_inputs


def setup_inputs(seed=0):
    import zlib

    import numpy as np

    out = dict(_drawn_inputs(seed))
    spreads = {}
    factors = {'L0_ffn_gate_scale': 6.377,
     'L0_ffn_up_scale': 7.38,
     'L0_ffn_down_scale': 7.163,
     'L1_attn_c_attn_w': 3.206,
     'L1_attn_c_attn_b': 21.967,
     'L1_attn_c_proj_w': 3.006,
     'L1_attn_c_proj_b': 27.848,
     'L1_attn_cam_gate': 28.347,
     'L1_ffn_Wscale_ug': 4.736,
     'L1_ffn_Wscale_dp': 6.608}
    for name, (base, spread) in spreads.items():
        noise = np.random.default_rng([zlib.crc32(name.encode()), seed]).standard_normal(out[name].shape)
        drawn = base * np.exp(spread * noise) if base else spread * noise
        out[name] = jnp.asarray(drawn.astype(out[name].dtype))
    for name, factor in factors.items():
        out[name] = (out[name] * factor).astype(out[name].dtype)
    return out
```

```python
from contextlib import ExitStack

import concourse.bass as bass
from concourse import mybir

F32 = mybir.dt.float32
F32R = mybir.dt.float32r
BF16 = mybir.dt.bfloat16
I32 = mybir.dt.int32
ALU = mybir.AluOpType
ACT = mybir.ActivationFunctionType
AX_X = mybir.AxisListType.X

P = 128
BATCH, SEQ, D = 4, 256, 256
TOK = BATCH * SEQ
TILES = TOK // P
KC = D // P
HEADS, DH = 16, 128
PAIRS = HEADS // 2
UNITS = 2 * BATCH
I0 = 768
C0 = I0 // P
I1 = 1024
C1 = I1 // P
HALF = TOK // 2

QKV_COLS = 3 * KC * 2 * DH
WO_COLS = 2 * D
PAIR_COLS = QKV_COLS + WO_COLS
UG_PIECE = KC * 2 * I1 // PAIRS
WD_PIECE = C1 * D // PAIRS
Q8_PIECE = 3 * KC * I0 // PAIRS
PREP_COLS = UG_PIECE + WD_PIECE + Q8_PIECE
DCOLS = D // PAIRS

INV_SQRT_DH = 1.0 / float(DH) ** 0.5
SCALE1 = 0.25
EPS = 1e-5
FP8_MAX = 448.0
FP8_MIN_NORMAL = 2.0 ** -6
ROUND_TO_4_BITS = 1.5 * 2.0 ** 20
MASKED = -1e10

V_BQK, V_SU, V_SUDP, V_GS0, V_US0, V_WUP, V_WGATE, V_CAMG, V_W0, V_W1, V_N = (
    0, 4, 6, 14, 20, 26, 34, 42, 43, 44, 45)
R_DS, R_VB, R_PB, R_WDP = range(4)
M_ID, M_H, M_NH, M_MASK, M_N = 0, P, 2 * P, 3 * P, 3 * P + 2 * SEQ

WAVE_OF = {"gu0": 1, "down0": 2, "ln2": 3, "proj": 6, "score": 7, "turn": 8, "ctx": 9,
           "score2": 10, "turn2": 11, "mix": 12, "out": 13, "ln3": 14, "had": 15, "gu1": 16, "down1": 17}


def tail_order():
    order = [("ln1", 0), ("ln1", 1), ("ln1", 2)]
    for wave in range(max(WAVE_OF.values()) + BATCH):
        for stage in sorted(WAVE_OF, key=WAVE_OF.get, reverse=True):
            b = wave - WAVE_OF[stage]
            if 0 <= b < BATCH:
                order.append((stage, b))
            if (stage, b) == ("gu0", 0):
                order.append(("ln1", 3))
    return order


TAIL = tail_order()
IN_LAST_PAIR = 2
ROT_TILES = {"ln1": 1, "ln2": 1, "ln3": 1, "gu0": C0, "gu1": C1, "proj": 3, "ctx": 1, "mix": 1, "had": 1}


def numbering(tiles):
    first, n = {}, 0
    for stage, b in TAIL:
        if stage in tiles:
            first[stage, b] = n
            n += tiles[stage]
    return first, n


ROT, ROT_N = numbering(ROT_TILES)
GU, GU_N = numbering({"gu0": C0, "gu1": C1})
SOFT, SOFT_N = numbering({"score": 1, "score2": 1})
TURN, TURN_N = numbering({"turn": 1, "turn2": 1})
ONTO, ONTO_N = numbering({"down0": 1, "out": 1, "down1": 1})
LN, LN_N = numbering({"ln1": 1, "ln2": 1, "ln3": 1})


def build_program(nc, x_in, pair_in, prep_in, mats_in, vecs_in, rows_in, out):
    with ExitStack() as ctx:
        def sb(name, shape, dt=F32):
            return ctx.enter_context(nc.sbuf_tensor(name, shape, dt))

        def psum(name):
            return ctx.enter_context(nc.psum_tensor(name, [P, 512], F32))

        def sem(name):
            return ctx.enter_context(nc.semaphore(name))

        xres = sb("xres", [P, TILES, D])
        xt_hi = sb("xt_hi", [P, KC, TOK], F32R)
        xt_lo = sb("xt_lo", [P, KC, TOK], F32R)
        pair_raw = sb("pair_raw", [P, PAIR_COLS])
        wqkv_hi = sb("wqkv_hi", [P, 3, KC, 2 * DH], F32R)
        wqkv_lo = sb("wqkv_lo", [P, 3, KC, 2 * DH], F32R)
        wo_hi = sb("wo_hi", [P, 2, D], F32R)
        wo_lo = sb("wo_lo", [P, 2, D], F32R)
        REG = 6 * TOK
        reg_hi = sb("reg_hi", [P, REG], F32R)
        reg_lo = sb("reg_lo", [P, REG], F32R)
        prob = sb("prob", [P, 2, 512])
        probn = sb("probn", [P, 2, 512])
        pt_hi = sb("pt_hi", [P, 2, 4, P], F32R)
        pt_lo = sb("pt_lo", [P, 2, 4, P], F32R)
        z_hi = sb("z_hi", [P, 2, SEQ], F32R)
        z_lo = sb("z_lo", [P, 2, SEQ], F32R)
        q8 = sb("q8", [P, PAIRS, Q8_PIECE], F32R)
        ug_hi = sb("ug_hi", [P, PAIRS, UG_PIECE], F32R)
        ug_lo = sb("ug_lo", [P, PAIRS, UG_PIECE], F32R)
        wd_hi = sb("wd_hi", [P, C1, PAIRS, DCOLS], F32R)
        wd_lo = sb("wd_lo", [P, C1, PAIRS, DCOLS], F32R)
        prep = sb("prep", [P, PREP_COLS])
        scratch = sb("scratch", [P, Q8_PIECE])
        bfly = sb("bfly", [P, 2, WD_PIECE])
        bf_hi = sb("bf_hi", [P, WD_PIECE], F32R)
        bf_lo = sb("bf_lo", [P, WD_PIECE], F32R)
        fused = sb("fused", [P, 2, SEQ])
        xn = sb("xn", [P, 2, 2, D])
        ident = sb("ident", [P, P])
        had_p = sb("had_p", [P, P], F32R)
        had_n = sb("had_n", [P, P], F32R)
        ident_b = sb("ident_b", [P, P], BF16)
        mask_b = sb("mask_b", [P, 2, SEQ], BF16)
        vecs = sb("vecs", [P, V_N])
        rows = sb("rows", [P, 4, D])
        stats = sb("stats", [P, TILES, 6])
        mv = sb("mv", [P, TILES, 2])
        nwt = sb("nwt", [P, 4, TILES])
        cam = sb("cam", [P, 6])
        wscale = sb("wscale", [P, 2 * C1])
        rmax = sb("rmax", [P, 2 * UNITS, 2])
        nbias = sb("nbias", [P, 2 * UNITS, 2])
        rsum = sb("rsum", [P, 2 * UNITS, 2])
        rinv = sb("rinv", [P, 2 * UNITS, 2])

        bank_pj = [psum("bank_pj0"), psum("bank_pj1")]
        bank_s = [psum("bank_s0"), psum("bank_s1")]
        bank_t = psum("bank_t")
        bank_z = [psum("bank_z0"), psum("bank_z1")]
        bank_o = psum("bank_o")
        bank_rot = bank_pj + bank_s

        q_hi, q_lo = (r[:, 0:2 * TOK].rearrange("p (h t) -> p h t", h=2) for r in (reg_hi, reg_lo))
        k_hi, k_lo = (r[:, 2 * TOK:4 * TOK].rearrange("p (h t) -> p h t", h=2) for r in (reg_hi, reg_lo))
        v_hi, v_lo = (r[:, 4 * TOK:6 * TOK].rearrange("p (t e) -> p t e", t=TILES) for r in (reg_hi, reg_lo))
        q8_all = q8[:, :, :].rearrange("p a b -> p (a b)")
        gate0_w = q8_all[:, 0:KC * I0].rearrange("p (k c m) -> p k c m", k=KC, c=C0)
        up0_w = q8_all[:, KC * I0:2 * KC * I0].rearrange("p (k c m) -> p k c m", k=KC, c=C0)
        down0_w = q8_all[:, 2 * KC * I0:3 * KC * I0].rearrange("p (c m) -> p c m", c=C0)
        ug_h, ug_l = (w[:, :, :].rearrange("p a b -> p (a b)").rearrange(
            "p (k c g m) -> p k c g m", k=KC, c=C1, g=2) for w in (ug_hi, ug_lo))
        wd_h, wd_l = (w[:, :, :, :].rearrange("p c a b -> p c (a b)") for w in (wd_hi, wd_lo))
        out_v = out.rearrange("b (t p) d -> p (b t) d", p=P)
        x_v = x_in.rearrange("b (t p) d -> p (b t) d", p=P)

        q8_pow = scratch
        gate_act = scratch[:, 0:2 * SEQ].rearrange("p (a c) -> p a c", a=2)

        def f32(ap):
            return ap.bitcast(F32)

        def hidden(r, slot, chunks):
            return r[:, slot * 2 * TOK:slot * 2 * TOK + chunks * SEQ].rearrange("p (c t) -> p c t", c=chunks)

        def attn1(r, b):
            part = r[:, b * 6 * SEQ:(b + 1) * 6 * SEQ].rearrange("p (n c) -> p n c", c=SEQ)
            return part[:, 0:2], part[:, 2:4], part[:, 4:6]

        def vec(c, n=1):
            return vecs[:, c:c + n]

        def row(r, n):
            return rows[:, r, :].unsqueeze(1).broadcast_to([P, n, D])

        def rot(n):
            return bank_rot[n % 4]

        loaded_x = sem("loaded_x")
        loaded_const = sem("loaded_const")
        loaded_pair = sem("loaded_pair")
        loaded_prep = sem("loaded_prep")
        stored = sem("stored")
        consts_ready = sem("consts_ready")
        zeros_ready = sem("zeros_ready")
        dve = sem("dve")
        pool_first = sem("pool_first")
        pool_went = sem("pool_went")
        ug_hi_done = sem("ug_hi_done")
        pool_step = sem("pool_step")
        ln_done = sem("ln_done")
        lnt_ready = sem("lnt_ready")
        lnt_hi = sem("lnt_hi")
        lnt_split = sem("lnt_split")
        w_qkv = sem("w_qkv")
        wo_hi_done = sem("wo_hi_done")
        w_o = sem("w_o")
        proj_ready = sem("proj_ready")
        proj_hi = sem("proj_hi")
        proj_split = sem("proj_split")
        s_ready = sem("s_ready")
        max_done = sem("max_done")
        nbias_done = sem("nbias_done")
        exp_done = sem("exp_done")
        rinv_done = sem("rinv_done")
        norm_done = sem("norm_done")
        t_ready = sem("t_ready")
        t_hi = sem("t_hi")
        t_split = sem("t_split")
        z_ready = sem("z_ready")
        zhi_done = sem("zhi_done")
        z_split = sem("z_split")
        o_ready = sem("o_ready")
        o_added = sem("o_added")
        wdmm_ready = sem("wdmm_ready")
        bf_ready = sem("bf_ready")
        prep_q8 = sem("prep_q8")
        prep_pool = sem("prep_pool")
        wd_done = sem("wd_done")
        q8_step = sem("q8_step")
        rot_ready = sem("rot_ready")
        rot_hi = sem("rot_hi")
        rot_free = sem("rot_free")
        bias_added = sem("bias_added")
        fuse_hi = sem("fuse_hi")
        fuse_lo = sem("fuse_lo")
        camq_sum = sem("camq_sum")
        camq_hi = sem("camq_hi")
        camq_split = sem("camq_split")
        cam_arg = sem("cam_arg")
        cam_exp = sem("cam_exp")
        x_final = sem("x_final")


        N_CONST = 5
        CH = 6
        TPP = 2 * CH
        OPP = BATCH + 1
        ALL_UNITS = PAIRS * UNITS
        STEPS = UNITS + 4
        PROJ_STEPS = CH // 2
        LN1_STEP = {8: 0, 10: 1}

        def proj_dst(hi, half, n):
            q, k, v = (q_hi, k_hi, v_hi) if hi else (q_lo, k_lo, v_lo)
            if n < 4:
                return (q, k)[n // 2][:, n % 2, half * HALF:(half + 1) * HALF]
            t = half * (TILES // 2) + (n - 4) * 2
            return v[:, t:t + 2, :]

        def proj_src(n):
            bank = bank_pj[n % 2]
            return bank[:, :] if n < 4 else bank[:, :].rearrange("p (t e) -> p t e", t=2)

        def two(ap):
            return ap.rearrange("p (a c) -> p a c", a=2)

        def tokens(b):
            return slice(b * SEQ, (b + 1) * SEQ)

        block = ctx.enter_context(nc.Block())

        @block.sync
        def _(sp):
            sp.dma_start(xres[:, :, :], x_v).then_inc(loaded_x, 16)
            sp.dma_start(pair_raw[:, :], pair_in[0]).then_inc(loaded_pair, 16)
            sp.dma_start(ident[:, :], mats_in[:, M_ID:M_ID + P]).then_inc(loaded_const, 16)
            sp.dma_start(prob[:, 0, 0:2 * P], mats_in[:, M_H:M_MASK]).then_inc(loaded_const, 16)
            sp.dma_start(probn[:, 0, :], mats_in[:, M_MASK:M_N]).then_inc(loaded_const, 16)
            sp.dma_start(vecs[:, :], vecs_in).then_inc(loaded_const, 16)
            sp.dma_start(rows[:, :, :], rows_in).then_inc(loaded_const, 16)
            sp.dma_start(prep[:, :], prep_in[0]).then_inc(loaded_prep, 16)
            sp.wait_ge(w_o, 1)
            sp.dma_start(pair_raw[:, :], pair_in[1]).then_inc(loaded_pair, 16)
            with sp.Fori(0, PAIRS - 1) as i:
                sp.wait_ge(prep_q8, i + 1)
                sp.wait_ge(prep_pool, i + 1)
                sp.dma_start(prep[:, :], prep_in[i + 1]).then_inc(loaded_prep, 16)
                sp.wait_ge(w_o, i + 2)
                sp.dma_start(pair_raw[:, :], pair_in[i + 2]).then_inc(loaded_pair, 16)
            for b in range(BATCH):
                sp.wait_ge(x_final, b + 1)
                sp.dma_start(out_v[:, 2 * b:2 * b + 2, :], xres[:, 2 * b:2 * b + 2, :]).then_inc(stored, 16)
            sp.wait_ge(stored, 16 * BATCH)

        @block.tensor
        def _(pe):
            def products(dst, pairs, start=True, stop=True):
                for n, (lhs, rhs) in enumerate(pairs):
                    mm = nc.tensor.matmul(dst, lhs, rhs, start=start and n == 0, stop=stop and n == len(pairs) - 1)
                return mm

            def three(lhs, rhs):
                (lh, ll), (rh, rl) = lhs, rhs
                return [(lh, rh), (lh, rl), (ll, rh)]

            def ln_transposes(dst, b):
                for k in range(KC):
                    for t in range(2):
                        mm = nc.tensor.transpose(dst[:, k * SEQ + t * P:k * SEQ + (t + 1) * P],
                                                 xn[:, b % 2, t, k * P:(k + 1) * P], ident[:, :])
                return mm

            def rot_wait(n):
                if n >= 4:
                    pe.wait_ge(rot_free, n - 3)
                elif n >= 2:
                    pe.wait_ge(exp_done, ALL_UNITS)
                else:
                    pe.wait_ge(proj_split, PAIRS * TPP)

            def ln_tile(stage, b):
                pe.wait_ge(ln_done, BATCH + LN[stage, b] + 1)
                rot_wait(ROT[stage, b])
                ln_transposes(rot(ROT[stage, b]), b).then_inc(rot_ready, 1)

            def proj_tile(half, n):
                bank = bank_pj[n % 2]
                if n < 4:
                    which, h = n // 2, n % 2
                    mm = products(bank[:, :], [
                        p for k in range(KC) for p in three(
                            [w[:, which, k, h * DH:(h + 1) * DH] for w in (wqkv_hi, wqkv_lo)],
                            [x[:, k, half * HALF:(half + 1) * HALF] for x in (xt_hi, xt_lo)])])
                else:
                    for t in range(2):
                        t0 = half * HALF + ((n - 4) * 2 + t) * P
                        mm = products(bank[:, t * 2 * DH:(t + 1) * 2 * DH], [
                            p for k in range(KC) for p in three(
                                [x[:, k, t0:t0 + P] for x in (xt_hi, xt_lo)],
                                [w[:, 2, k, :] for w in (wqkv_hi, wqkv_lo)])])
                mm.then_inc(proj_ready, 1)

            def scores(i, j):
                b, h = divmod(j, 2)
                pe.wait_ge(proj_split, i * TPP + (4 if b < 2 else CH + 4))
                if j >= 2:
                    pe.wait_ge(exp_done, i * UNITS + j - 1)
                for qt in range(2):
                    t0 = b * SEQ + qt * P
                    dst = bank_s[j % 2][:, qt * SEQ:(qt + 1) * SEQ]
                    nc.tensor.matmul(dst, ident_b[:, :], mask_b[:, qt, :], start=True, stop=False)
                    mm = products(dst, three([q[:, h, t0:t0 + P] for q in (q_hi, q_lo)],
                                             [k[:, h, tokens(b)] for k in (k_hi, k_lo)]), start=False)
                mm.then_inc(s_ready, 1)

            def turn(i, j):
                pe.wait_ge(norm_done, i * UNITS + j + 1)
                if j >= 1:
                    pe.wait_ge(t_split, i * UNITS + j)
                for n in range(3):
                    mm = nc.tensor.transpose(bank_t[:, n * P:(n + 1) * P], probn[:, j % 2, n * P:(n + 1) * P],
                                             ident[:, :])
                mm.then_inc(t_ready, 1)

            def attend(i, j):
                b, h = divmod(j, 2)
                pe.wait_ge(proj_split, i * TPP + (CH if b < 2 else TPP))
                pe.wait_ge(t_split, i * UNITS + j + 1)
                if j >= 2:
                    pe.wait_ge(z_split, i * UNITS + j - 1)
                mm = products(bank_z[j % 2][:, 0:SEQ], [p for t in range(2) for p in three(
                    [v[:, 2 * b + t, h * DH:(h + 1) * DH] for v in (v_hi, v_lo)],
                    [pt[:, j % 2, 1:3, :] if t == 0 else pt[:, j % 2, 0:4:3, :] for pt in (pt_hi, pt_lo)])])
                mm.then_inc(z_ready, 1)

            def project(i, b):
                pe.wait_ge(z_split, i * UNITS + 2 * b + 2)
                pe.wait_ge(w_o, i + 1)
                pe.wait_ge(o_added, i * OPP + 1 + b)
                for qt in range(2):
                    mm = products(bank_o[:, qt * D:(qt + 1) * D], [p for h in range(2) for p in three(
                        [z[:, h, qt * P:(qt + 1) * P] for z in (z_hi, z_lo)],
                        [w[:, h, :] for w in (wo_hi, wo_lo)])])
                mm.then_inc(o_ready, 1)

            def wd_piece(i):
                pe.wait_ge(bf_ready, i + 1)
                products(bank_o[:, 0:WD_PIECE], [(had_p[:, :], bf_hi[:, :]), (had_p[:, :], bf_lo[:, :])])\
                    .then_inc(wdmm_ready, 1)

            def pair(i, last):
                for s in range(STEPS):
                    if 2 <= s < UNITS + 2:
                        turn(i, s - 2)
                    if s < UNITS:
                        scores(i, s)
                    if s >= 5 and s % 2 == 1:
                        project(i, (s - 5) // 2)
                    if 3 <= s < UNITS + 3:
                        attend(i, s - 3)
                    if s == 3:
                        wd_piece(i)
                    if s < PROJ_STEPS:
                        for n in (2 * s, 2 * s + 1):
                            pe.wait_ge(proj_split, i * TPP + CH + n - 1)
                            proj_tile(1, n)
                    if UNITS <= s < UNITS + PROJ_STEPS and not last:
                        if s == UNITS:
                            pe.wait_ge(w_qkv, i + 2)
                        for n in (2 * (s - UNITS), 2 * (s - UNITS) + 1):
                            pe.wait_ge(proj_split, i * TPP + TPP + n - 1)
                            proj_tile(0, n)
                    if last and s in LN1_STEP:
                        ln_tile("ln1", LN1_STEP[s])

            pe.wait_ge(loaded_const, 16 * N_CONST)
            for b in range(BATCH):
                pe.wait_ge(ln_done, b + 1)
                ln_transposes((bank_s + bank_z)[b], b).then_inc(lnt_ready, 1)
            pe.wait_ge(lnt_split, 2)
            pe.wait_ge(w_qkv, 1)
            for n in range(CH):
                if n >= 2:
                    pe.wait_ge(proj_split, n - 1)
                proj_tile(0, n)
            pe.wait_ge(lnt_split, BATCH)
            pe.wait_ge(consts_ready, 1)
            pe.wait_ge(zeros_ready, 1)
            with pe.Fori(0, PAIRS - 1) as i:
                pair(i, False)
            pair(PAIRS - 1, True)

            def x_parts(k, t):
                return [x[:, k, t] for x in (xt_hi, xt_lo)]

            def gate_up(stage, b):
                ln = ("ln1", b) if stage == "gu0" else ("had", b)
                pe.wait_ge(rot_free, ROT[ln] + 1)
                for c in range(ROT_TILES[stage]):
                    n = ROT[stage, b] + c
                    rot_wait(n)
                    for g in range(2):
                        dst = rot(n)[:, g * SEQ:(g + 1) * SEQ]
                        if stage == "gu0":
                            w = (gate0_w, up0_w)[g]
                            mm = products(dst, [(w[:, k, c, :], x) for k in range(KC) for x in x_parts(k, tokens(b))])
                        else:
                            mm = products(dst, [p for k in range(KC) for p in three(
                                [w[:, k, c, g, :] for w in (ug_h, ug_l)], x_parts(k, tokens(b)))])
                    mm.then_inc(rot_ready, 1)

            def down(stage, b):
                chunks = C0 if stage == "down0" else C1
                pe.wait_ge(fuse_lo, GU["gu0" if stage == "down0" else "gu1", b] + chunks)
                pe.wait_ge(o_added, PAIRS * OPP + ONTO[stage, b])
                h_hi, h_lo = hidden(reg_hi, b % 3, chunks), hidden(reg_lo, b % 3, chunks)
                for t in range(2):
                    ts = slice(t * P, (t + 1) * P)
                    if stage == "down0":
                        pairs = [(h[:, c, ts], down0_w[:, c, :]) for c in range(chunks) for h in (h_hi, h_lo)]
                    else:
                        pairs = [p for c in range(chunks) for p in three(
                            [h_hi[:, c, ts], h_lo[:, c, ts]], [wd_h[:, c, :], wd_l[:, c, :]])]
                    mm = products(bank_o[:, t * D:(t + 1) * D], pairs)
                mm.then_inc(o_ready, 1)

            def qkv1(b):
                pe.wait_ge(rot_free, ROT["ln2", b] + 1)
                pe.wait_ge(w_qkv, PAIRS + 1)
                for which in range(3):
                    n = ROT["proj", b] + which
                    rot_wait(n)
                    for e in range(2):
                        if which < 2:
                            pairs = [p for k in range(KC) for p in three(
                                [w[:, which, k, e * P:(e + 1) * P] for w in (wqkv_hi, wqkv_lo)],
                                x_parts(k, tokens(b)))]
                        else:
                            t0 = b * SEQ + e * P
                            pairs = [p for k in range(KC) for p in three(
                                x_parts(k, slice(t0, t0 + P)), [w[:, 2, k, :] for w in (wqkv_hi, wqkv_lo)])]
                        mm = products(rot(n)[:, e * SEQ:(e + 1) * SEQ], pairs)
                    mm.then_inc(rot_ready, 1)

            def scores1(stage, b):
                if stage == "score":
                    pe.wait_ge(rot_free, ROT["proj", b] + 3)
                else:
                    pe.wait_ge(camq_split, b + 1)
                if b >= 1:
                    pe.wait_ge(exp_done, ALL_UNITS + SOFT[stage, b - 1] + 1)
                (qh, kh, _), (ql, kl, _) = attn1(reg_hi, b), attn1(reg_lo, b)
                for qt in range(2):
                    ts = slice(qt * P, (qt + 1) * P)
                    mm = products(bank_z[stage == "score2"][:, qt * SEQ:(qt + 1) * SEQ], [
                        p for e in range(1 if stage == "score" else 2) for p in three(
                            [qh[:, e, ts], ql[:, e, ts]], [kh[:, e, :], kl[:, e, :]])])
                mm.then_inc(s_ready, 1)

            def turn1(stage, b):
                n = SOFT["score" if stage == "turn" else "score2", b]
                pe.wait_ge(norm_done, ALL_UNITS + n + 1)
                pe.wait_ge(t_split, ALL_UNITS + TURN[stage, b])
                for kt in range(2):
                    for qt in range(2):
                        mm = nc.tensor.transpose(bank_t[:, kt * SEQ + qt * P:kt * SEQ + (qt + 1) * P],
                                                 probn[:, n % 2, qt * SEQ + kt * P:qt * SEQ + (kt + 1) * P], ident[:, :])
                mm.then_inc(t_ready, 1)

            def values1(stage, b):
                m = TURN["turn" if stage == "ctx" else "turn2", b]
                n = ROT[stage, b]
                pe.wait_ge(t_split, ALL_UNITS + m + 1)
                rot_wait(n)
                (_, _, vh), (_, _, vl) = attn1(reg_hi, b), attn1(reg_lo, b)
                for e in range(1 if stage == "ctx" else 2):
                    es = slice(e * P, (e + 1) * P)
                    mm = products(rot(n)[:, e * SEQ:(e + 1) * SEQ], [p for kt in range(2) for p in three(
                        [vh[:, kt, es], vl[:, kt, es]], [pt[:, m % 2, 2 * kt:2 * kt + 2, :] for pt in (pt_hi, pt_lo)])])
                mm.then_inc(rot_ready, 1)

            def out1(b):
                pe.wait_ge(rot_free, ROT["mix", b] + 1)
                pe.wait_ge(w_o, PAIRS + 1)
                pe.wait_ge(o_added, PAIRS * OPP + ONTO["out", b])
                for qt in range(2):
                    mm = products(bank_o[:, qt * D:(qt + 1) * D], [p for e in range(2) for p in three(
                        [z[:, e, qt * P:(qt + 1) * P] for z in (z_hi, z_lo)], [w[:, e, :] for w in (wo_hi, wo_lo)])])
                mm.then_inc(o_ready, 1)

            def hadamard(b):
                n = ROT["had", b]
                pe.wait_ge(rot_free, ROT["ln3", b] + 1)
                rot_wait(n)
                for e, second in enumerate((had_p, had_n)):
                    mm = products(rot(n)[:, e * SEQ:(e + 1) * SEQ], [
                        (h[:, :], x) for k, h in enumerate((had_p, second)) for x in x_parts(k, tokens(b))])
                mm.then_inc(rot_ready, 1)

            pe.wait_ge(prep_q8, PAIRS)
            pe.wait_ge(prep_pool, PAIRS)
            for stage, b in TAIL[IN_LAST_PAIR:]:
                if stage in ("ln1", "ln2", "ln3"):
                    ln_tile(stage, b)
                elif stage in ("gu0", "gu1"):
                    gate_up(stage, b)
                elif stage in ("down0", "down1"):
                    down(stage, b)
                elif stage == "proj":
                    qkv1(b)
                elif stage in ("score", "score2"):
                    scores1(stage, b)
                elif stage in ("turn", "turn2"):
                    turn1(stage, b)
                elif stage in ("ctx", "mix"):
                    values1(stage, b)
                elif stage == "out":
                    out1(b)
                elif stage == "had":
                    hadamard(b)

        @block.scalar
        def _(act):
            def copy(dst, src, **kw):
                return nc.scalar.activation(dst, src, ACT.Copy, **kw)

            def proj_part(half, n, number):
                act.wait_ge(proj_ready, number + 1)
                copy(proj_dst(True, half, n), proj_src(n)).then_inc(proj_hi, 1)

            def exps(i, j):
                act.wait_ge(nbias_done, i * UNITS + j + 1)
                bank = bank_s[j % 2]
                for dst, src, qt in ((prob[:, j % 2, 0:P], bank[:, 0:P], 0),
                                     (prob[:, j % 2, P:3 * P], bank[:, SEQ:2 * SEQ], 1)):
                    a = nc.scalar.activation(dst, src, ACT.Exp, bias=nbias[:, j, qt:qt + 1], scale=INV_SQRT_DH,
                                             accum_out=rsum[:, j, qt:qt + 1])
                a.then_inc(exp_done, 1)

            def pair(i, last):
                for s in range(STEPS):
                    if 2 <= s < UNITS + 2:
                        j = s - 2
                        act.wait_ge(t_ready, i * UNITS + j + 1)
                        copy(pt_hi[:, j % 2, 1:4, :], bank_t[:, 0:3 * P].rearrange("p (a c) -> p a c", a=3))\
                            .then_inc(t_hi, 1)
                    if s < UNITS:
                        exps(i, s)
                    if 3 <= s < UNITS + 3:
                        j = s - 3
                        act.wait_ge(z_ready, i * UNITS + j + 1)
                        copy(z_hi[:, j % 2, :], bank_z[j % 2][:, 0:SEQ]).then_inc(zhi_done, 1)
                    if s == 4:
                        act.wait_ge(loaded_prep, 16 * (i + 1))
                        copy(ug_hi[:, i, :], prep[:, 0:UG_PIECE]).then_inc(ug_hi_done, 1)
                    if s < PROJ_STEPS:
                        for n in (2 * s, 2 * s + 1):
                            proj_part(1, n, i * TPP + CH + n)
                    if UNITS <= s < UNITS + PROJ_STEPS and not last:
                        for n in (2 * (s - UNITS), 2 * (s - UNITS) + 1):
                            proj_part(0, n, i * TPP + TPP + n)
                    if last and s in LN1_STEP:
                        x_hi("ln1", LN1_STEP[s])

            def x_hi(stage, b):
                n = ROT[stage, b]
                act.wait_ge(rot_ready, n + 1)
                copy(xt_hi[:, :, tokens(b)], two(rot(n)[:, :])).then_inc(rot_hi, 1)

            act.wait_ge(loaded_const, 16 * N_CONST)
            copy(ident_b[:, :], ident[:, :])
            copy(had_p[:, :], prob[:, 0, 0:P])
            copy(had_n[:, :], prob[:, 0, P:2 * P])
            copy(mask_b[:, :, :], two(probn[:, 0, :])).then_inc(consts_ready, 1)
            for b in range(BATCH):
                act.wait_ge(lnt_ready, b + 1)
                copy(xt_hi[:, :, tokens(b)], two((bank_s + bank_z)[b][:, :])).then_inc(lnt_hi, 1)
            for n in range(CH):
                proj_part(0, n, n)
            act.wait_ge(cam_arg, 1)
            nc.scalar.activation(cam[:, 1:2], cam[:, 0:1], ACT.Exp, scale=-1.0).then_inc(cam_exp, 1)
            with act.Fori(0, PAIRS - 1) as i:
                pair(i, False)
            pair(PAIRS - 1, True)

            def gate_up(stage, b):
                chunks = ROT_TILES[stage]
                h_hi = hidden(reg_hi, b % 3, chunks)

                def hidden_hi(c):
                    g = GU[stage, b] + c
                    act.wait_ge(rot_free, ROT[stage, b] + c + 1)
                    copy(h_hi[:, c, :], fused[:, g % 2, :]).then_inc(fuse_hi, 1)

                for c in range(chunks):
                    g, n = GU[stage, b] + c, ROT[stage, b] + c
                    act.wait_ge(rot_ready, n + 1)
                    scale = vec(V_GS0 + c) if stage == "gu0" else wscale[:, C1 + c:C1 + c + 1]
                    nc.scalar.activation(gate_act[:, g % 2, :], rot(n)[:, 0:SEQ], ACT.Silu, scale=scale)\
                        .then_inc(rot_hi, 1)
                    if c >= 1:
                        hidden_hi(c - 1)
                hidden_hi(chunks - 1)

            def soft(stage, b):
                n = SOFT[stage, b]
                bank = bank_z[stage == "score2"]
                act.wait_ge(nbias_done, ALL_UNITS + n + 1)
                for qt in range(2):
                    ts = slice(qt * SEQ, (qt + 1) * SEQ)
                    a = nc.scalar.activation(prob[:, n % 2, ts], bank[:, ts], ACT.Exp, scale=SCALE1,
                                             bias=nbias[:, UNITS + n, qt:qt + 1],
                                             accum_out=rsum[:, UNITS + n, qt:qt + 1])
                a.then_inc(exp_done, 1)

            for stage, b in TAIL[IN_LAST_PAIR:]:
                n = ROT.get((stage, b))
                if stage in ("ln1", "ln2", "had"):
                    x_hi(stage, b)
                elif stage == "ln3":
                    act.wait_ge(rot_ready, n + 1)
                    for k in range(KC):
                        a = copy(xt_hi[:, k, tokens(b)], rot(n)[:, k * SEQ:(k + 1) * SEQ], scale=vec(V_SU + k))
                    a.then_inc(rot_hi, 1)
                elif stage in ("gu0", "gu1"):
                    gate_up(stage, b)
                elif stage == "proj":
                    for which in range(3):
                        dst = attn1(reg_hi, b)[which]
                        if which < 2:
                            act.wait_ge(rot_ready, n + which + 1)
                            for e in range(2):
                                a = nc.scalar.activation(dst[:, e, :], rot(n + which)[:, e * SEQ:(e + 1) * SEQ],
                                                         ACT.Identity, bias=vec(V_BQK + 2 * which + e))
                            a.then_inc(rot_hi, 1)
                        else:
                            act.wait_ge(bias_added, b + 1)
                            copy(dst, bfly[:, :, :]).then_inc(rot_hi, 1)
                elif stage in ("score", "score2"):
                    soft(stage, b)
                elif stage in ("turn", "turn2"):
                    m = TURN[stage, b]
                    act.wait_ge(t_ready, ALL_UNITS + m + 1)
                    copy(pt_hi[:, m % 2, :, :], bank_t[:, :].rearrange("p (a c) -> p a c", a=4)).then_inc(t_hi, 1)
                elif stage == "ctx":
                    act.wait_ge(rot_ready, n + 1)
                    nc.scalar.activation(gate_act[:, 0, :], rot(n)[:, 0:SEQ], ACT.Tanh, scale=vec(V_CAMG))\
                        .then_inc(rot_hi, 1)
                    act.wait_ge(camq_sum, b + 1)
                    copy(attn1(reg_hi, b)[0][:, 0, :], gate_act[:, 1, :]).then_inc(camq_hi, 1)
                elif stage == "mix":
                    act.wait_ge(rot_ready, n + 1)
                    copy(z_hi[:, :, :], two(rot(n)[:, :])).then_inc(rot_hi, 1)

        @block.vector
        def _(v):
            taken = [0]

            def step(ins):
                taken[0] += 1
                ins.then_inc(dve, 1)
                v.wait_ge(dve, taken[0])

            def lo(dst, src, hi):
                return nc.vector.tensor_tensor(dst, src, f32(hi), ALU.subtract)

            def ln_rstd(t0, nt):
                sl = slice(t0, t0 + nt)
                for t in range(t0, t0 + nt):
                    a = nc.vector.bn_stats(stats[:, t, :], xres[:, t, :])
                step(a)
                for t in range(t0, t0 + nt):
                    a = nc.vector.bn_aggr(mv[:, t, :], stats[:, t, :])
                step(a)
                ve, y, tmp = nwt[:, 0, sl], nwt[:, 1, sl], nwt[:, 2, sl]
                step(nc.vector.tensor_scalar(ve, mv[:, sl, 1], EPS, None, ALU.add))
                step(nc.vector.tensor_scalar(y.bitcast(I32), ve.bitcast(I32), 1, None, ALU.logical_shift_right))
                step(nc.vector.tensor_scalar(y.bitcast(I32), y.bitcast(I32), -1, 0x5F3759DF, ALU.mult, ALU.add))
                for _ in range(3):
                    step(nc.vector.tensor_tensor(tmp, y, y, ALU.mult))
                    step(nc.vector.scalar_tensor_tensor(out=tmp, in0=tmp, scalar=-0.5, in1=ve, op0=ALU.mult, op1=ALU.mult))
                    step(nc.vector.scalar_tensor_tensor(out=y, in0=tmp, scalar=1.5, in1=y, op0=ALU.add, op1=ALU.mult))

            def ln_apply(b):
                for t in range(2):
                    tile = 2 * b + t
                    a = nc.vector.tensor_scalar(xn[:, b % 2, t, :], xres[:, tile, :], mv[:, tile, 0:1],
                                                nwt[:, 1, tile:tile + 1], ALU.subtract, ALU.mult)
                a.then_inc(ln_done, 1)

            def proj_part(half, n, number):
                v.wait_ge(proj_hi, number + 1)
                lo(proj_dst(False, half, n), proj_src(n), proj_dst(True, half, n)).then_inc(proj_split, 1)

            def maxima(i, j):
                v.wait_ge(s_ready, i * UNITS + j + 1)
                bank = bank_s[j % 2]
                nc.vector.reduce_max(rmax[:, j, 0:1], bank[:, 0:P], AX_X)
                nc.vector.reduce_max(rmax[:, j, 1:2], bank[:, SEQ:2 * SEQ], AX_X).then_inc(max_done, 1)
                v.wait_ge(max_done, i * UNITS + j + 1)
                nc.vector.tensor_scalar(nbias[:, j, :], rmax[:, j, :], -INV_SQRT_DH, None, ALU.mult)\
                    .then_inc(nbias_done, 1)

            def fp8_round(i):
                w = prep[:, UG_PIECE + WD_PIECE:PREP_COLS]
                n_steps = 7

                def q8s(ins, n):
                    ins.then_inc(q8_step, 1)
                    v.wait_ge(q8_step, i * n_steps + n)

                v.wait_ge(loaded_prep, 16 * (i + 1))
                q8s(nc.vector.tensor_scalar(q8_pow[:, :].bitcast(I32), w.bitcast(I32), 0x7F800000, None,
                                            ALU.bitwise_and), 1)
                q8s(nc.vector.tensor_scalar(q8_pow[:, :], q8_pow[:, :], FP8_MIN_NORMAL, ROUND_TO_4_BITS,
                                            ALU.max, ALU.mult), 2)
                q8s(nc.vector.tensor_tensor(w, w, q8_pow[:, :], ALU.add), 3)
                q8s(nc.vector.tensor_tensor(w, w, q8_pow[:, :], ALU.subtract), 4)
                q8s(nc.vector.tensor_scalar(q8_pow[:, :].bitcast(I32), w.bitcast(I32), 0x7FFFFFFF, None,
                                            ALU.bitwise_and), 5)
                q8s(nc.vector.tensor_scalar(q8_pow[:, :], q8_pow[:, :], FP8_MAX, 3e38, ALU.is_gt, ALU.mult), 6)
                q8s(nc.vector.tensor_scalar(q8_pow[:, :], q8_pow[:, :], 3e38, 0.0, ALU.mult, ALU.mult), 7)
                nc.vector.tensor_tensor(q8[:, i, :], q8_pow[:, :], w, ALU.add).then_inc(prep_q8, 1)

            def wd_piece(i):
                signed = bfly[:, 0, :].rearrange("p (c m) -> p c m", c=C1)
                v.wait_ge(wdmm_ready, i + 1)
                nc.vector.tensor_tensor(signed, bank_o[:, 0:WD_PIECE].rearrange("p (c m) -> p c m", c=C1),
                                        vec(V_SUDP, C1).unsqueeze(2).broadcast_to([P, C1, DCOLS]), ALU.mult)\
                    .then_inc(o_added, 1)
                v.wait_ge(o_added, i * OPP + 1)
                nc.vector.tensor_copy(wd_hi[:, :, i, :], signed).then_inc(wd_done, 1)
                v.wait_ge(wd_done, 2 * i + 1)
                lo(wd_lo[:, :, i, :], signed, wd_hi[:, :, i, :]).then_inc(wd_done, 1)

            def pair(i, last):
                for s in range(STEPS):
                    if 2 <= s < UNITS + 2:
                        j = s - 2
                        v.wait_ge(t_hi, i * UNITS + j + 1)
                        lo(pt_lo[:, j % 2, 1:4, :], bank_t[:, 0:3 * P].rearrange("p (a c) -> p a c", a=3),
                           pt_hi[:, j % 2, 1:4, :]).then_inc(t_split, 1)
                    if s < UNITS:
                        maxima(i, s)
                    if 3 <= s < UNITS + 3:
                        j = s - 3
                        v.wait_ge(zhi_done, i * UNITS + j + 1)
                        lo(z_lo[:, j % 2, :], bank_z[j % 2][:, 0:SEQ], z_hi[:, j % 2, :]).then_inc(z_split, 1)
                    if s == 3:
                        wd_piece(i)
                    if s >= 5 and s % 2 == 1:
                        b = (s - 5) // 2
                        v.wait_ge(o_ready, i * BATCH + b + 1)
                        nc.vector.tensor_tensor(xres[:, 2 * b:2 * b + 2, :], two(bank_o[:, :]),
                                                xres[:, 2 * b:2 * b + 2, :], ALU.add).then_inc(o_added, 1)
                        if last:
                            v.wait_ge(o_added, i * OPP + 2 + b)
                            if b >= 2:
                                v.wait_ge(rot_ready, ROT["ln1", b - 2] + 1)
                            ln_rstd(2 * b, 2)
                            ln_apply(b)
                    if s < UNITS:
                        v.wait_ge(exp_done, i * UNITS + s + 1)
                        nc.vector.reciprocal(rinv[:, s, :], rsum[:, s, :]).then_inc(rinv_done, 1)
                    if s < PROJ_STEPS:
                        for n in (2 * s, 2 * s + 1):
                            proj_part(1, n, i * TPP + CH + n)
                    if UNITS <= s < UNITS + PROJ_STEPS and not last:
                        for n in (2 * (s - UNITS), 2 * (s - UNITS) + 1):
                            proj_part(0, n, i * TPP + TPP + n)
                    if s == UNITS - 1:
                        fp8_round(i)
                    if last and s in LN1_STEP:
                        x_lo("ln1", LN1_STEP[s])

            def x_lo(stage, b):
                n = ROT[stage, b]
                v.wait_ge(rot_hi, n + 1)
                lo(xt_lo[:, :, tokens(b)], two(rot(n)[:, :]), xt_hi[:, :, tokens(b)]).then_inc(rot_free, 1)

            v.wait_ge(loaded_x, 16)
            ln_rstd(0, TILES)
            ln_apply(0)
            ln_apply(1)
            for b in range(BATCH):
                v.wait_ge(lnt_hi, b + 1)
                lo(xt_lo[:, :, tokens(b)], two((bank_s + bank_z)[b][:, :]), xt_hi[:, :, tokens(b)])\
                    .then_inc(lnt_split, 1)
                if b < 2:
                    ln_apply(b + 2)
            v.wait_ge(loaded_const, 16 * N_CONST)
            nc.vector.scalar_tensor_tensor(out=cam[:, 0:1], in0=vec(V_W1), scalar=0.5, in1=vec(V_W0),
                                           op0=ALU.mult, op1=ALU.add).then_inc(cam_arg, 1)
            for n in range(CH):
                proj_part(0, n, n)
            v.wait_ge(cam_exp, 1)
            step(nc.vector.tensor_scalar(cam[:, 2:3], cam[:, 1:2], 1.0, None, ALU.add))
            step(nc.vector.reciprocal(cam[:, 3:4], cam[:, 2:3]))
            step(nc.vector.tensor_scalar(wscale[:, :], vec(V_WUP, 2 * C1), 1.0 / 16, None, ALU.mult))
            with v.Fori(0, PAIRS - 1) as i:
                pair(i, False)
            pair(PAIRS - 1, True)

            def onto(stage, b):
                v.wait_ge(o_ready, PAIRS * BATCH + ONTO[stage, b] + 1)
                res, got, tmp = xres[:, 2 * b:2 * b + 2, :], two(bank_o[:, :]), bfly[:, :, :]
                if stage == "down0":
                    a = nc.vector.tensor_tensor(tmp, got, row(R_DS, 2), ALU.mult)
                elif stage == "out":
                    a = nc.vector.tensor_tensor(tmp, got, row(R_PB, 2), ALU.add)
                else:
                    a = nc.vector.scalar_tensor_tensor(out=tmp, in0=got, scalar=1.0 / 32, in1=row(R_WDP, 2),
                                                       op0=ALU.mult, op1=ALU.mult)
                a.then_inc(o_added, 1)
                v.wait_ge(o_added, PAIRS * OPP + ONTO[stage, b] + 1)
                a = nc.vector.tensor_tensor(res, tmp, res, ALU.add)
                if stage == "down1":
                    a.then_inc(x_final, 1)
                    return
                step(a)
                ln_rstd(2 * b, 2)
                before = {"down0": ("ln1", b + 2) if b < 2 else ("ln2", b - 2),
                          "out": ("ln2", b + 2) if b < 2 else ("ln3", b - 2)}[stage]
                v.wait_ge(rot_ready, ROT[before] + 1)
                ln_apply(b)

            def gate_up(stage, b):
                for c in range(ROT_TILES[stage]):
                    g, n = GU[stage, b] + c, ROT[stage, b] + c
                    v.wait_ge(rot_hi, n + 1)
                    if g >= 2:
                        v.wait_ge(fuse_lo, g - 1)
                    scale = vec(V_US0 + c) if stage == "gu0" else wscale[:, c:c + 1]
                    nc.vector.scalar_tensor_tensor(out=fused[:, g % 2, :], in0=rot(n)[:, SEQ:2 * SEQ], scalar=scale,
                                                   in1=gate_act[:, g % 2, :], op0=ALU.mult, op1=ALU.mult)\
                        .then_inc(rot_free, 1)

            def qkv1(b):
                for which in range(3):
                    n = ROT["proj", b] + which
                    hi, low = attn1(reg_hi, b)[which], attn1(reg_lo, b)[which]
                    if which < 2:
                        v.wait_ge(rot_hi, n + 1)
                        for e in range(2):
                            a = nc.vector.scalar_tensor_tensor(
                                out=low[:, e, :], in0=rot(n)[:, e * SEQ:(e + 1) * SEQ],
                                scalar=vec(V_BQK + 2 * which + e), in1=f32(hi[:, e, :]),
                                op0=ALU.add, op1=ALU.subtract)
                        a.then_inc(rot_free, 1)
                    else:
                        v.wait_ge(rot_ready, n + 1)
                        nc.vector.tensor_tensor(bfly[:, :, :], two(rot(n)[:, :]), row(R_VB, 2), ALU.add)\
                            .then_inc(bias_added, 1)
                        v.wait_ge(bias_added, b + 1)
                        v.wait_ge(rot_hi, n + 1)
                        lo(low, bfly[:, :, :], hi).then_inc(rot_free, 1)

            def soft(stage, b):
                n = SOFT[stage, b]
                m = UNITS + n
                v.wait_ge(s_ready, ALL_UNITS + n + 1)
                nc.vector.reduce_max(rmax[:, m, :], two(bank_z[stage == "score2"][:, :]), AX_X).then_inc(max_done, 1)
                v.wait_ge(max_done, ALL_UNITS + n + 1)
                nc.vector.tensor_scalar(nbias[:, m, :], rmax[:, m, :], -SCALE1, None, ALU.mult).then_inc(nbias_done, 1)
                v.wait_ge(exp_done, ALL_UNITS + n + 1)
                nc.vector.reciprocal(rinv[:, m, :], rsum[:, m, :]).then_inc(rinv_done, 1)

            for stage, b in TAIL[IN_LAST_PAIR:]:
                n = ROT.get((stage, b))
                if stage in ("ln1", "ln2", "had"):
                    x_lo(stage, b)
                elif stage == "ln3":
                    v.wait_ge(rot_hi, n + 1)
                    for k in range(KC):
                        a = nc.vector.scalar_tensor_tensor(
                            out=xt_lo[:, k, tokens(b)], in0=rot(n)[:, k * SEQ:(k + 1) * SEQ], scalar=vec(V_SU + k),
                            in1=f32(xt_hi[:, k, tokens(b)]), op0=ALU.mult, op1=ALU.subtract)
                    a.then_inc(rot_free, 1)
                elif stage in ("gu0", "gu1"):
                    gate_up(stage, b)
                elif stage in ("down0", "out", "down1"):
                    onto(stage, b)
                elif stage == "proj":
                    qkv1(b)
                elif stage in ("score", "score2"):
                    soft(stage, b)
                elif stage in ("turn", "turn2"):
                    m = TURN[stage, b]
                    v.wait_ge(t_hi, ALL_UNITS + m + 1)
                    lo(pt_lo[:, m % 2, :, :], bank_t[:, :].rearrange("p (a c) -> p a c", a=4), pt_hi[:, m % 2, :, :])\
                        .then_inc(t_split, 1)
                elif stage == "ctx":
                    q0_hi, q0_lo = (attn1(r, b)[0][:, 0, :] for r in (reg_hi, reg_lo))
                    total = gate_act[:, 1, :]
                    v.wait_ge(rot_hi, n + 1)
                    nc.vector.scalar_tensor_tensor(out=total, in0=gate_act[:, 0, :], scalar=cam[:, 3:4],
                                                   in1=f32(q0_hi), op0=ALU.mult, op1=ALU.add).then_inc(rot_free, 1)
                    v.wait_ge(rot_free, n + 1)
                    nc.vector.tensor_tensor(total, total, f32(q0_lo), ALU.add).then_inc(camq_sum, 1)
                    v.wait_ge(camq_hi, b + 1)
                    lo(q0_lo, total, q0_hi).then_inc(camq_split, 1)
                elif stage == "mix":
                    v.wait_ge(rot_hi, n + 1)
                    lo(z_lo[:, :, :], two(rot(n)[:, :]), z_hi[:, :, :]).then_inc(rot_free, 1)

        @block.gpsimd
        def _(pool):
            def hi(dst, src):
                return nc.gpsimd.tensor_scalar(dst, src, 1.0, 1.0, ALU.mult, ALU.mult)

            def lo(dst, src, hi_part):
                return nc.gpsimd.tensor_tensor(dst, src, f32(hi_part), ALU.subtract)

            def raw_qkv(which):
                return pair_raw[:, which * 2 * D:(which + 1) * 2 * D].rearrange("p (k m) -> p k m", k=KC)

            def raw_wo():
                return pair_raw[:, QKV_COLS:PAIR_COLS].rearrange("p (h m) -> p h m", h=2)

            N_STEPS = 7

            def wait(s, value):
                pool.wait_ge(s, value)
                pool.sem_inc(pool_went, 1)

            def pair(i):
                def pstep(ins, n):
                    ins.then_inc(pool_step, 1)
                    wait(pool_step, i * N_STEPS + n)

                def butterfly(dst, src, d):
                    s, t = (x.rearrange("p (g a x) -> p g a x", a=2, x=d * DCOLS) for x in (src, dst))
                    nc.gpsimd.tensor_tensor(t[:, :, 0, :], s[:, :, 0, :], s[:, :, 1, :], ALU.add)
                    return nc.gpsimd.tensor_tensor(t[:, :, 1, :], s[:, :, 0, :], s[:, :, 1, :], ALU.subtract)

                for j in range(UNITS):
                    wait(rinv_done, i * UNITS + j + 1)
                    nc.gpsimd.tensor_scalar(probn[:, j % 2, 0:P], prob[:, j % 2, 0:P], rinv[:, j, 0:1], 1.0,
                                            ALU.mult, ALU.mult)
                    nc.gpsimd.tensor_scalar(probn[:, j % 2, P:3 * P], prob[:, j % 2, P:3 * P], rinv[:, j, 1:2], 1.0,
                                            ALU.mult, ALU.mult).then_inc(norm_done, 1)
                    if j == 0:
                        wait(loaded_prep, 16 * (i + 1))
                        pstep(butterfly(bfly[:, 0, 0:WD_PIECE], prep[:, UG_PIECE:UG_PIECE + WD_PIECE], 1), 1)
                        pstep(butterfly(bfly[:, 1, 0:WD_PIECE], bfly[:, 0, 0:WD_PIECE], 2), 2)
                    if j == 1:
                        pstep(butterfly(bfly[:, 0, 0:WD_PIECE], bfly[:, 1, 0:WD_PIECE], 4), 3)
                        pstep(hi(bf_hi[:, :], bfly[:, 0, 0:WD_PIECE]), 4)
                        lo(bf_lo[:, :], bfly[:, 0, 0:WD_PIECE], bf_hi[:, :]).then_inc(bf_ready, 1)
                    if 3 <= j < 6:
                        which = j - 3
                        if which == 0:
                            wait(loaded_pair, 16 * (i + 2))
                            wait(proj_ready, i * TPP + TPP)
                        pstep(hi(wqkv_hi[:, which, :, :], raw_qkv(which)), 5 + which)
                        a = lo(wqkv_lo[:, which, :, :], raw_qkv(which), wqkv_hi[:, which, :, :])
                        if which == 2:
                            a.then_inc(w_qkv, 1)
                    if j == 6:
                        wait(ug_hi_done, i + 1)
                        lo(ug_lo[:, i, :], prep[:, 0:UG_PIECE], ug_hi[:, i, :]).then_inc(prep_pool, 1)
                wait(o_ready, i * BATCH + BATCH)
                hi(wo_hi[:, :, :], raw_wo()).then_inc(wo_hi_done, 1)
                wait(wo_hi_done, i + 2)
                lo(wo_lo[:, :, :], raw_wo(), wo_hi[:, :, :]).then_inc(w_o, 1)

            for r in (pt_hi, pt_lo):
                a = nc.gpsimd.memset(f32(r[:, :, 0, :]), 0.0)
            a.then_inc(zeros_ready, 1)
            pool.wait_ge(loaded_pair, 16)
            for which in range(3):
                hi(wqkv_hi[:, which, :, :], raw_qkv(which)).then_inc(pool_first, 1)
                pool.wait_ge(pool_first, which + 1)
                a = lo(wqkv_lo[:, which, :, :], raw_qkv(which), wqkv_hi[:, which, :, :])
            a.then_inc(w_qkv, 1)
            hi(wo_hi[:, :, :], raw_wo()).then_inc(wo_hi_done, 1)
            pool.wait_ge(wo_hi_done, 1)
            lo(wo_lo[:, :, :], raw_wo(), wo_hi[:, :, :]).then_inc(w_o, 1)
            with pool.Fori(0, PAIRS - 1) as i:
                pair(i)
            pair(PAIRS - 1)

            for stage, b in TAIL[IN_LAST_PAIR:]:
                if stage in ("score", "score2"):
                    n = SOFT[stage, b]
                    pool.wait_ge(rinv_done, ALL_UNITS + n + 1)
                    for qt in range(2):
                        ts = slice(qt * SEQ, (qt + 1) * SEQ)
                        a = nc.gpsimd.tensor_scalar(probn[:, n % 2, ts], prob[:, n % 2, ts],
                                                    rinv[:, UNITS + n, qt:qt + 1], 1.0, ALU.mult, ALU.mult)
                    a.then_inc(norm_done, 1)
                elif stage in ("gu0", "gu1"):
                    chunks = ROT_TILES[stage]
                    h_hi, h_lo = hidden(reg_hi, b % 3, chunks), hidden(reg_lo, b % 3, chunks)
                    for c in range(chunks):
                        g = GU[stage, b] + c
                        pool.wait_ge(fuse_hi, g + 1)
                        lo(h_lo[:, c, :], fused[:, g % 2, :], h_hi[:, c, :]).then_inc(fuse_lo, 1)


def kernel(L0_attn_x, L0_attn_W_K, L0_attn_W_Q, L0_attn_W_V, L0_attn_W_O, L0_ffn_gate_w, L0_ffn_up_w, L0_ffn_down_w,
           L0_ffn_gate_scale, L0_ffn_up_scale, L0_ffn_down_scale, L1_attn_c_attn_w, L1_attn_c_attn_b,
           L1_attn_c_proj_w, L1_attn_c_proj_b, L1_attn_cam_gate, L1_attn_cam_w0, L1_attn_cam_w1, L1_ffn_SU_ug,
           L1_ffn_SU_dp, L1_ffn_Wscale_ug, L1_ffn_Wscale_dp, L1_ffn_W_up, L1_ffn_W_gate, L1_ffn_W_down):
    args_by_name = dict(locals())
    import numpy as np
    import concourse.bacc as bacc
    from concourse import mybir as mb
    from concourse.bass_utils import run_bass_kernel_spmd

    a = {k: np.asarray(x) for k, x in args_by_name.items()}

    def chunks(w):
        return w.reshape(-1, P, w.shape[-1]).transpose(1, 0, 2)

    def pair_qkv(w):
        w = w.reshape(PAIRS, 2 * DH, KC, P).transpose(0, 3, 2, 1)
        return w.reshape(PAIRS, P, -1)

    wo = a["L0_attn_W_O"].T.reshape(PAIRS, 2, P, D).transpose(0, 2, 1, 3).reshape(PAIRS, P, -1)
    pairs = np.concatenate([pair_qkv(a["L0_attn_W_Q"]), pair_qkv(a["L0_attn_W_K"]), pair_qkv(a["L0_attn_W_V"]), wo], -1)
    c_attn = chunks(a["L1_attn_c_attn_w"]).reshape(P, KC, 3, D).transpose(0, 2, 1, 3).reshape(P, -1)
    c_proj = chunks(a["L1_attn_c_proj_w"]).reshape(P, -1)
    pairs = np.concatenate([pairs, np.concatenate([c_attn, c_proj], -1)[None]], 0)

    up, gate = (chunks(a["L1_ffn_W_" + n].T).reshape(P, KC, C1, P) for n in ("up", "gate"))
    ug = np.stack([gate, up], 3).reshape(P, PAIRS, UG_PIECE).transpose(1, 0, 2)
    wd = chunks(a["L1_ffn_W_down"].T).reshape(P, C1, PAIRS, DCOLS).transpose(2, 0, 1, 3).reshape(PAIRS, P, -1)
    q8 = np.concatenate([chunks(a["L0_ffn_" + n]).reshape(P, -1) for n in ("gate_w", "up_w", "down_w")], -1)
    q8 = q8.reshape(P, PAIRS, Q8_PIECE).transpose(1, 0, 2)
    prep = np.concatenate([ug, wd, q8], -1)

    had = np.ones((1, 1), np.float32)
    while len(had) < P:
        had = np.block([[had, had], [had, -had]])
    mask = np.where(np.arange(SEQ)[None, None, :] > np.arange(P)[:, None, None] + P * np.arange(2)[None, :, None],
                    np.float32(MASKED), np.float32(0))
    mats = np.concatenate([np.eye(P, dtype=np.float32), had, -had, mask.reshape(P, -1)], 1).astype(np.float32)

    def cols(x):
        return x.reshape(-1, P).T

    vecs = np.concatenate(
        [cols(a["L1_attn_c_attn_b"][:2 * D]), cols(a["L1_ffn_SU_ug"]), cols(a["L1_ffn_SU_dp"]),
         cols(a["L0_ffn_gate_scale"]), cols(a["L0_ffn_up_scale"]), cols(a["L1_ffn_Wscale_ug"]),
         cols(a["L1_attn_cam_gate"]), np.repeat(a["L1_attn_cam_w0"][None], P, 0),
         np.repeat(a["L1_attn_cam_w1"][None], P, 0)], 1)
    rows = np.stack([a["L0_ffn_down_scale"], a["L1_attn_c_attn_b"][2 * D:], a["L1_attn_c_proj_b"],
                     a["L1_ffn_Wscale_dp"]], 0)
    rows = np.repeat(rows[None], P, 0)

    arrays = {n: np.ascontiguousarray(x) for n, x in (
        ("x", a["L0_attn_x"]), ("pairs", pairs), ("prep", prep), ("mats", mats), ("vecs", vecs), ("rows", rows))}
    nc = bacc.Bacc("TRN2", target_bir_lowering=False, num_devices=1)
    args = [nc.dram_tensor(f"in_{n}", x.shape, mb.dt.from_np(x.dtype), kind="ExternalInput").ap()
            for n, x in arrays.items()]
    out = nc.dram_tensor("out", (BATCH, SEQ, D), mb.dt.float32, kind="ExternalOutput").ap()
    build_program(nc, *args, out)
    r = run_bass_kernel_spmd(nc, [{f"in_{n}": x for n, x in arrays.items()}], core_ids=[0])
    return r.results[0]["out"]
```

```python
from contextlib import ExitStack

import concourse.bass as bass
from concourse import mybir

F32 = mybir.dt.float32
F32R = mybir.dt.float32r
BF16 = mybir.dt.bfloat16
I32 = mybir.dt.int32
ALU = mybir.AluOpType
ACT = mybir.ActivationFunctionType
AX_X = mybir.AxisListType.X

P = 128
BATCH, SEQ, D = 4, 256, 256
TOK = BATCH * SEQ
TILES = TOK // P
KC = D // P
HEADS, DH = 16, 128
PAIRS = HEADS // 2
UNITS = 2 * BATCH
I0 = 768
C0 = I0 // P
I1 = 1024
C1 = I1 // P
HALF = TOK // 2
WARMING = 32
SLOTS = 4

QKV_COLS = 3 * KC * 2 * DH
WO_COLS = 2 * D
PAIR_COLS = QKV_COLS + WO_COLS
UG_PIECE = KC * 2 * I1 // PAIRS
WD_PIECE = C1 * D // PAIRS
Q8_PIECE = 3 * KC * I0 // PAIRS
PREP_COLS = UG_PIECE + WD_PIECE + Q8_PIECE
DCOLS = D // PAIRS

INV_SQRT_DH = 1.0 / float(DH) ** 0.5
SCALE1 = 0.25
EPS = 1e-5
FP8_MAX = 448.0
FP8_MIN_NORMAL = 2.0 ** -6
ROUND_TO_4_BITS = 1.5 * 2.0 ** 20
MASKED = -1e10

V_BQK, V_SU, V_SUDP, V_GS0, V_US0, V_WUP, V_WGATE, V_CAMG, V_W0, V_W1, V_N = (
    0, 4, 6, 14, 20, 26, 34, 42, 43, 44, 45)
R_DS, R_VB, R_PB, R_WDP = range(4)
M_ID, M_H, M_NH, M_MASK, M_N = 0, P, 2 * P, 3 * P, 4 * P

ORDER = """
head:5 root1:0 head:6 norm1:0 ln1:0 head:7 gu0:0.0 gu0:0.1 head:8 root1:1 hid0:0.0 gu0:0.2 gu0:0.3 norm1:1
hid0:0.1 hid0:0.2 hid0:0.3 gu0:0.4 head:9 hid0:0.4 head:10 gu0:0.5 ln1:1 hid0:0.5 head:11 gu0:1.0 gu0:1.1
root1:2 hid0:1.0 norm1:2 hid0:1.1 down0:0 gu0:1.2 root1:3 ln1:2 gu0:1.3 root2:0 gu0:1.4 norm1:3 hid0:1.2
hid0:1.3 gu0:1.5 norm2:0 gu0:2.0 hid0:1.4 hid0:1.5 gu0:2.1 gu0:2.2 hid0:2.0 gu0:2.3 ln1:3 hid0:2.1 hid0:2.2
gu0:2.4 ln2:0 hid0:2.3 hid0:2.4 down0:1 proj:0.0 proj:0.1 gu0:2.5 gu0:3.0 hid0:2.5 root2:1 gu0:3.1 score:0
proj:0.2 norm2:1 vsplit:0 sum:0 hid0:3.0 hid0:3.1 down0:2 gu0:3.2 gu0:3.3 root2:2 turn:0 hid0:3.2 ln2:1
gu0:3.4 gu0:3.5 norm2:2 ctx:0 proj:1.0 camq:0 proj:1.1 hid0:3.3 hid0:3.4 proj:1.2 hid0:3.5 ln2:2 vsplit:1
score:1 score2:0 sum:1 sum2:0 down0:3 turn:1 proj:2.0 proj:2.1 ctx:1 turn2:0 camq:1 root2:3 score:2 norm2:3
proj:2.2 mix:0 vsplit:2 sum:2 ln2:3 score2:1 out:0 root3:0 turn:2 proj:3.0 proj:3.1 ctx:2 sum2:1 norm3:0
camq:2 proj:3.2 ln3:0 turn2:1 score2:2 mix:1 had:0 sum2:2 score:3 out:1 gu1:0.0 gu1:0.1 root3:1 norm3:1
hid1:0.0 hid1:0.1 gu1:0.2 gu1:0.3 hid1:0.2 hid1:0.3 gu1:0.4 turn2:2 vsplit:3 sum:3 gu1:0.5 gu1:0.6 hid1:0.4
hid1:0.5 ln3:1 gu1:0.7 turn:3 mix:2 hid1:0.6 had:1 ctx:3 camq:3 hid1:0.7 out:2 gu1:1.0 gu1:1.1 root3:2
hid1:1.0 gu1:1.2 gu1:1.3 hid1:1.1 hid1:1.2 score2:3 hid1:1.3 sum2:3 norm3:2 gu1:1.4 down1:0 turn2:3 ln3:2
gu1:1.5 mix:3 hid1:1.4 gu1:1.6 hid1:1.5 had:2 out:3 hid1:1.6 gu1:1.7 root3:3 gu1:2.0 norm3:3 gu1:2.1 hid1:1.7
gu1:2.2 hid1:2.0 gu1:2.3 hid1:2.1 ln3:3 hid1:2.2 hid1:2.3 gu1:2.4 hid1:2.4 gu1:2.5 had:3 gu1:2.6 hid1:2.5
hid1:2.6 gu1:2.7 hid1:2.7 gu1:3.0 gu1:3.1 gu1:3.2 hid1:3.0 gu1:3.3 down1:1 hid1:3.1 hid1:3.2 gu1:3.4 gu1:3.5
hid1:3.3 hid1:3.4 hid1:3.5 gu1:3.6 gu1:3.7 down1:2 hid1:3.6 hid1:3.7 down1:3
"""


def stages():
    entries = []
    for entry in ORDER.split():
        stage, at = entry.split(":")
        b, part = at.split(".") if "." in at else (at, 0)
        entries.append((stage, int(b), int(part)))
    return entries


TAIL = stages()
FIRST_TAIL_STEP = min(b for stage, b, _ in TAIL if stage == "head")
LAST_OUT = {5: 0, 7: 1, UNITS + 1: 2, UNITS + 3: 3}


def numbering(*stages, without=()):
    return {e: n for n, e in enumerate(e for e in TAIL if e[0] in stages and e not in without)}


IN_ROT = ("ln1", "ln2", "ln3", "gu0", "gu1", "proj", "ctx", "mix", "had")
ROT = numbering(*IN_ROT)
HI = numbering(*IN_ROT, without=[("proj", b, 2) for b in range(BATCH)])
GU = numbering("gu0", "gu1")
SOFT = numbering("score", "score2")
TURN = numbering("turn", "turn2")
ONTO = numbering("down0", "out", "down1")
NORM = numbering("norm1", "norm2", "norm3")
STATS = {e: n for n, e in enumerate(
    e for e in TAIL if e[0] in ("down0", "out") or e[0] == "head" and e[1] in LAST_OUT)}


ROOT = numbering("root1", "root2", "root3")


def stats_before(layernorm, b):
    if layernorm == 1:
        return STATS["head", next(s for s, batch in LAST_OUT.items() if batch == b), 0]
    return STATS["down0" if layernorm == 2 else "out", b, 0]


def build_program(nc, x_in, pair_in, prep_in, mats_in, vecs_in, rows_in, out):
    with ExitStack() as ctx:
        def sb(name, shape, dt=F32):
            return ctx.enter_context(nc.sbuf_tensor(name, shape, dt))

        def psum(name):
            return ctx.enter_context(nc.psum_tensor(name, [P, 512], F32))

        def sem(name):
            return ctx.enter_context(nc.semaphore(name))

        xres = sb("xres", [P, TILES, D])
        xt_hi = sb("xt_hi", [P, KC, TOK], F32R)
        xt_lo = sb("xt_lo", [P, KC, TOK], F32R)
        qkv_raw = sb("qkv_raw", [P, QKV_COLS])
        wo_raw = sb("wo_raw", [P, WO_COLS])
        wqkv_hi = sb("wqkv_hi", [P, 3, KC, 2 * DH], F32R)
        wqkv_lo = sb("wqkv_lo", [P, 3, KC, 2 * DH], F32R)
        wo_hi = sb("wo_hi", [P, 2, D], F32R)
        wo_lo = sb("wo_lo", [P, 2, D], F32R)
        REG = 6 * TOK
        reg_hi = sb("reg_hi", [P, REG], F32R)
        reg_lo = sb("reg_lo", [P, REG], F32R)
        prob = sb("prob", [P, 2, 512])
        probn = sb("probn", [P, 2, 512])
        pt_hi = sb("pt_hi", [P, 2, 4, P], F32R)
        pt_lo = sb("pt_lo", [P, 2, 4, P], F32R)
        z_hi = sb("z_hi", [P, 2, SEQ], F32R)
        z_lo = sb("z_lo", [P, 2, SEQ], F32R)
        q8 = sb("q8", [P, PAIRS, Q8_PIECE], F32R)
        ug_hi = sb("ug_hi", [P, PAIRS, UG_PIECE], F32R)
        ug_lo = sb("ug_lo", [P, PAIRS, UG_PIECE], F32R)
        wd_hi = sb("wd_hi", [P, C1, PAIRS, DCOLS], F32R)
        wd_lo = sb("wd_lo", [P, C1, PAIRS, DCOLS], F32R)
        prep = sb("prep", [P, PREP_COLS])
        scratch = sb("scratch", [P, Q8_PIECE])
        bfly = sb("bfly", [P, 2, WD_PIECE])
        bf_hi = sb("bf_hi", [P, WD_PIECE], F32R)
        bf_lo = sb("bf_lo", [P, WD_PIECE], F32R)
        fused_ab = sb("fused_ab", [P, 2 * SEQ])
        xn = sb("xn", [P, 2, 2, D])
        ident = sb("ident", [P, P])
        had_p = sb("had_p", [P, P], F32R)
        had_n = sb("had_n", [P, P], F32R)
        ident_b = sb("ident_b", [P, P], BF16)
        mask_b = sb("mask_b", [P, P], BF16)
        vecs = sb("vecs", [P, V_N])
        rows = sb("rows", [P, 4, D])
        stats = sb("stats", [P, TILES, 6])
        mv = sb("mv", [P, TILES, 2])
        nwt = sb("nwt", [P, 4, TILES])
        cam = sb("cam", [P, 6])
        wscale = sb("wscale", [P, 2 * C1])
        rmax = sb("rmax", [P, 2 * UNITS, 2])
        nbias = sb("nbias", [P, 2 * UNITS, 2])
        rsum = sb("rsum", [P, 2 * UNITS, 2])
        rinv = sb("rinv", [P, 2 * UNITS, 2])

        bank_pj = [psum("bank_pj0"), psum("bank_pj1")]
        bank_s = [psum("bank_s0"), psum("bank_s1")]
        bank_t = psum("bank_t")
        bank_z = [psum("bank_z0"), psum("bank_z1")]
        bank_o = psum("bank_o")
        bank_rot = bank_pj + bank_s

        q_hi, q_lo = (r[:, 0:2 * TOK].rearrange("p (h t) -> p h t", h=2) for r in (reg_hi, reg_lo))
        k_hi, k_lo = (r[:, 2 * TOK:4 * TOK].rearrange("p (h t) -> p h t", h=2) for r in (reg_hi, reg_lo))
        v_hi, v_lo = (r[:, 4 * TOK:6 * TOK].rearrange("p (t e) -> p t e", t=TILES) for r in (reg_hi, reg_lo))
        q8_all = q8[:, :, :].rearrange("p a b -> p (a b)")
        gate0_w = q8_all[:, 0:KC * I0].rearrange("p (k c m) -> p k c m", k=KC, c=C0)
        up0_w = q8_all[:, KC * I0:2 * KC * I0].rearrange("p (k c m) -> p k c m", k=KC, c=C0)
        down0_w = q8_all[:, 2 * KC * I0:3 * KC * I0].rearrange("p (c m) -> p c m", c=C0)
        ug_h, ug_l = (w[:, :, :].rearrange("p a b -> p (a b)").rearrange(
            "p (k c g m) -> p k c g m", k=KC, c=C1, g=2) for w in (ug_hi, ug_lo))
        wd_h, wd_l = (w[:, :, :, :].rearrange("p c a b -> p c (a b)") for w in (wd_hi, wd_lo))
        out_v = out.rearrange("b (t p) d -> p (b t) d", p=P)
        x_v = x_in.rearrange("b (t p) d -> p (b t) d", p=P)

        q8_pow = scratch
        gate_act = [qkv_raw[:, n * SEQ:(n + 1) * SEQ] for n in range(SLOTS)]
        fused = [r[:, n * SEQ:(n + 1) * SEQ] for r in (fused_ab, scratch) for n in range(2)]
        normed = [xn[:, 0], xn[:, 1]] + [
            prep[:, n * 2 * D:(n + 1) * 2 * D].rearrange("p (a c) -> p a c", a=2) for n in range(2)]
        v_sum = wo_raw[:, :].rearrange("p (a c) -> p a c", a=2)
        cam_tanh = qkv_raw[:, SLOTS * SEQ:(SLOTS + 1) * SEQ]
        cam_total = qkv_raw[:, (SLOTS + 1) * SEQ:(SLOTS + 2) * SEQ]

        def f32(ap):
            return ap.bitcast(F32)

        def hidden(r, stage, b):
            first, chunks = (b * C0 * SEQ, C0) if stage == "gu0" else (b % 3 * C1 * SEQ, C1)
            return r[:, first:first + chunks * SEQ].rearrange("p (c t) -> p c t", c=chunks)

        def attn1(r, b):
            part = r[:, b * 6 * SEQ:(b + 1) * 6 * SEQ].rearrange("p (n c) -> p n c", c=SEQ)
            return part[:, 0:2], part[:, 2:4], part[:, 4:6]

        def vec(c, n=1):
            return vecs[:, c:c + n]

        def row(r, n):
            return rows[:, r, :].unsqueeze(1).broadcast_to([P, n, D])

        def rot(n):
            return bank_rot[n % 4]

        loaded_x = [sem(f"loaded_x{b}") for b in range(BATCH)]
        loaded_ident = sem("loaded_ident")
        loaded_const = sem("loaded_const")
        loaded_rows = sem("loaded_rows")
        loaded_first = [sem(f"loaded_first{n}") for n in range(3)]
        loaded_qkv = sem("loaded_qkv")
        loaded_wo = sem("loaded_wo")
        loaded_prep = sem("loaded_prep")
        stored = sem("stored")
        consts_ready = sem("consts_ready")
        zeros_ready = sem("zeros_ready")
        dve = sem("dve")
        pool_first = sem("pool_first")
        pool_went = sem("pool_went")
        ug_hi_done = sem("ug_hi_done")
        pool_step = sem("pool_step")
        ln_done = sem("ln_done")
        lnt_ready = sem("lnt_ready")
        lnt_hi = sem("lnt_hi")
        lnt_split = sem("lnt_split")
        w_q = sem("w_q")
        w_k = sem("w_k")
        w_v = sem("w_v")
        wo_hi_done = sem("wo_hi_done")
        w_o = sem("w_o")
        proj_ready = sem("proj_ready")
        proj_hi = sem("proj_hi")
        proj_split = sem("proj_split")
        s_ready = sem("s_ready")
        max_done = sem("max_done")
        nbias_done = sem("nbias_done")
        exp_done = sem("exp_done")
        rinv_done = sem("rinv_done")
        norm_done = sem("norm_done")
        t_ready = sem("t_ready")
        t_hi = sem("t_hi")
        t_split = sem("t_split")
        z_ready = sem("z_ready")
        zhi_done = sem("zhi_done")
        z_split = sem("z_split")
        o_ready = sem("o_ready")
        o_added = sem("o_added")
        wdmm_ready = sem("wdmm_ready")
        bf_ready = sem("bf_ready")
        prep_q8 = sem("prep_q8")
        prep_pool = sem("prep_pool")
        wd_done = sem("wd_done")
        q8_step = sem("q8_step")
        rot_ready = sem("rot_ready")
        rot_hi = sem("rot_hi")
        rot_free = sem("rot_free")
        stats_done = sem("stats_done")
        newton = sem("newton")
        root_done = sem("root_done")
        v_hi_done = sem("v_hi_done")
        v_split = sem("v_split")
        fuse_hi = sem("fuse_hi")
        fuse_lo = sem("fuse_lo")
        camq_sum = sem("camq_sum")
        camq_hi = sem("camq_hi")
        camq_split = sem("camq_split")
        cam_arg = sem("cam_arg")
        cam_exp = sem("cam_exp")
        x_final = sem("x_final")


        N_CONST = 2
        CH = 6
        TPP = 2 * CH
        OPP = BATCH + 1
        ALL_UNITS = PAIRS * UNITS
        PROJ_AT = (((1, 0), (1, 1)), ((1, 2),), ((1, 3),), ((1, 4),), ((1, 5), (0, 0)), ((0, 1), (0, 2)), ((0, 3),),
                   ((0, 4), (0, 5)))
        OUT_AT = {1: 2, 3: 3, 5: 0, 7: 1}
        WD_AT = 6

        def proj_tiles(s, own, following):
            return [(half, n, (CH if half else TPP) + n) for half, n in PROJ_AT[s] if (own if half else following)]

        def proj_dst(hi, half, n):
            q, k, v = (q_hi, k_hi, v_hi) if hi else (q_lo, k_lo, v_lo)
            if n < 4:
                return (q, k)[n // 2][:, n % 2, half * HALF:(half + 1) * HALF]
            t = half * (TILES // 2) + (n - 4) * 2
            return v[:, t:t + 2, :]

        def proj_src(n):
            bank = bank_pj[n % 2]
            return bank[:, :] if n < 4 else bank[:, :].rearrange("p (t e) -> p t e", t=2)

        def two(ap):
            return ap.rearrange("p (a c) -> p a c", a=2)

        def tokens(b):
            return slice(b * SEQ, (b + 1) * SEQ)

        block = ctx.enter_context(nc.Block())

        @block.sync
        def _(sp):
            sp.dma_start(ident[:, :], mats_in[:, M_ID:M_ID + P]).then_inc(loaded_ident, 16)
            for b in range(BATCH):
                sp.dma_start(xres[:, 2 * b:2 * b + 2, :], x_v[:, 2 * b:2 * b + 2, :]).then_inc(loaded_x[b], 16)
            for which in range(3):
                ws = slice(which * 2 * D, (which + 1) * 2 * D)
                sp.dma_start(qkv_raw[:, ws], pair_in[0, :, ws]).then_inc(loaded_first[which], 16)
            sp.dma_start(prob[:, 0, 0:3 * P], mats_in[:, M_H:M_N]).then_inc(loaded_const, 16)
            sp.dma_start(vecs[:, :], vecs_in).then_inc(loaded_const, 16)
            sp.dma_start(wo_raw[:, :], pair_in[0, :, QKV_COLS:PAIR_COLS]).then_inc(loaded_wo, 16)
            sp.dma_start(prep[:, :], prep_in[0]).then_inc(loaded_prep, 16)
            sp.dma_start(rows[:, :, :], rows_in).then_inc(loaded_rows, 16)
            sp.wait_ge(w_v, 1)
            sp.dma_start(qkv_raw[:, :], pair_in[1, :, 0:QKV_COLS]).then_inc(loaded_qkv, 16)
            with sp.Fori(0, PAIRS - 1) as i:
                sp.wait_ge(w_o, i + 1)
                sp.dma_start(wo_raw[:, :], pair_in[i + 1, :, QKV_COLS:PAIR_COLS]).then_inc(loaded_wo, 16)
                sp.wait_ge(w_v, i + 2)
                sp.dma_start(qkv_raw[:, :], pair_in[i + 2, :, 0:QKV_COLS]).then_inc(loaded_qkv, 16)
                sp.wait_ge(prep_q8, i + 1)
                sp.wait_ge(prep_pool, i + 1)
                sp.dma_start(prep[:, :], prep_in[i + 1]).then_inc(loaded_prep, 16)
            sp.wait_ge(w_o, PAIRS)
            sp.dma_start(wo_raw[:, :], pair_in[PAIRS, :, QKV_COLS:PAIR_COLS]).then_inc(loaded_wo, 16)
            for b in range(BATCH):
                sp.wait_ge(x_final, b + 1)
                sp.dma_start(out_v[:, 2 * b:2 * b + 2, :], xres[:, 2 * b:2 * b + 2, :]).then_inc(stored, 16)
            sp.wait_ge(stored, 16 * BATCH)

        @block.tensor
        def _(pe):
            def products(dst, pairs, start=True, stop=True):
                for n, (lhs, rhs) in enumerate(pairs):
                    mm = nc.tensor.matmul(dst, lhs, rhs, start=start and n == 0, stop=stop and n == len(pairs) - 1)
                return mm

            def three(lhs, rhs):
                (lh, ll), (rh, rl) = lhs, rhs
                return [(lh, rh), (lh, rl), (ll, rh)]

            def ln_transposes(dst, tok):
                for k in range(KC):
                    for t in range(2):
                        mm = nc.tensor.transpose(dst[:, k * SEQ + t * P:k * SEQ + (t + 1) * P],
                                                 tok[:, t, k * P:(k + 1) * P], ident[:, :])
                return mm

            def rot_wait(n):
                if n >= 4:
                    pe.wait_ge(rot_free, n - 3)
                elif n >= 2:
                    pe.wait_ge(exp_done, ALL_UNITS)
                else:
                    pe.wait_ge(proj_split, PAIRS * TPP)

            def proj_tile(half, n):
                bank = bank_pj[n % 2]
                if n < 4:
                    which, h = n // 2, n % 2
                    mm = products(bank[:, :], [
                        p for k in range(KC) for p in three(
                            [w[:, which, k, h * DH:(h + 1) * DH] for w in (wqkv_hi, wqkv_lo)],
                            [x[:, k, half * HALF:(half + 1) * HALF] for x in (xt_hi, xt_lo)])])
                else:
                    for t in range(2):
                        t0 = half * HALF + ((n - 4) * 2 + t) * P
                        mm = products(bank[:, t * 2 * DH:(t + 1) * 2 * DH], [
                            p for k in range(KC) for p in three(
                                [x[:, k, t0:t0 + P] for x in (xt_hi, xt_lo)],
                                [w[:, 2, k, :] for w in (wqkv_hi, wqkv_lo)])])
                mm.then_inc(proj_ready, 1)

            def scores(i, j, prev):
                b, h = divmod(j, 2)
                pe.wait_ge(proj_split, i * TPP + (4 if b < 2 else CH + 4))
                if j >= 2 or prev:
                    pe.wait_ge(exp_done, i * UNITS + j - 1)
                for qt in range(2):
                    t0 = b * SEQ + qt * P
                    dst = bank_s[j % 2][:, qt * SEQ:(qt + 1) * SEQ]
                    products(dst, three([q[:, h, t0:t0 + P] for q in (q_hi, q_lo)],
                                        [k[:, h, tokens(b)] for k in (k_hi, k_lo)]), start=qt == 0, stop=False)
                blocks = bank_s[j % 2][:, :].rearrange("p (a c) -> p a c", a=4)[:, 0:4:3, :]
                nc.tensor.matmul(blocks, ident_b[:, :], mask_b[:, :].unsqueeze(1).broadcast_to([P, 2, P]),
                                 start=False, stop=True).then_inc(s_ready, 1)

            def turn(i, j, prev):
                pe.wait_ge(norm_done, i * UNITS + j + 1)
                if j >= 1 or prev:
                    pe.wait_ge(t_split, i * UNITS + j)
                for n in range(3):
                    mm = nc.tensor.transpose(bank_t[:, n * P:(n + 1) * P], probn[:, j % 2, n * P:(n + 1) * P],
                                             ident[:, :])
                mm.then_inc(t_ready, 1)

            def attend(i, j, prev):
                b, h = divmod(j % UNITS, 2)
                if j >= 0:
                    pe.wait_ge(proj_split, i * TPP + (CH if b < 2 else TPP))
                else:
                    pe.wait_ge(proj_split, i * TPP)
                pe.wait_ge(t_split, i * UNITS + j + 1)
                if j >= 2 or prev:
                    pe.wait_ge(z_split, i * UNITS + j - 1)
                mm = products(bank_z[j % 2][:, 0:SEQ], [p for t in range(2) for p in three(
                    [v[:, 2 * b + t, h * DH:(h + 1) * DH] for v in (v_hi, v_lo)],
                    [pt[:, j % 2, 1:3, :] if t == 0 else pt[:, j % 2, 0:4:3, :] for pt in (pt_hi, pt_lo)])])
                mm.then_inc(z_ready, 1)

            def project(i, b, prev):
                pe.wait_ge(z_split, i * UNITS + (2 * b + 2 if b < 2 else 2 * b + 2 - UNITS))
                if b < 2:
                    pe.wait_ge(w_o, i + 1)
                if prev:
                    pe.wait_ge(o_added, i * OPP + {2: -2, 3: -1, 0: 0, 1: 2}[b])
                elif b == 1:
                    pe.wait_ge(o_added, 2)
                for qt in range(2):
                    mm = products(bank_o[:, qt * D:(qt + 1) * D], [p for h in range(2) for p in three(
                        [z[:, h, qt * P:(qt + 1) * P] for z in (z_hi, z_lo)],
                        [w[:, h, :] for w in (wo_hi, wo_lo)])])
                mm.then_inc(o_ready, 1)

            def wd_piece(i):
                pe.wait_ge(bf_ready, i + 1)
                pe.wait_ge(o_added, i * OPP + 1)
                products(bank_o[:, 0:WD_PIECE], [(had_p[:, :], bf_hi[:, :]), (had_p[:, :], bf_lo[:, :])])\
                    .then_inc(wdmm_ready, 1)

            def head_step(i, s, prev=True, own=True, following=True):
                attending = prev if s < 3 else own
                if attending and s % 2 == 0:
                    attend(i, s - 3, prev)
                if prev if s < 2 else own:
                    turn(i, s - 2, prev)
                if own:
                    scores(i, s, prev)
                if s in OUT_AT and (prev if s < 4 else own):
                    project(i, OUT_AT[s], prev)
                if attending and s % 2 == 1:
                    attend(i, s - 3, prev)
                if s == WD_AT:
                    wd_piece(i)
                for half, n, number in proj_tiles(s, own, following):
                    if half == 0 and n % 2 == 0:
                        pe.wait_ge((w_q, w_k, w_v)[n // 2], i + 2)
                    pe.wait_ge(proj_split, i * TPP + number - 1)
                    proj_tile(half, n)

            def first_turned(b):
                pe.wait_ge(ln_done, b + 1)
                ln_transposes((bank_s + bank_z)[b], xn[:, b % 2]).then_inc(lnt_ready, 1)

            pe.wait_ge(loaded_ident, 16)
            def warm(times):
                for _ in range(times):
                    nc.tensor.transpose(bank_o[:, 0:P], ident[:, :], ident[:, :])

            warm(WARMING)
            first_turned(0)
            first_turned(1)
            warm(WARMING // 4)
            pe.wait_ge(lnt_split, 2)
            for n in range(CH):
                if n % 2 == 0:
                    pe.wait_ge((w_q, w_k, w_v)[n // 2], 1)
                if n >= 2:
                    pe.wait_ge(proj_split, n - 1)
                proj_tile(0, n)
                if n == 2:
                    first_turned(2)
                    first_turned(3)
            pe.wait_ge(lnt_split, BATCH)
            pe.wait_ge(consts_ready, 1)
            pe.wait_ge(zeros_ready, 1)
            for s in range(UNITS):
                head_step(0, s, prev=False)
            with pe.Fori(1, PAIRS - 1) as i:
                for s in range(UNITS):
                    head_step(i, s)
            for s in range(FIRST_TAIL_STEP):
                head_step(PAIRS - 1, s, following=False)

            def x_parts(k, t):
                return [x[:, k, t] for x in (xt_hi, xt_lo)]

            def rot_tile(e, contents):
                rot_wait(ROT[e])
                contents(rot(ROT[e])).then_inc(rot_ready, 1)

            def halves(bank, of):
                for n in range(2):
                    mm = products(bank[:, n * SEQ:(n + 1) * SEQ], of(n))
                return mm

            def gate_up(e):
                stage, b, c = e
                pe.wait_ge(rot_free, ROT["ln1" if stage == "gu0" else "had", b, 0] + 1)
                xs = [x_parts(k, tokens(b)) for k in range(KC)]
                if stage == "gu0":
                    rot_tile(e, lambda bank: halves(bank, lambda g: [
                        ((gate0_w, up0_w)[g][:, k, c, :], x) for k in range(KC) for x in xs[k]]))
                else:
                    rot_tile(e, lambda bank: halves(bank, lambda g: [
                        p for k in range(KC) for p in three([w[:, k, c, g, :] for w in (ug_h, ug_l)], xs[k])]))

            def down(e):
                stage, b, _ = e
                gu, chunks = ("gu0", C0) if stage == "down0" else ("gu1", C1)
                pe.wait_ge(fuse_lo, GU[gu, b, chunks - 1] + 1)
                pe.wait_ge(o_added, PAIRS * OPP + ONTO[e])
                h_hi, h_lo = hidden(reg_hi, gu, b), hidden(reg_lo, gu, b)

                def of(t):
                    ts = slice(t * P, (t + 1) * P)
                    if stage == "down0":
                        return [(h[:, c, ts], down0_w[:, c, :]) for c in range(chunks) for h in (h_hi, h_lo)]
                    return [p for c in range(chunks) for p in three(
                        [h_hi[:, c, ts], h_lo[:, c, ts]], [wd_h[:, c, :], wd_l[:, c, :]])]
                halves(bank_o, of).then_inc(o_ready, 1)

            def qkv1(e):
                _, b, which = e
                pe.wait_ge(rot_free, ROT["ln2", b, 0] + 1)
                pe.wait_ge((w_q, w_k, w_v)[which], PAIRS + 1)

                def of(n):
                    if which < 2:
                        return [p for k in range(KC) for p in three(
                            [w[:, which, k, n * P:(n + 1) * P] for w in (wqkv_hi, wqkv_lo)], x_parts(k, tokens(b)))]
                    t0 = b * SEQ + n * P
                    return [p for k in range(KC) for p in three(
                        x_parts(k, slice(t0, t0 + P)), [w[:, 2, k, :] for w in (wqkv_hi, wqkv_lo)])]
                rot_tile(e, lambda bank: halves(bank, of))

            def scores1(e):
                stage, b, _ = e
                if stage == "score":
                    pe.wait_ge(rot_free, ROT["proj", b, 1] + 1)
                else:
                    pe.wait_ge(camq_split, b + 1)
                if SOFT[e] >= 2:
                    pe.wait_ge(exp_done, ALL_UNITS + SOFT[e] - 1)
                (qh, kh, _), (ql, kl, _) = attn1(reg_hi, b), attn1(reg_lo, b)
                halves(bank_z[SOFT[e] % 2], lambda qt: [p for k in range(1 if stage == "score" else 2) for p in three(
                    [q[:, k, qt * P:(qt + 1) * P] for q in (qh, ql)], [kh[:, k, :], kl[:, k, :]])]).then_inc(s_ready, 1)

            def turn1(e):
                stage, b, _ = e
                n = SOFT["score" if stage == "turn" else "score2", b, 0]
                pe.wait_ge(norm_done, ALL_UNITS + n + 1)
                pe.wait_ge(t_split, ALL_UNITS + TURN[e])
                for kt in range(2):
                    for qt in range(2):
                        mm = nc.tensor.transpose(bank_t[:, kt * SEQ + qt * P:kt * SEQ + (qt + 1) * P],
                                                 probn[:, n % 2, qt * SEQ + kt * P:qt * SEQ + (kt + 1) * P], ident[:, :])
                mm.then_inc(t_ready, 1)

            def values1(e):
                stage, b, _ = e
                m = TURN["turn" if stage == "ctx" else "turn2", b, 0]
                pe.wait_ge(t_split, ALL_UNITS + m + 1)
                pe.wait_ge(v_split, b + 1)
                (_, _, vh), (_, _, vl) = attn1(reg_hi, b), attn1(reg_lo, b)

                def of(n):
                    es = slice(n * P, (n + 1) * P)
                    return [p for kt in range(2) for p in three(
                        [vh[:, kt, es], vl[:, kt, es]], [pt[:, m % 2, 2 * kt:2 * kt + 2, :] for pt in (pt_hi, pt_lo)])]
                rot_tile(e, lambda bank: products(bank[:, 0:SEQ], of(0)) if stage == "ctx" else halves(bank, of))

            def out1(e):
                pe.wait_ge(rot_free, ROT["mix", e[1], 0] + 1)
                pe.wait_ge(w_o, PAIRS + 1)
                pe.wait_ge(o_added, PAIRS * OPP + ONTO[e])
                halves(bank_o, lambda qt: [p for k in range(2) for p in three(
                    [z[:, k, qt * P:(qt + 1) * P] for z in (z_hi, z_lo)],
                    [w[:, k, :] for w in (wo_hi, wo_lo)])]).then_inc(o_ready, 1)

            def hadamard(e):
                b = e[1]
                pe.wait_ge(rot_free, ROT["ln3", b, 0] + 1)
                rot_tile(e, lambda bank: halves(bank, lambda n: [
                    (h[:, :], x) for k, h in enumerate((had_p, (had_p, had_n)[n])) for x in x_parts(k, tokens(b))]))

            for e in TAIL:
                stage, b, _ = e
                if stage == "head" and b < UNITS:
                    head_step(PAIRS - 1, b, following=False)
                elif stage == "head":
                    head_step(PAIRS, b - UNITS, own=False, following=False)
                elif stage in ("ln1", "ln2", "ln3"):
                    pe.wait_ge(ln_done, BATCH + NORM["norm" + stage[2], b, 0] + 1)
                    rot_tile(e, lambda bank: ln_transposes(bank, normed[b]))
                elif stage in ("gu0", "gu1"):
                    pe.wait_ge(prep_q8, PAIRS)
                    pe.wait_ge(prep_pool, PAIRS)
                    gate_up(e)
                elif stage in ("down0", "down1"):
                    down(e)
                elif stage == "proj":
                    qkv1(e)
                elif stage in ("score", "score2"):
                    scores1(e)
                elif stage in ("turn", "turn2"):
                    turn1(e)
                elif stage in ("ctx", "mix"):
                    values1(e)
                elif stage == "out":
                    out1(e)
                elif stage == "had":
                    hadamard(e)

        @block.scalar
        def _(act):
            def copy(dst, src, **kw):
                return nc.scalar.activation(dst, src, ACT.Copy, **kw)

            def proj_part(half, n, number):
                act.wait_ge(proj_ready, number + 1)
                copy(proj_dst(True, half, n), proj_src(n)).then_inc(proj_hi, 1)

            def exps(i, j):
                act.wait_ge(nbias_done, i * UNITS + j + 1)
                bank = bank_s[j % 2]
                for dst, src, qt in ((prob[:, j % 2, 0:P], bank[:, 0:P], 0),
                                     (prob[:, j % 2, P:3 * P], bank[:, SEQ:2 * SEQ], 1)):
                    a = nc.scalar.activation(dst, src, ACT.Exp, bias=nbias[:, j, qt:qt + 1], scale=INV_SQRT_DH,
                                             accum_out=rsum[:, j, qt:qt + 1])
                a.then_inc(exp_done, 1)

            def output(i, s):
                act.wait_ge(z_ready, i * UNITS + s - 2)
                copy(z_hi[:, (s - 3) % 2, :], bank_z[(s - 3) % 2][:, 0:SEQ]).then_inc(zhi_done, 1)

            def head_step(i, s, prev=True, own=True, following=True):
                attending = prev if s < 3 else own
                if attending and s % 2 == 0:
                    output(i, s)
                if prev if s < 2 else own:
                    act.wait_ge(t_ready, i * UNITS + s - 1)
                    copy(pt_hi[:, s % 2, 1:4, :], bank_t[:, 0:3 * P].rearrange("p (a c) -> p a c", a=3))\
                        .then_inc(t_hi, 1)
                if own:
                    exps(i, s)
                if attending and s % 2 == 1:
                    output(i, s)
                if own and s == 3:
                    act.wait_ge(loaded_prep, 16 * (i + 1))
                    copy(ug_hi[:, i, :], prep[:, 0:UG_PIECE]).then_inc(ug_hi_done, 1)
                for half, n, number in proj_tiles(s, own, following):
                    proj_part(half, n, i * TPP + number)

            def first_hi(b):
                act.wait_ge(lnt_ready, b + 1)
                copy(xt_hi[:, :, tokens(b)], two((bank_s + bank_z)[b][:, :])).then_inc(lnt_hi, 1)

            first_hi(0)
            first_hi(1)
            act.wait_ge(loaded_ident, 16)
            act.wait_ge(loaded_const, 16 * N_CONST)
            copy(ident_b[:, :], ident[:, :])
            copy(had_p[:, :], prob[:, 0, 0:P])
            copy(had_n[:, :], prob[:, 0, P:2 * P])
            copy(mask_b[:, :], prob[:, 0, 2 * P:3 * P]).then_inc(consts_ready, 1)
            for n in range(CH):
                proj_part(0, n, n)
                if n == 2:
                    first_hi(2)
                    first_hi(3)
            act.wait_ge(cam_arg, 1)
            nc.scalar.activation(cam[:, 1:2], cam[:, 0:1], ACT.Exp, scale=-1.0).then_inc(cam_exp, 1)
            for s in range(UNITS):
                head_step(0, s, prev=False)
            with act.Fori(1, PAIRS - 1) as i:
                for s in range(UNITS):
                    head_step(i, s)
            for s in range(FIRST_TAIL_STEP):
                head_step(PAIRS - 1, s, following=False)

            def first(e):
                act.wait_ge(rot_ready, ROT[e] + 1)
                return rot(ROT[e])

            for e in TAIL:
                stage, b, c = e
                if stage == "head" and b < UNITS:
                    head_step(PAIRS - 1, b, following=False)
                elif stage == "head":
                    head_step(PAIRS, b - UNITS, own=False, following=False)
                elif stage in ("ln1", "ln2", "had"):
                    copy(xt_hi[:, :, tokens(b)], two(first(e)[:, :])).then_inc(rot_hi, 1)
                elif stage == "ln3":
                    bank = first(e)
                    for k in range(KC):
                        a = copy(xt_hi[:, k, tokens(b)], bank[:, k * SEQ:(k + 1) * SEQ], scale=vec(V_SU + k))
                    a.then_inc(rot_hi, 1)
                elif stage in ("gu0", "gu1"):
                    if GU[e] == 0:
                        act.wait_ge(w_v, PAIRS + 1)
                    scale = vec(V_GS0 + c) if stage == "gu0" else wscale[:, C1 + c:C1 + c + 1]
                    nc.scalar.activation(gate_act[GU[e] % SLOTS], first(e)[:, 0:SEQ], ACT.Silu, scale=scale)\
                        .then_inc(rot_hi, 1)
                elif stage in ("hid0", "hid1"):
                    gu = "gu" + stage[3]
                    act.wait_ge(rot_free, ROT[gu, b, c] + 1)
                    copy(hidden(reg_hi, gu, b)[:, c, :], fused[GU[gu, b, c] % SLOTS]).then_inc(fuse_hi, 1)
                elif stage == "proj" and c < 2:
                    bank = first(e)
                    for n in range(2):
                        a = nc.scalar.activation(attn1(reg_hi, b)[c][:, n, :], bank[:, n * SEQ:(n + 1) * SEQ],
                                                 ACT.Identity, bias=vec(V_BQK + 2 * c + n))
                    a.then_inc(rot_hi, 1)
                elif stage == "vsplit":
                    act.wait_ge(rot_free, ROT["proj", b, 2] + 1)
                    copy(attn1(reg_hi, b)[2], v_sum).then_inc(v_hi_done, 1)
                elif stage in ("score", "score2"):
                    n = SOFT[e]
                    act.wait_ge(nbias_done, ALL_UNITS + n + 1)
                    for qt in range(2):
                        ts = slice(qt * SEQ, (qt + 1) * SEQ)
                        a = nc.scalar.activation(prob[:, n % 2, ts], bank_z[n % 2][:, ts], ACT.Exp, scale=SCALE1,
                                                 bias=nbias[:, UNITS + n, qt:qt + 1],
                                                 accum_out=rsum[:, UNITS + n, qt:qt + 1])
                    a.then_inc(exp_done, 1)
                elif stage in ("turn", "turn2"):
                    m = TURN[e]
                    act.wait_ge(t_ready, ALL_UNITS + m + 1)
                    copy(pt_hi[:, m % 2, :, :], bank_t[:, :].rearrange("p (a c) -> p a c", a=4)).then_inc(t_hi, 1)
                elif stage == "ctx":
                    nc.scalar.activation(cam_tanh, first(e)[:, 0:SEQ], ACT.Tanh, scale=vec(V_CAMG)).then_inc(rot_hi, 1)
                elif stage == "camq":
                    act.wait_ge(camq_sum, b + 1)
                    copy(attn1(reg_hi, b)[0][:, 0, :], cam_total).then_inc(camq_hi, 1)
                elif stage == "mix":
                    copy(z_hi[:, :, :], two(first(e)[:, :])).then_inc(rot_hi, 1)

        @block.vector
        def _(v):
            taken = [0]

            def step(ins):
                taken[0] += 1
                ins.then_inc(dve, 1)
                v.wait_ge(dve, taken[0])

            def lo(dst, src, hi):
                return nc.vector.tensor_tensor(dst, src, f32(hi), ALU.subtract)

            def ln_stats(t0, nt):
                sl = slice(t0, t0 + nt)
                for t in range(t0, t0 + nt):
                    a = nc.vector.bn_stats(stats[:, t, :], xres[:, t, :])
                step(a)
                for t in range(t0, t0 + nt):
                    a = nc.vector.bn_aggr(mv[:, t, :], stats[:, t, :])
                step(a)
                return ln_guess(t0, nt)

            def ln_guess(t0, nt):
                sl = slice(t0, t0 + nt)
                step(nc.vector.tensor_scalar(nwt[:, 0, sl], mv[:, sl, 1], EPS, None, ALU.add))
                return nc.vector.tensor_scalar(nwt[:, 1, sl].bitcast(I32), nwt[:, 0, sl].bitcast(I32), -0.5, 0x5F3759DF,
                                               ALU.mult, ALU.add)

            def ln_apply(tok, b):
                for t in range(2):
                    tile = 2 * b + t
                    a = nc.vector.tensor_scalar(tok[:, t, :], xres[:, tile, :], mv[:, tile, 0:1],
                                                nwt[:, 1, tile:tile + 1], ALU.subtract, ALU.mult)
                a.then_inc(ln_done, 1)

            def proj_part(half, n, number):
                v.wait_ge(proj_hi, number + 1)
                lo(proj_dst(False, half, n), proj_src(n), proj_dst(True, half, n)).then_inc(proj_split, 1)

            def maxima(i, j):
                v.wait_ge(s_ready, i * UNITS + j + 1)
                bank = bank_s[j % 2]
                nc.vector.reduce_max(rmax[:, j, 0:1], bank[:, 0:P], AX_X)
                nc.vector.reduce_max(rmax[:, j, 1:2], bank[:, SEQ:2 * SEQ], AX_X).then_inc(max_done, 1)
                v.wait_ge(max_done, i * UNITS + j + 1)
                nc.vector.tensor_scalar(nbias[:, j, :], rmax[:, j, :], -INV_SQRT_DH, None, ALU.mult)\
                    .then_inc(nbias_done, 1)

            def fp8_round(i, s):
                w = prep[:, UG_PIECE + WD_PIECE:PREP_COLS]

                def q8s(ins, n):
                    ins.then_inc(q8_step, 1)
                    v.wait_ge(q8_step, i * 7 + n)

                if s == 1:
                    v.wait_ge(loaded_prep, 16 * (i + 1))
                    q8s(nc.vector.tensor_scalar(q8_pow[:, :].bitcast(I32), w.bitcast(I32), 0x7F800000, None,
                                                ALU.bitwise_and), 1)
                    q8s(nc.vector.tensor_scalar(q8_pow[:, :], q8_pow[:, :], FP8_MIN_NORMAL, ROUND_TO_4_BITS,
                                                ALU.max, ALU.mult), 2)
                elif s == 2:
                    q8s(nc.vector.tensor_tensor(w, w, q8_pow[:, :], ALU.add), 3)
                elif s == 3:
                    q8s(nc.vector.tensor_tensor(w, w, q8_pow[:, :], ALU.subtract), 4)
                elif s == 4:
                    q8s(nc.vector.tensor_scalar(q8_pow[:, :].bitcast(I32), w.bitcast(I32), 0x7FFFFFFF, None,
                                                ALU.bitwise_and), 5)
                    q8s(nc.vector.tensor_scalar(q8_pow[:, :], q8_pow[:, :], FP8_MAX, 3e38, ALU.is_gt, ALU.mult), 6)
                elif s == 6:
                    q8s(nc.vector.tensor_scalar(q8_pow[:, :], q8_pow[:, :], 3e38, 0.0, ALU.mult, ALU.mult), 7)
                elif s == 7:
                    nc.vector.tensor_tensor(q8[:, i, :], q8_pow[:, :], w, ALU.add).then_inc(prep_q8, 1)

            def wd_piece(i):
                signed = bfly[:, 0, :].rearrange("p (c m) -> p c m", c=C1)
                v.wait_ge(wdmm_ready, i + 1)
                nc.vector.tensor_tensor(signed, bank_o[:, 0:WD_PIECE].rearrange("p (c m) -> p c m", c=C1),
                                        vec(V_SUDP, C1).unsqueeze(2).broadcast_to([P, C1, DCOLS]), ALU.mult)\
                    .then_inc(o_added, 1)
                v.wait_ge(o_added, i * OPP + 2)
                nc.vector.tensor_copy(wd_hi[:, :, i, :], signed).then_inc(wd_done, 1)
                v.wait_ge(wd_done, 2 * i + 1)
                lo(wd_lo[:, :, i, :], signed, wd_hi[:, :, i, :]).then_inc(wd_done, 1)

            def output(i, s):
                v.wait_ge(zhi_done, i * UNITS + s - 2)
                lo(z_lo[:, (s - 3) % 2, :], bank_z[(s - 3) % 2][:, 0:SEQ], z_hi[:, (s - 3) % 2, :])\
                    .then_inc(z_split, 1)

            def head_step(i, s, prev=True, own=True, following=True):
                attending = prev if s < 3 else own
                if attending and s % 2 == 0:
                    output(i, s)
                if prev if s < 2 else own:
                    v.wait_ge(t_hi, i * UNITS + s - 1)
                    lo(pt_lo[:, s % 2, 1:4, :], bank_t[:, 0:3 * P].rearrange("p (a c) -> p a c", a=3),
                       pt_hi[:, s % 2, 1:4, :]).then_inc(t_split, 1)
                if own:
                    maxima(i, s)
                if s in OUT_AT and (prev if s < 4 else own):
                    b = OUT_AT[s]
                    v.wait_ge(o_ready, i * BATCH + {2: -1, 3: 0, 0: 1, 1: 2}[b])
                    nc.vector.tensor_tensor(xres[:, 2 * b:2 * b + 2, :], two(bank_o[:, :]),
                                            xres[:, 2 * b:2 * b + 2, :], ALU.add).then_inc(o_added, 1)
                if s == WD_AT:
                    wd_piece(i)
                if own and s % 2 == 0:
                    fp8_round(i, s)
                if own:
                    v.wait_ge(exp_done, i * UNITS + s + 1)
                    nc.vector.reciprocal(rinv[:, s, :], rsum[:, s, :]).then_inc(rinv_done, 1)
                if attending and s % 2 == 1:
                    output(i, s)
                for half, n, number in proj_tiles(s, own, following):
                    proj_part(half, n, i * TPP + number)
                if own and s % 2 == 1:
                    fp8_round(i, s)
                if s in OUT_AT and not following and (own if s > 4 else not own):
                    b = OUT_AT[s]
                    v.wait_ge(o_added, PAIRS * OPP - {2: 1, 3: 0, 0: 4, 1: 2}[b])
                    ln_stats(2 * b, 2).then_inc(stats_done, 1)

            def first_stats(b):
                for n in (b, b + 1):
                    v.wait_ge(loaded_x[n], 16)
                    for t in (2 * n, 2 * n + 1):
                        a = nc.vector.bn_stats(stats[:, t, :], xres[:, t, :])
                step(a)

            def first_guess(b):
                for t in range(2 * b, 2 * b + 4):
                    a = nc.vector.bn_aggr(mv[:, t, :], stats[:, t, :])
                step(a)
                step(ln_guess(2 * b, 4))

            def first_newton(b, steps):
                ve, y, tmp = (nwt[:, n, 2 * b:2 * b + 4] for n in range(3))
                for _ in range(steps):
                    step(nc.vector.tensor_tensor(tmp, y, y, ALU.mult))
                    step(nc.vector.scalar_tensor_tensor(out=tmp, in0=tmp, scalar=-0.5, in1=ve, op0=ALU.mult, op1=ALU.mult))
                    step(nc.vector.scalar_tensor_tensor(out=y, in0=tmp, scalar=1.5, in1=y, op0=ALU.add, op1=ALU.mult))

            def first_lo(b):
                v.wait_ge(lnt_hi, b + 1)
                lo(xt_lo[:, :, tokens(b)], two((bank_s + bank_z)[b][:, :]), xt_hi[:, :, tokens(b)])\
                    .then_inc(lnt_split, 1)

            first_stats(0)
            first_guess(0)
            first_newton(0, 3)
            ln_apply(xn[:, 0], 0)
            ln_apply(xn[:, 1], 1)
            first_stats(2)
            first_lo(0)
            first_lo(1)
            first_guess(2)
            first_newton(2, 2)
            proj_part(0, 0, 0)
            first_newton(2, 1)
            v.wait_ge(lnt_ready, 2)
            ln_apply(xn[:, 0], 2)
            ln_apply(xn[:, 1], 3)
            proj_part(0, 1, 1)
            proj_part(0, 2, 2)
            first_lo(2)
            first_lo(3)
            v.wait_ge(loaded_const, 16 * N_CONST)
            nc.vector.scalar_tensor_tensor(out=cam[:, 0:1], in0=vec(V_W1), scalar=0.5, in1=vec(V_W0),
                                           op0=ALU.mult, op1=ALU.add).then_inc(cam_arg, 1)
            for n in range(3, CH):
                proj_part(0, n, n)
            v.wait_ge(cam_exp, 1)
            step(nc.vector.tensor_scalar(cam[:, 2:3], cam[:, 1:2], 1.0, None, ALU.add))
            step(nc.vector.reciprocal(cam[:, 3:4], cam[:, 2:3]))
            step(nc.vector.tensor_scalar(wscale[:, :], vec(V_WUP, 2 * C1), 1.0 / 16, None, ALU.mult))
            for s in range(UNITS):
                head_step(0, s, prev=False)
            with v.Fori(1, PAIRS - 1) as i:
                for s in range(UNITS):
                    head_step(i, s)
            for s in range(FIRST_TAIL_STEP):
                head_step(PAIRS - 1, s, following=False)

            def onto(e):
                stage, b, _ = e
                v.wait_ge(o_ready, PAIRS * BATCH + ONTO[e] + 1)
                res, got, tmp = xres[:, 2 * b:2 * b + 2, :], two(bank_o[:, :]), bfly[:, :, :]
                if stage == "down0":
                    a = nc.vector.tensor_tensor(tmp, got, row(R_DS, 2), ALU.mult)
                elif stage == "out":
                    a = nc.vector.tensor_tensor(tmp, got, row(R_PB, 2), ALU.add)
                else:
                    if b >= 1:
                        v.wait_ge(x_final, b)
                    a = nc.vector.scalar_tensor_tensor(out=tmp, in0=got, scalar=1.0 / 32, in1=row(R_WDP, 2),
                                                       op0=ALU.mult, op1=ALU.mult)
                a.then_inc(o_added, 1)
                v.wait_ge(o_added, PAIRS * OPP + ONTO[e] + 1)
                a = nc.vector.tensor_tensor(res, tmp, res, ALU.add)
                if stage == "down1":
                    a.then_inc(x_final, 1)
                else:
                    step(a)
                    ln_stats(2 * b, 2).then_inc(stats_done, 1)

            def rest(e):
                v.wait_ge(rot_hi, HI[e] + 1)
                return rot(ROT[e])

            v.wait_ge(loaded_rows, 16)
            for e in TAIL:
                stage, b, c = e
                if stage == "head" and b < UNITS:
                    head_step(PAIRS - 1, b, following=False)
                elif stage == "head":
                    head_step(PAIRS, b - UNITS, own=False, following=False)
                elif stage in ("norm1", "norm2", "norm3"):
                    v.wait_ge(root_done, ROOT["root" + stage[4], b, 0] + 1)
                    if e == ("norm1", 2, 0):
                        v.wait_ge(prep_pool, PAIRS)
                    ln_apply(normed[b], b)
                elif stage in ("ln1", "ln2", "had"):
                    lo(xt_lo[:, :, tokens(b)], two(rest(e)[:, :]), xt_hi[:, :, tokens(b)]).then_inc(rot_free, 1)
                elif stage == "ln3":
                    bank = rest(e)
                    for k in range(KC):
                        a = nc.vector.scalar_tensor_tensor(
                            out=xt_lo[:, k, tokens(b)], in0=bank[:, k * SEQ:(k + 1) * SEQ], scalar=vec(V_SU + k),
                            in1=f32(xt_hi[:, k, tokens(b)]), op0=ALU.mult, op1=ALU.subtract)
                    a.then_inc(rot_free, 1)
                elif stage in ("gu0", "gu1"):
                    g = GU[e]
                    if g >= SLOTS:
                        v.wait_ge(fuse_lo, g - SLOTS + 1)
                    scale = vec(V_US0 + c) if stage == "gu0" else wscale[:, c:c + 1]
                    nc.vector.scalar_tensor_tensor(out=fused[g % SLOTS], in0=rest(e)[:, SEQ:2 * SEQ], scalar=scale,
                                                   in1=gate_act[g % SLOTS], op0=ALU.mult, op1=ALU.mult)\
                        .then_inc(rot_free, 1)
                elif stage in ("down0", "out", "down1"):
                    onto(e)
                elif stage == "proj" and c < 2:
                    bank, hi, low = rest(e), attn1(reg_hi, b)[c], attn1(reg_lo, b)[c]
                    for n in range(2):
                        a = nc.vector.scalar_tensor_tensor(
                            out=low[:, n, :], in0=bank[:, n * SEQ:(n + 1) * SEQ], scalar=vec(V_BQK + 2 * c + n),
                            in1=f32(hi[:, n, :]), op0=ALU.add, op1=ALU.subtract)
                    a.then_inc(rot_free, 1)
                elif stage == "proj":
                    v.wait_ge(rot_ready, ROT[e] + 1)
                    if b == 0:
                        v.wait_ge(w_o, PAIRS + 1)
                    else:
                        v.wait_ge(v_split, b)
                    nc.vector.tensor_tensor(v_sum, two(rot(ROT[e])[:, :]), row(R_VB, 2), ALU.add)\
                        .then_inc(rot_free, 1)
                elif stage == "vsplit":
                    v.wait_ge(v_hi_done, b + 1)
                    lo(attn1(reg_lo, b)[2], v_sum, attn1(reg_hi, b)[2]).then_inc(v_split, 1)
                elif stage in ("score", "score2"):
                    n = SOFT[e]
                    m = UNITS + n
                    v.wait_ge(s_ready, ALL_UNITS + n + 1)
                    nc.vector.reduce_max(rmax[:, m, :], two(bank_z[n % 2][:, :]), AX_X).then_inc(max_done, 1)
                    v.wait_ge(max_done, ALL_UNITS + n + 1)
                    nc.vector.tensor_scalar(nbias[:, m, :], rmax[:, m, :], -SCALE1, None, ALU.mult)\
                        .then_inc(nbias_done, 1)
                elif stage in ("sum", "sum2"):
                    n = SOFT["score" + stage[3:], b, 0]
                    v.wait_ge(exp_done, ALL_UNITS + n + 1)
                    nc.vector.reciprocal(rinv[:, UNITS + n, :], rsum[:, UNITS + n, :]).then_inc(rinv_done, 1)
                elif stage in ("turn", "turn2"):
                    m = TURN[e]
                    v.wait_ge(t_hi, ALL_UNITS + m + 1)
                    lo(pt_lo[:, m % 2, :, :], bank_t[:, :].rearrange("p (a c) -> p a c", a=4), pt_hi[:, m % 2, :, :])\
                        .then_inc(t_split, 1)
                elif stage == "ctx":
                    q0_hi, q0_lo = (attn1(r, b)[0][:, 0, :] for r in (reg_hi, reg_lo))
                    rest(e)
                    if b >= 1:
                        v.wait_ge(camq_split, b)
                    nc.vector.scalar_tensor_tensor(out=cam_total, in0=cam_tanh, scalar=cam[:, 3:4],
                                                   in1=f32(q0_hi), op0=ALU.mult, op1=ALU.add).then_inc(rot_free, 1)
                    v.wait_ge(rot_free, ROT[e] + 1)
                    nc.vector.tensor_tensor(cam_total, cam_total, f32(q0_lo), ALU.add).then_inc(camq_sum, 1)
                elif stage == "camq":
                    q0_hi, q0_lo = (attn1(r, b)[0][:, 0, :] for r in (reg_hi, reg_lo))
                    v.wait_ge(camq_hi, b + 1)
                    lo(q0_lo, cam_total, q0_hi).then_inc(camq_split, 1)
                elif stage == "mix":
                    lo(z_lo[:, :, :], two(rest(e)[:, :]), z_hi[:, :, :]).then_inc(rot_free, 1)

        @block.gpsimd
        def _(pool):
            def hi(dst, src):
                return nc.gpsimd.tensor_scalar(dst, src, 1.0, 1.0, ALU.mult, ALU.mult)

            def lo(dst, src, hi_part):
                return nc.gpsimd.tensor_tensor(dst, src, f32(hi_part), ALU.subtract)

            def raw_qkv(which):
                return qkv_raw[:, which * 2 * D:(which + 1) * 2 * D].rearrange("p (k m) -> p k m", k=KC)

            def raw_wo():
                return wo_raw[:, :].rearrange("p (h m) -> p h m", h=2)

            def wait(s, value):
                pool.wait_ge(s, value)
                pool.sem_inc(pool_went, 1)

            def butterfly(dst, src, d):
                s, t = (x.rearrange("p (g a x) -> p g a x", a=2, x=d * DCOLS) for x in (src, dst))
                nc.gpsimd.tensor_tensor(t[:, :, 0, :], s[:, :, 0, :], s[:, :, 1, :], ALU.add)
                return nc.gpsimd.tensor_tensor(t[:, :, 1, :], s[:, :, 0, :], s[:, :, 1, :], ALU.subtract)

            def head_step(i, s, prev=True):
                def pstep(ins, n):
                    ins.then_inc(pool_step, 1)
                    wait(pool_step, i * 7 + n)

                def split_w(which, n):
                    if which == 0:
                        wait(loaded_qkv, 16 * (i + 1))
                    wait(proj_ready, i * TPP + CH + 2 * which + 2)
                    pstep(hi(wqkv_hi[:, which, :, :], raw_qkv(which)), n)
                    lo(wqkv_lo[:, which, :, :], raw_qkv(which), wqkv_hi[:, which, :, :])\
                        .then_inc((w_q, w_k, w_v)[which], 1)

                wait(rinv_done, i * UNITS + s + 1)
                nc.gpsimd.tensor_scalar(probn[:, s % 2, 0:P], prob[:, s % 2, 0:P], rinv[:, s, 0:1], 1.0,
                                        ALU.mult, ALU.mult)
                nc.gpsimd.tensor_scalar(probn[:, s % 2, P:3 * P], prob[:, s % 2, P:3 * P], rinv[:, s, 1:2], 1.0,
                                        ALU.mult, ALU.mult).then_inc(norm_done, 1)
                if s == 1:
                    split_w(0, 1)
                    wait(loaded_prep, 16 * (i + 1))
                    pstep(butterfly(bfly[:, 0, 0:WD_PIECE], prep[:, UG_PIECE:UG_PIECE + WD_PIECE], 1), 2)
                elif s == 2:
                    pstep(butterfly(bfly[:, 1, 0:WD_PIECE], bfly[:, 0, 0:WD_PIECE], 2), 3)
                    split_w(1, 4)
                elif s == 3:
                    if prev:
                        wait(o_ready, i * BATCH)
                        split_wo(i)
                    pstep(butterfly(bfly[:, 0, 0:WD_PIECE], bfly[:, 1, 0:WD_PIECE], 4), 5)
                elif s == 4:
                    split_w(2, 6)
                    pstep(hi(bf_hi[:, :], bfly[:, 0, 0:WD_PIECE]), 7)
                    lo(bf_lo[:, :], bfly[:, 0, 0:WD_PIECE], bf_hi[:, :]).then_inc(bf_ready, 1)
                elif s == 5:
                    wait(ug_hi_done, i + 1)
                    lo(ug_lo[:, i, :], prep[:, 0:UG_PIECE], ug_hi[:, i, :]).then_inc(prep_pool, 1)

            def split_wo(i):
                wait(loaded_wo, 16 * (i + 1))
                hi(wo_hi[:, :, :], raw_wo()).then_inc(wo_hi_done, 1)
                wait(wo_hi_done, i + 1)
                lo(wo_lo[:, :, :], raw_wo(), wo_hi[:, :, :]).then_inc(w_o, 1)

            for r in (pt_hi, pt_lo):
                a = nc.gpsimd.memset(f32(r[:, :, 0, :]), 0.0)
            a.then_inc(zeros_ready, 1)
            for which in range(3):
                pool.wait_ge(loaded_first[which], 16)
                hi(wqkv_hi[:, which, :, :], raw_qkv(which)).then_inc(pool_first, 1)
                pool.wait_ge(pool_first, which + 1)
                lo(wqkv_lo[:, which, :, :], raw_qkv(which), wqkv_hi[:, which, :, :])\
                    .then_inc((w_q, w_k, w_v)[which], 1)
            split_wo(0)
            for s in range(UNITS):
                head_step(0, s, prev=False)
            with pool.Fori(1, PAIRS - 1) as i:
                for s in range(UNITS):
                    head_step(i, s)
            for s in range(FIRST_TAIL_STEP):
                head_step(PAIRS - 1, s)

            steps = 0
            for e in TAIL:
                stage, b, c = e
                if stage == "head" and b < UNITS:
                    head_step(PAIRS - 1, b)
                elif e == ("head", UNITS + 3, 0):
                    pool.wait_ge(o_ready, PAIRS * BATCH)
                    split_wo(PAIRS)
                elif stage in ("root1", "root2", "root3"):
                    n = stats_before(int(stage[4]), b)
                    ve, y, tmp = (nwt[:, k, 2 * b:2 * b + 2] for k in range(3))
                    pool.wait_ge(stats_done, n + 1)
                    for k in range(3):
                        for ins in (lambda: nc.gpsimd.tensor_tensor(tmp, y, y, ALU.mult),
                                    lambda: nc.gpsimd.tensor_tensor(tmp, tmp, ve, ALU.mult),
                                    lambda: nc.gpsimd.tensor_scalar(tmp, tmp, -0.5, 1.5, ALU.mult, ALU.add)):
                            ins().then_inc(newton, 1)
                            steps += 1
                            pool.wait_ge(newton, steps)
                        a = nc.gpsimd.tensor_tensor(y, y, tmp, ALU.mult)
                        if k < 2:
                            a.then_inc(newton, 1)
                            steps += 1
                            pool.wait_ge(newton, steps)
                    a.then_inc(root_done, 1)
                elif stage in ("sum", "sum2"):
                    n = SOFT["score" + stage[3:], b, 0]
                    pool.wait_ge(rinv_done, ALL_UNITS + n + 1)
                    for qt in range(2):
                        ts = slice(qt * SEQ, (qt + 1) * SEQ)
                        a = nc.gpsimd.tensor_scalar(probn[:, n % 2, ts], prob[:, n % 2, ts],
                                                    rinv[:, UNITS + n, qt:qt + 1], 1.0, ALU.mult, ALU.mult)
                    a.then_inc(norm_done, 1)
                elif stage in ("hid0", "hid1"):
                    gu = "gu" + stage[3]
                    g = GU[gu, b, c]
                    pool.wait_ge(fuse_hi, g + 1)
                    lo(hidden(reg_lo, gu, b)[:, c, :], fused[g % SLOTS], hidden(reg_hi, gu, b)[:, c, :])\
                        .then_inc(fuse_lo, 1)


def kernel(L0_attn_x, L0_attn_W_K, L0_attn_W_Q, L0_attn_W_V, L0_attn_W_O, L0_ffn_gate_w, L0_ffn_up_w, L0_ffn_down_w,
           L0_ffn_gate_scale, L0_ffn_up_scale, L0_ffn_down_scale, L1_attn_c_attn_w, L1_attn_c_attn_b,
           L1_attn_c_proj_w, L1_attn_c_proj_b, L1_attn_cam_gate, L1_attn_cam_w0, L1_attn_cam_w1, L1_ffn_SU_ug,
           L1_ffn_SU_dp, L1_ffn_Wscale_ug, L1_ffn_Wscale_dp, L1_ffn_W_up, L1_ffn_W_gate, L1_ffn_W_down):
    args_by_name = dict(locals())
    import numpy as np
    import concourse.bacc as bacc
    from concourse import mybir as mb
    from concourse.bass_utils import run_bass_kernel_spmd

    a = {k: np.asarray(x) for k, x in args_by_name.items()}

    def chunks(w):
        return w.reshape(-1, P, w.shape[-1]).transpose(1, 0, 2)

    def pair_qkv(w):
        w = w.reshape(PAIRS, 2 * DH, KC, P).transpose(0, 3, 2, 1)
        return w.reshape(PAIRS, P, -1)

    wo = a["L0_attn_W_O"].T.reshape(PAIRS, 2, P, D).transpose(0, 2, 1, 3).reshape(PAIRS, P, -1)
    pairs = np.concatenate([pair_qkv(a["L0_attn_W_Q"]), pair_qkv(a["L0_attn_W_K"]), pair_qkv(a["L0_attn_W_V"]), wo], -1)
    c_attn = chunks(a["L1_attn_c_attn_w"]).reshape(P, KC, 3, D).transpose(0, 2, 1, 3).reshape(P, -1)
    c_proj = chunks(a["L1_attn_c_proj_w"]).reshape(P, -1)
    pairs = np.concatenate([pairs, np.concatenate([c_attn, c_proj], -1)[None]], 0)

    up, gate = (chunks(a["L1_ffn_W_" + n].T).reshape(P, KC, C1, P) for n in ("up", "gate"))
    ug = np.stack([gate, up], 3).reshape(P, PAIRS, UG_PIECE).transpose(1, 0, 2)
    wd = chunks(a["L1_ffn_W_down"].T).reshape(P, C1, PAIRS, DCOLS).transpose(2, 0, 1, 3).reshape(PAIRS, P, -1)
    q8 = np.concatenate([chunks(a["L0_ffn_" + n]).reshape(P, -1) for n in ("gate_w", "up_w", "down_w")], -1)
    q8 = q8.reshape(P, PAIRS, Q8_PIECE).transpose(1, 0, 2)
    prep = np.concatenate([ug, wd, q8], -1)

    had = np.ones((1, 1), np.float32)
    while len(had) < P:
        had = np.block([[had, had], [had, -had]])
    mask = np.where(np.arange(P)[None, :] > np.arange(P)[:, None], np.float32(MASKED), np.float32(0))
    mats = np.concatenate([np.eye(P, dtype=np.float32), had, -had, mask], 1).astype(np.float32)

    def cols(x):
        return x.reshape(-1, P).T

    vecs = np.concatenate(
        [cols(a["L1_attn_c_attn_b"][:2 * D]), cols(a["L1_ffn_SU_ug"]), cols(a["L1_ffn_SU_dp"]),
         cols(a["L0_ffn_gate_scale"]), cols(a["L0_ffn_up_scale"]), cols(a["L1_ffn_Wscale_ug"]),
         cols(a["L1_attn_cam_gate"]), np.repeat(a["L1_attn_cam_w0"][None], P, 0),
         np.repeat(a["L1_attn_cam_w1"][None], P, 0)], 1)
    rows = np.stack([a["L0_ffn_down_scale"], a["L1_attn_c_attn_b"][2 * D:], a["L1_attn_c_proj_b"],
                     a["L1_ffn_Wscale_dp"]], 0)
    rows = np.repeat(rows[None], P, 0)

    arrays = {n: np.ascontiguousarray(x) for n, x in (
        ("x", a["L0_attn_x"]), ("pairs", pairs), ("prep", prep), ("mats", mats), ("vecs", vecs), ("rows", rows))}
    nc = bacc.Bacc("TRN2", target_bir_lowering=False, num_devices=1)
    args = [nc.dram_tensor(f"in_{n}", x.shape, mb.dt.from_np(x.dtype), kind="ExternalInput").ap()
            for n, x in arrays.items()]
    out = nc.dram_tensor("out", (BATCH, SEQ, D), mb.dt.float32, kind="ExternalOutput").ap()
    build_program(nc, *args, out)
    r = run_bass_kernel_spmd(nc, [{f"in_{n}": x for n, x in arrays.items()}], core_ids=[0])
    return r.results[0]["out"]
```

```python
from contextlib import ExitStack

import concourse.bass as bass
from concourse import mybir

F32 = mybir.dt.float32
F32R = mybir.dt.float32r
BF16 = mybir.dt.bfloat16
I32 = mybir.dt.int32
ALU = mybir.AluOpType
ACT = mybir.ActivationFunctionType
AX_X = mybir.AxisListType.X

P = 128
BATCH, SEQ, D = 4, 256, 256
TOK = BATCH * SEQ
TILES = TOK // P
KC = D // P
HEADS, DH = 16, 128
PAIRS = HEADS // 2
UNITS = 2 * BATCH
I0 = 768
C0 = I0 // P
I1 = 1024
C1 = I1 // P
HALF = TOK // 2
WARMING = 36
SLOTS = 4

QKV_COLS = 3 * KC * 2 * DH
WO_COLS = 2 * D
PAIR_COLS = QKV_COLS + WO_COLS
UG_PIECE = KC * 2 * I1 // PAIRS
WD_PIECE = C1 * D // PAIRS
Q8_PIECE = 3 * KC * I0 // PAIRS
PREP_COLS = UG_PIECE + WD_PIECE + Q8_PIECE
DCOLS = D // PAIRS

INV_SQRT_DH = 1.0 / float(DH) ** 0.5
SCALE1 = 0.25
EPS = 1e-5
FP8_MAX = 448.0
FP8_MIN_NORMAL = 2.0 ** -6
ROUND_TO_4_BITS = 1.5 * 2.0 ** 20
MASKED = -1e10

V_BQK, V_SU, V_SUDP, V_GS0, V_US0, V_WUP, V_WGATE, V_CAMG, V_W0, V_W1, V_N = (
    0, 4, 6, 14, 20, 26, 34, 42, 43, 44, 45)
R_DS, R_VB, R_PB, R_WDP = range(4)
M_ID, M_H, M_NH, M_MASK, M_N = 0, P, 2 * P, 3 * P, 4 * P

TILES_AT = (((1, 0), (1, 1)), ((1, 2),), ((1, 3),), ((1, 4),), ((1, 5), (0, 0)), ((0, 1), (0, 2)), ((0, 3),),
            ((0, 4), (0, 5)))
STEP_NAMES = (
    ("turn", "values", "scores", "sums", "tile", "tile", "split"),
    ("turn", "scores", "out", "sums", "values", "tile", "round", "split"),
    ("turn", "values", "scores", "round", "sums", "tile", "split"),
    ("turn", "scores", "out", "sums", "values", "ughi", "tile", "round", "split"),
    ("turn", "values", "scores", "round", "sums", "tile", "tile", "split"),
    ("turn", "scores", "out", "sums", "values", "tile", "tile", "split"),
    ("turn", "values", "scores", "hwd", "round", "sums", "tile"),
    ("turn", "scores", "out", "sums", "values", "tile", "tile", "round"))
STEP_PIECES = [[(name, s, names[:n].count(name)) for n, name in enumerate(names)] for s, names in enumerate(STEP_NAMES)]
OUT_USES = {1: -2, 3: -1, 5: 0, 7: 2, UNITS + 1: 3, UNITS + 3: 4}
OUT_DONE = {1: -1, 3: 0, 5: 1, 7: 2, UNITS + 1: 3, UNITS + 3: 4}


def pieces(s, prev=True):
    first = {"values": 3, "turn": 2, "out": 5}
    return [p for p in STEP_PIECES[s] if prev or s >= first.get(p[0], 0)]


ORDER = """
turn:0 scores:0 sums:0 values:0 tile:0 turn:1 scores:1 out:1 tile:0.1 sums:1 values:1 turn:2 scores:2 round:1
round:2 split:1 sums:2 values:2 tile:1 turn:3 tile:2 scores:3 round:3 round:4 split:2 sums:3 out:3 values:3
tile:3 round:6 turn:4 tile:4 values:4 split:3 turn:5 scores:4 scores:5 split:4 sums:4 out:5 sums:5 stats1:0
values:5 ughi:3 root1:0 values:6 turn:6 scores:6 hwd:6 round:7 norm1:0 sums:6 turn:7 split:5 out:7 values:7
ln1:0 values:8 scores:7 stats1:1 sums:7 turn:8 out:9 stats1:2 gu0:0.0 gu0:0.1 values:9 root1:1 turn:9 hid0:0.0
hid0:0.1 norm1:1 gu0:0.2 gu0:0.3 root1:2 gu0:0.4 values:10 ln1:1 norm1:2 hid0:0.2 gu0:0.5 hid0:0.3 out:11
hid0:0.4 hid0:0.5 gu0:1.0 stats1:3 gu0:1.1 ln1:2 hid0:1.0 gu0:1.2 down0:0 root1:3 hid0:1.1 hid0:1.2 gu0:1.3
norm1:3 gu0:1.4 hid0:1.3 hid0:1.4 gu0:1.5 stats2:0 gu0:2.0 hid0:1.5 root2:0 ln1:3 gu0:2.1 hid0:2.0 down0:1
norm2:0 hid0:2.1 gu0:2.2 gu0:2.3 gu0:2.4 stats2:1 hid0:2.2 hid0:2.3 hid0:2.4 gu0:2.5 ln2:0 hid0:2.5 gu0:3.0
gu0:3.1 gu0:3.2 root2:1 proj:0.0 norm2:1 wosplit:0 proj:0.1 proj:0.2 hid0:3.0 gu0:3.3 ln2:1 score:0 down0:2
hid0:3.1 sum:0 stats2:2 root2:2 hid0:3.2 proj:1.0 proj:1.1 hid0:3.3 vsplit:0 pturn:0 score:1 norm2:2 sum:1 ctx:0
gu0:3.4 camq:0 gu0:3.5 proj:1.2 hid0:3.4 ln2:2 pturn:1 vsplit:1 hid0:3.5 score2:0 down0:3 sum2:0 stats2:3
proj:2.0 proj:2.1 pturn2:0 ctx:1 proj:2.2 camq:1 root2:3 norm2:3 mix:0 score:2 score2:1 sum:2 proj_out:0 ln2:3
vsplit:2 sum2:1 pturn:2 stats3:0 proj:3.0 ctx:2 root3:0 pturn2:1 proj:3.1 norm3:0 proj:3.2 camq:2 mix:1 ln3:0
score:3 proj_out:1 had:0 score2:2 sum:3 stats3:1 gu1:0.0 gu1:0.1 root3:1 sum2:2 hid1:0.0 hid1:0.1 gu1:0.2
norm3:1 pturn:3 gu1:0.3 vsplit:3 gu1:0.4 hid1:0.2 pturn2:2 ln3:1 ctx:3 gu1:0.5 mix:2 hid1:0.3 gu1:0.6 hid1:0.4
had:1 hid1:0.5 camq:3 gu1:0.7 proj_out:2 stats3:2 hid1:0.6 gu1:1.0 hid1:0.7 score2:3 root3:2 sum2:3 gu1:1.1
hid1:1.0 norm3:2 down1:0 pturn2:3 ln3:2 hid1:1.1 gu1:1.2 gu1:1.3 hid1:1.2 hid1:1.3 gu1:1.4 gu1:1.5 mix:3 had:2
hid1:1.4 gu1:1.6 gu1:1.7 hid1:1.5 proj_out:3 stats3:3 hid1:1.6 root3:3 hid1:1.7 gu1:2.0 norm3:3 hid1:2.0 gu1:2.1
hid1:2.1 gu1:2.2 down1:1 ln3:3 hid1:2.2 gu1:2.3 gu1:2.4 had:3 hid1:2.3 hid1:2.4 gu1:2.5 gu1:2.6 gu1:2.7 hid1:2.5
hid1:2.6 hid1:2.7 gu1:3.0 gu1:3.1 hid1:3.0 hid1:3.1 gu1:3.2 hid1:3.2 gu1:3.3 gu1:3.4 gu1:3.5 hid1:3.3 gu1:3.6
down1:2 hid1:3.4 hid1:3.5 hid1:3.6 gu1:3.7 hid1:3.7 down1:3
"""


def stages():
    entries = []
    for entry in ORDER.split():
        stage, at = entry.split(":")
        b, part = at.split(".") if "." in at else (at, 0)
        entries.append((stage, int(b), int(part)))
    return entries


TAIL = stages()
HEAD_PIECES = {name for step in STEP_PIECES for name, _, _ in step}


def numbering(*stages, without=()):
    return {e: n for n, e in enumerate(e for e in TAIL if e[0] in stages and e not in without)}


IN_ROT = ("ln1", "ln2", "ln3", "gu0", "gu1", "proj", "ctx", "mix", "had")
ROT = numbering(*IN_ROT)
HI = numbering(*IN_ROT, without=[("proj", b, 2) for b in range(BATCH)])
ADDED = numbering("down0", "proj_out")
GU = numbering("gu0", "gu1")
SOFT = numbering("score", "score2")
TURN = numbering("pturn", "pturn2")
ONTO = numbering("down0", "proj_out", "down1")
NORM = numbering("norm1", "norm2", "norm3")
STATS = numbering("stats1", "stats2", "stats3")
ROOT = numbering("root1", "root2", "root3")


def build_program(nc, x_in, pair_in, prep_in, mats_in, vecs_in, rows_in, out):
    with ExitStack() as ctx:
        def sb(name, shape, dt=F32):
            return ctx.enter_context(nc.sbuf_tensor(name, shape, dt))

        def psum(name):
            return ctx.enter_context(nc.psum_tensor(name, [P, 512], F32))

        def sem(name):
            return ctx.enter_context(nc.semaphore(name))

        xres = sb("xres", [P, TILES, D])
        xt_hi = sb("xt_hi", [P, KC, TOK], F32R)
        xt_lo = sb("xt_lo", [P, KC, TOK], F32R)
        qkv_raw = sb("qkv_raw", [P, QKV_COLS])
        wo_raw = sb("wo_raw", [P, WO_COLS])
        wqkv_hi = sb("wqkv_hi", [P, 3, KC, 2 * DH], F32R)
        wqkv_lo = sb("wqkv_lo", [P, 3, KC, 2 * DH], F32R)
        wo_hi = sb("wo_hi", [P, 2, D], F32R)
        wo_lo = sb("wo_lo", [P, 2, D], F32R)
        REG = 6 * TOK
        reg_hi = sb("reg_hi", [P, REG], F32R)
        reg_lo = sb("reg_lo", [P, REG], F32R)
        prob = sb("prob", [P, 2, 512])
        probn = sb("probn", [P, 2, 512])
        pt_hi = sb("pt_hi", [P, 2, 4, P], F32R)
        pt_lo = sb("pt_lo", [P, 2, 4, P], F32R)
        z_hi = sb("z_hi", [P, 2, SEQ], F32R)
        z_lo = sb("z_lo", [P, 2, SEQ], F32R)
        q8 = sb("q8", [P, PAIRS, Q8_PIECE], F32R)
        ug_hi = sb("ug_hi", [P, PAIRS, UG_PIECE], F32R)
        ug_lo = sb("ug_lo", [P, PAIRS, UG_PIECE], F32R)
        wd_hi = sb("wd_hi", [P, C1, PAIRS, DCOLS], F32R)
        wd_lo = sb("wd_lo", [P, C1, PAIRS, DCOLS], F32R)
        prep = sb("prep", [P, PREP_COLS])
        scratch = sb("scratch", [P, Q8_PIECE])
        bfly = sb("bfly", [P, 2, WD_PIECE])
        bf_hi = sb("bf_hi", [P, WD_PIECE], F32R)
        bf_lo = sb("bf_lo", [P, WD_PIECE], F32R)
        fused_ab = sb("fused_ab", [P, 2 * SEQ])
        xn = sb("xn", [P, 2, 2, D])
        ident = sb("ident", [P, P])
        had_p = sb("had_p", [P, P], F32R)
        had_n = sb("had_n", [P, P], F32R)
        ident_b = sb("ident_b", [P, P], BF16)
        mask_b = sb("mask_b", [P, P], BF16)
        vecs = sb("vecs", [P, V_N])
        rows = sb("rows", [P, 4, D])
        stats = sb("stats", [P, TILES, 6])
        mv = sb("mv", [P, TILES, 2])
        nwt = sb("nwt", [P, 4, TILES])
        cam = sb("cam", [P, 6])
        wscale = sb("wscale", [P, 2 * C1])
        rmax = sb("rmax", [P, 2 * UNITS, 2])
        nbias = sb("nbias", [P, 2 * UNITS, 2])
        rsum = sb("rsum", [P, 2 * UNITS, 2])
        rinv = sb("rinv", [P, 2 * UNITS, 2])

        bank_pj = [psum("bank_pj0"), psum("bank_pj1")]
        bank_s = [psum("bank_s0"), psum("bank_s1")]
        bank_t = psum("bank_t")
        bank_z = [psum("bank_z0"), psum("bank_z1")]
        bank_o = psum("bank_o")
        bank_rot = bank_pj + bank_s

        q_hi, q_lo = (r[:, 0:2 * TOK].rearrange("p (h t) -> p h t", h=2) for r in (reg_hi, reg_lo))
        k_hi, k_lo = (r[:, 2 * TOK:4 * TOK].rearrange("p (h t) -> p h t", h=2) for r in (reg_hi, reg_lo))
        v_hi, v_lo = (r[:, 4 * TOK:6 * TOK].rearrange("p (t e) -> p t e", t=TILES) for r in (reg_hi, reg_lo))
        q8_all = q8[:, :, :].rearrange("p a b -> p (a b)")
        gate0_w = q8_all[:, 0:KC * I0].rearrange("p (k c m) -> p k c m", k=KC, c=C0)
        up0_w = q8_all[:, KC * I0:2 * KC * I0].rearrange("p (k c m) -> p k c m", k=KC, c=C0)
        down0_w = q8_all[:, 2 * KC * I0:3 * KC * I0].rearrange("p (c m) -> p c m", c=C0)
        ug_h, ug_l = (w[:, :, :].rearrange("p a b -> p (a b)").rearrange(
            "p (k c g m) -> p k c g m", k=KC, c=C1, g=2) for w in (ug_hi, ug_lo))
        wd_h, wd_l = (w[:, :, :, :].rearrange("p c a b -> p c (a b)") for w in (wd_hi, wd_lo))
        out_v = out.rearrange("b (t p) d -> p (b t) d", p=P)
        x_v = x_in.rearrange("b (t p) d -> p (b t) d", p=P)

        q8_pow = scratch
        gate_act = [qkv_raw[:, n * SEQ:(n + 1) * SEQ] for n in range(SLOTS)]
        fused = [r[:, n * SEQ:(n + 1) * SEQ] for r in (fused_ab, scratch) for n in range(2)]
        normed = [xn[:, 0], xn[:, 1]] + [
            prep[:, n * 2 * D:(n + 1) * 2 * D].rearrange("p (a c) -> p a c", a=2) for n in range(2)]
        v_sum = wo_raw[:, :].rearrange("p (a c) -> p a c", a=2)
        cam_tanh = qkv_raw[:, SLOTS * SEQ:(SLOTS + 1) * SEQ]
        cam_total = qkv_raw[:, (SLOTS + 1) * SEQ:(SLOTS + 2) * SEQ]

        def f32(ap):
            return ap.bitcast(F32)

        def hidden(r, stage, b):
            first, chunks = (b * C0 * SEQ, C0) if stage == "gu0" else (b % 3 * C1 * SEQ, C1)
            return r[:, first:first + chunks * SEQ].rearrange("p (c t) -> p c t", c=chunks)

        def attn1(r, b):
            part = r[:, b * 6 * SEQ:(b + 1) * 6 * SEQ].rearrange("p (n c) -> p n c", c=SEQ)
            return part[:, 0:2], part[:, 2:4], part[:, 4:6]

        def vec(c, n=1):
            return vecs[:, c:c + n]

        def row(r, n):
            return rows[:, r, :].unsqueeze(1).broadcast_to([P, n, D])

        def rot(n):
            return bank_rot[n % 4]

        loaded_x = [sem(f"loaded_x{b}") for b in range(BATCH)]
        loaded_ident = sem("loaded_ident")
        loaded_const = sem("loaded_const")
        loaded_rows = sem("loaded_rows")
        loaded_first = [sem(f"loaded_first{n}") for n in range(3)]
        loaded_qkv = sem("loaded_qkv")
        loaded_wo = sem("loaded_wo")
        loaded_prep = sem("loaded_prep")
        stored = sem("stored")
        consts_ready = sem("consts_ready")
        zeros_ready = sem("zeros_ready")
        dve = sem("dve")
        pool_first = sem("pool_first")
        pool_went = sem("pool_went")
        ug_hi_done = sem("ug_hi_done")
        pool_step = sem("pool_step")
        ln_done = sem("ln_done")
        lnt_ready = sem("lnt_ready")
        lnt_hi = sem("lnt_hi")
        lnt_split = sem("lnt_split")
        w_q = sem("w_q")
        w_k = sem("w_k")
        w_v = sem("w_v")
        wo_hi_done = sem("wo_hi_done")
        w_o = sem("w_o")
        proj_ready = sem("proj_ready")
        proj_hi = sem("proj_hi")
        proj_split = sem("proj_split")
        s_ready = sem("s_ready")
        max_done = sem("max_done")
        nbias_done = sem("nbias_done")
        exp_done = sem("exp_done")
        rinv_done = sem("rinv_done")
        norm_done = sem("norm_done")
        t_ready = sem("t_ready")
        t_hi = sem("t_hi")
        t_split = sem("t_split")
        z_ready = sem("z_ready")
        zhi_done = sem("zhi_done")
        z_split = sem("z_split")
        o_ready = sem("o_ready")
        o_added = sem("o_added")
        wdmm_ready = sem("wdmm_ready")
        bf_ready = sem("bf_ready")
        prep_q8 = sem("prep_q8")
        prep_pool = sem("prep_pool")
        wd_done = sem("wd_done")
        q8_step = sem("q8_step")
        rot_ready = sem("rot_ready")
        rot_hi = sem("rot_hi")
        rot_free = sem("rot_free")
        stats_done = sem("stats_done")
        newton = sem("newton")
        root_done = sem("root_done")
        v_hi_done = sem("v_hi_done")
        v_split = sem("v_split")
        fuse_hi = sem("fuse_hi")
        fuse_lo = sem("fuse_lo")
        camq_sum = sem("camq_sum")
        camq_hi = sem("camq_hi")
        camq_split = sem("camq_split")
        cam_arg = sem("cam_arg")
        cam_exp = sem("cam_exp")
        x_added = sem("x_added")
        x_final = sem("x_final")


        N_CONST = 2
        CH = 6
        TPP = 2 * CH
        OPP = BATCH + 1
        ALL_UNITS = PAIRS * UNITS
        def tile_at(s, k):
            half, n = TILES_AT[s][k]
            return half, n, (CH if half else TPP) + n

        def proj_dst(hi, half, n):
            q, k, v = (q_hi, k_hi, v_hi) if hi else (q_lo, k_lo, v_lo)
            if n < 4:
                return (q, k)[n // 2][:, n % 2, half * HALF:(half + 1) * HALF]
            t = half * (TILES // 2) + (n - 4) * 2
            return v[:, t:t + 2, :]

        def proj_src(n):
            bank = bank_pj[n % 2]
            return bank[:, :] if n < 4 else bank[:, :].rearrange("p (t e) -> p t e", t=2)

        def two(ap):
            return ap.rearrange("p (a c) -> p a c", a=2)

        def tokens(b):
            return slice(b * SEQ, (b + 1) * SEQ)

        block = ctx.enter_context(nc.Block())

        @block.sync
        def _(sp):
            sp.dma_start(ident[:, :], mats_in[:, M_ID:M_ID + P]).then_inc(loaded_ident, 16)
            for b in range(BATCH):
                sp.dma_start(xres[:, 2 * b:2 * b + 2, :], x_v[:, 2 * b:2 * b + 2, :]).then_inc(loaded_x[b], 16)
            for which in range(3):
                ws = slice(which * 2 * D, (which + 1) * 2 * D)
                sp.dma_start(qkv_raw[:, ws], pair_in[0, :, ws]).then_inc(loaded_first[which], 16)
            sp.dma_start(prob[:, 0, 0:3 * P], mats_in[:, M_H:M_N]).then_inc(loaded_const, 16)
            sp.dma_start(vecs[:, :], vecs_in).then_inc(loaded_const, 16)
            sp.dma_start(wo_raw[:, :], pair_in[0, :, QKV_COLS:PAIR_COLS]).then_inc(loaded_wo, 16)
            sp.dma_start(prep[:, :], prep_in[0]).then_inc(loaded_prep, 16)
            sp.dma_start(rows[:, :, :], rows_in).then_inc(loaded_rows, 16)
            sp.wait_ge(w_v, 1)
            sp.dma_start(qkv_raw[:, :], pair_in[1, :, 0:QKV_COLS]).then_inc(loaded_qkv, 16)
            with sp.Fori(0, PAIRS - 1) as i:
                sp.wait_ge(w_o, i + 1)
                sp.dma_start(wo_raw[:, :], pair_in[i + 1, :, QKV_COLS:PAIR_COLS]).then_inc(loaded_wo, 16)
                sp.wait_ge(w_v, i + 2)
                sp.dma_start(qkv_raw[:, :], pair_in[i + 2, :, 0:QKV_COLS]).then_inc(loaded_qkv, 16)
                sp.wait_ge(prep_q8, i + 1)
                sp.wait_ge(prep_pool, i + 1)
                sp.dma_start(prep[:, :], prep_in[i + 1]).then_inc(loaded_prep, 16)
            sp.wait_ge(w_o, PAIRS)
            sp.dma_start(wo_raw[:, :], pair_in[PAIRS, :, QKV_COLS:PAIR_COLS]).then_inc(loaded_wo, 16)
            for b in range(BATCH):
                sp.wait_ge(x_final, b + 1)
                sp.dma_start(out_v[:, 2 * b:2 * b + 2, :], xres[:, 2 * b:2 * b + 2, :]).then_inc(stored, 16)
            sp.wait_ge(stored, 16 * BATCH)

        @block.tensor
        def _(pe):
            def products(dst, pairs, start=True, stop=True):
                for n, (lhs, rhs) in enumerate(pairs):
                    mm = nc.tensor.matmul(dst, lhs, rhs, start=start and n == 0, stop=stop and n == len(pairs) - 1)
                return mm

            def three(lhs, rhs):
                (lh, ll), (rh, rl) = lhs, rhs
                return [(lh, rh), (lh, rl), (ll, rh)]

            def ln_transposes(dst, tok):
                for k in range(KC):
                    for t in range(2):
                        mm = nc.tensor.transpose(dst[:, k * SEQ + t * P:k * SEQ + (t + 1) * P],
                                                 tok[:, t, k * P:(k + 1) * P], ident[:, :])
                return mm

            def rot_wait(n):
                if n >= 4:
                    pe.wait_ge(rot_free, n - 3)
                elif n >= 2:
                    pe.wait_ge(exp_done, ALL_UNITS)
                else:
                    pe.wait_ge(proj_split, PAIRS * TPP)

            def proj_tile(half, n):
                bank = bank_pj[n % 2]
                if n < 4:
                    which, h = n // 2, n % 2
                    mm = products(bank[:, :], [
                        p for k in range(KC) for p in three(
                            [w[:, which, k, h * DH:(h + 1) * DH] for w in (wqkv_hi, wqkv_lo)],
                            [x[:, k, half * HALF:(half + 1) * HALF] for x in (xt_hi, xt_lo)])])
                else:
                    for t in range(2):
                        t0 = half * HALF + ((n - 4) * 2 + t) * P
                        mm = products(bank[:, t * 2 * DH:(t + 1) * 2 * DH], [
                            p for k in range(KC) for p in three(
                                [x[:, k, t0:t0 + P] for x in (xt_hi, xt_lo)],
                                [w[:, 2, k, :] for w in (wqkv_hi, wqkv_lo)])])
                mm.then_inc(proj_ready, 1)

            def scores(i, j, prev):
                b, h = divmod(j, 2)
                pe.wait_ge(proj_split, i * TPP + (4 if b < 2 else CH + 4))
                if j >= 2 or prev:
                    pe.wait_ge(exp_done, i * UNITS + j - 1)
                for qt in range(2):
                    t0 = b * SEQ + qt * P
                    dst = bank_s[j % 2][:, qt * SEQ:(qt + 1) * SEQ]
                    products(dst, three([q[:, h, t0:t0 + P] for q in (q_hi, q_lo)],
                                        [k[:, h, tokens(b)] for k in (k_hi, k_lo)]), start=qt == 0, stop=False)
                blocks = bank_s[j % 2][:, :].rearrange("p (a c) -> p a c", a=4)[:, 0:4:3, :]
                nc.tensor.matmul(blocks, ident_b[:, :], mask_b[:, :].unsqueeze(1).broadcast_to([P, 2, P]),
                                 start=False, stop=True).then_inc(s_ready, 1)

            def turn(i, j, prev):
                pe.wait_ge(norm_done, i * UNITS + j + 1)
                if j >= 1 or prev:
                    pe.wait_ge(t_split, i * UNITS + j)
                for n in range(3):
                    mm = nc.tensor.transpose(bank_t[:, n * P:(n + 1) * P], probn[:, j % 2, n * P:(n + 1) * P],
                                             ident[:, :])
                mm.then_inc(t_ready, 1)

            def attend(i, j, prev):
                b, h = divmod(j % UNITS, 2)
                if j >= 0:
                    pe.wait_ge(proj_split, i * TPP + (CH if b < 2 else TPP))
                else:
                    pe.wait_ge(proj_split, i * TPP)
                pe.wait_ge(t_split, i * UNITS + j + 1)
                if j >= 2 or prev:
                    pe.wait_ge(z_split, i * UNITS + j - 1)
                mm = products(bank_z[j % 2][:, 0:SEQ], [p for t in range(2) for p in three(
                    [v[:, 2 * b + t, h * DH:(h + 1) * DH] for v in (v_hi, v_lo)],
                    [pt[:, j % 2, 1:3, :] if t == 0 else pt[:, j % 2, 0:4:3, :] for pt in (pt_hi, pt_lo)])])
                mm.then_inc(z_ready, 1)

            def project(i, s, prev):
                pe.wait_ge(z_split, i * UNITS + s - 3)
                if s >= 5:
                    pe.wait_ge(w_o, i + 1)
                if prev or s > 5:
                    pe.wait_ge(o_added, i * OPP + OUT_USES[s])
                for qt in range(2):
                    mm = products(bank_o[:, qt * D:(qt + 1) * D], [p for h in range(2) for p in three(
                        [z[:, h, qt * P:(qt + 1) * P] for z in (z_hi, z_lo)],
                        [w[:, h, :] for w in (wo_hi, wo_lo)])])
                mm.then_inc(o_ready, 1)

            def wd_piece(i):
                pe.wait_ge(bf_ready, i + 1)
                pe.wait_ge(o_added, i * OPP + 1)
                products(bank_o[:, 0:WD_PIECE], [(had_p[:, :], bf_hi[:, :]), (had_p[:, :], bf_lo[:, :])])\
                    .then_inc(wdmm_ready, 1)

            def next_tile(i, half, n, number):
                if half == 0 and n % 2 == 0:
                    pe.wait_ge((w_q, w_k, w_v)[n // 2], i + 2)
                pe.wait_ge(proj_split, i * TPP + number - 1)
                proj_tile(half, n)

            def head_piece(i, piece, prev=True):
                name, s, k = piece
                if name == "values":
                    attend(i, s - 3, prev)
                elif name == "turn":
                    turn(i, s - 2, prev)
                elif name == "scores":
                    scores(i, s, prev)
                elif name == "out":
                    project(i, s, prev)
                elif name == "hwd":
                    wd_piece(i)
                elif name == "tile":
                    next_tile(i, *tile_at(s, k))

            def first_turned(b):
                pe.wait_ge(ln_done, b + 1)
                ln_transposes((bank_s + bank_z)[b], xn[:, b % 2]).then_inc(lnt_ready, 1)

            pe.wait_ge(loaded_ident, 16)
            for _ in range(WARMING):
                nc.tensor.transpose(bank_o[:, 0:P], ident[:, :], ident[:, :])
            first_turned(0)
            first_turned(1)
            pe.wait_ge(lnt_split, 2)
            for n in range(CH):
                if n % 2 == 0:
                    pe.wait_ge((w_q, w_k, w_v)[n // 2], 1)
                if n >= 2:
                    pe.wait_ge(proj_split, n - 1)
                proj_tile(0, n)
                if n == 3:
                    first_turned(2)
                    first_turned(3)
            pe.wait_ge(lnt_split, BATCH)
            pe.wait_ge(consts_ready, 1)
            pe.wait_ge(zeros_ready, 1)
            for s in range(UNITS):
                for piece in pieces(s, prev=False):
                    head_piece(0, piece, prev=False)
            with pe.Fori(1, PAIRS - 1) as i:
                for s in range(UNITS):
                    for piece in pieces(s):
                        head_piece(i, piece)

            def x_parts(k, t):
                return [x[:, k, t] for x in (xt_hi, xt_lo)]

            def rot_tile(e, contents):
                rot_wait(ROT[e])
                contents(rot(ROT[e])).then_inc(rot_ready, 1)

            def halves(bank, of):
                for n in range(2):
                    mm = products(bank[:, n * SEQ:(n + 1) * SEQ], of(n))
                return mm

            def gate_up(e):
                stage, b, c = e
                pe.wait_ge(rot_free, ROT["ln1" if stage == "gu0" else "had", b, 0] + 1)
                xs = [x_parts(k, tokens(b)) for k in range(KC)]
                if stage == "gu0":
                    rot_tile(e, lambda bank: halves(bank, lambda g: [
                        ((gate0_w, up0_w)[g][:, k, c, :], x) for k in range(KC) for x in xs[k]]))
                else:
                    rot_tile(e, lambda bank: halves(bank, lambda g: [
                        p for k in range(KC) for p in three([w[:, k, c, g, :] for w in (ug_h, ug_l)], xs[k])]))

            def down(e):
                stage, b, _ = e
                gu, chunks = ("gu0", C0) if stage == "down0" else ("gu1", C1)
                pe.wait_ge(o_added, PAIRS * OPP + ONTO[e])
                h_hi, h_lo = hidden(reg_hi, gu, b), hidden(reg_lo, gu, b)
                for c in range(chunks):
                    pe.wait_ge(fuse_lo, GU[gu, b, c] + 1)
                    for t in range(2):
                        hs = [h[:, c, t * P:(t + 1) * P] for h in (h_hi, h_lo)]
                        if stage == "down0":
                            pairs = [(h, down0_w[:, c, :]) for h in hs]
                        else:
                            pairs = three(hs, [wd_h[:, c, :], wd_l[:, c, :]])
                        mm = products(bank_o[:, t * D:(t + 1) * D], pairs, start=(c, t) == (0, 0),
                                      stop=(c, t) == (chunks - 1, 1))
                mm.then_inc(o_ready, 1)

            def qkv1(e):
                _, b, which = e
                pe.wait_ge(rot_free, ROT["ln2", b, 0] + 1)
                pe.wait_ge((w_q, w_k, w_v)[which], PAIRS + 1)

                def of(n):
                    if which < 2:
                        return [p for k in range(KC) for p in three(
                            [w[:, which, k, n * P:(n + 1) * P] for w in (wqkv_hi, wqkv_lo)], x_parts(k, tokens(b)))]
                    t0 = b * SEQ + n * P
                    return [p for k in range(KC) for p in three(
                        x_parts(k, slice(t0, t0 + P)), [w[:, 2, k, :] for w in (wqkv_hi, wqkv_lo)])]
                rot_tile(e, lambda bank: halves(bank, of))

            def scores1(e):
                stage, b, _ = e
                if stage == "score":
                    pe.wait_ge(rot_free, ROT["proj", b, 1] + 1)
                else:
                    pe.wait_ge(camq_split, b + 1)
                if SOFT[e] >= 2:
                    pe.wait_ge(exp_done, ALL_UNITS + SOFT[e] - 1)
                (qh, kh, _), (ql, kl, _) = attn1(reg_hi, b), attn1(reg_lo, b)
                halves(bank_z[SOFT[e] % 2], lambda qt: [p for k in range(1 if stage == "score" else 2) for p in three(
                    [q[:, k, qt * P:(qt + 1) * P] for q in (qh, ql)], [kh[:, k, :], kl[:, k, :]])]).then_inc(s_ready, 1)

            def turn1(e):
                stage, b, _ = e
                n = SOFT["score" if stage == "pturn" else "score2", b, 0]
                pe.wait_ge(norm_done, ALL_UNITS + n + 1)
                pe.wait_ge(t_split, ALL_UNITS + TURN[e])
                for kt in range(2):
                    for qt in range(2):
                        mm = nc.tensor.transpose(bank_t[:, kt * SEQ + qt * P:kt * SEQ + (qt + 1) * P],
                                                 probn[:, n % 2, qt * SEQ + kt * P:qt * SEQ + (kt + 1) * P], ident[:, :])
                mm.then_inc(t_ready, 1)

            def values1(e):
                stage, b, _ = e
                m = TURN["pturn" if stage == "ctx" else "pturn2", b, 0]
                pe.wait_ge(t_split, ALL_UNITS + m + 1)
                pe.wait_ge(v_split, b + 1)
                (_, _, vh), (_, _, vl) = attn1(reg_hi, b), attn1(reg_lo, b)

                def of(n):
                    es = slice(n * P, (n + 1) * P)
                    return [p for kt in range(2) for p in three(
                        [vh[:, kt, es], vl[:, kt, es]], [pt[:, m % 2, 2 * kt:2 * kt + 2, :] for pt in (pt_hi, pt_lo)])]
                rot_tile(e, lambda bank: products(bank[:, 0:SEQ], of(0)) if stage == "ctx" else halves(bank, of))

            def out1(e):
                pe.wait_ge(rot_free, ROT["mix", e[1], 0] + 1)
                pe.wait_ge(w_o, PAIRS + 1)
                pe.wait_ge(o_added, PAIRS * OPP + ONTO[e])
                halves(bank_o, lambda qt: [p for k in range(2) for p in three(
                    [z[:, k, qt * P:(qt + 1) * P] for z in (z_hi, z_lo)],
                    [w[:, k, :] for w in (wo_hi, wo_lo)])]).then_inc(o_ready, 1)

            def hadamard(e):
                b = e[1]
                pe.wait_ge(rot_free, ROT["ln3", b, 0] + 1)
                rot_tile(e, lambda bank: halves(bank, lambda n: [
                    (h[:, :], x) for k, h in enumerate((had_p, (had_p, had_n)[n])) for x in x_parts(k, tokens(b))]))

            for e in TAIL:
                stage, b, _ = e
                if stage in HEAD_PIECES:
                    head_piece(PAIRS - 1, e)
                elif stage in ("ln1", "ln2", "ln3"):
                    pe.wait_ge(ln_done, BATCH + NORM["norm" + stage[2], b, 0] + 1)
                    rot_tile(e, lambda bank: ln_transposes(bank, normed[b]))
                elif stage in ("gu0", "gu1"):
                    pe.wait_ge(prep_q8, PAIRS)
                    pe.wait_ge(prep_pool, PAIRS)
                    gate_up(e)
                elif stage in ("down0", "down1"):
                    down(e)
                elif stage == "proj":
                    qkv1(e)
                elif stage in ("score", "score2"):
                    scores1(e)
                elif stage in ("pturn", "pturn2"):
                    turn1(e)
                elif stage in ("ctx", "mix"):
                    values1(e)
                elif stage == "proj_out":
                    out1(e)
                elif stage == "had":
                    hadamard(e)

        @block.scalar
        def _(act):
            def copy(dst, src, **kw):
                return nc.scalar.activation(dst, src, ACT.Copy, **kw)

            def proj_part(half, n, number):
                act.wait_ge(proj_ready, number + 1)
                copy(proj_dst(True, half, n), proj_src(n)).then_inc(proj_hi, 1)

            def exps(i, j):
                act.wait_ge(nbias_done, i * UNITS + j + 1)
                bank = bank_s[j % 2]
                for dst, src, qt in ((prob[:, j % 2, 0:P], bank[:, 0:P], 0),
                                     (prob[:, j % 2, P:3 * P], bank[:, SEQ:2 * SEQ], 1)):
                    a = nc.scalar.activation(dst, src, ACT.Exp, bias=nbias[:, j, qt:qt + 1], scale=INV_SQRT_DH,
                                             accum_out=rsum[:, j, qt:qt + 1])
                a.then_inc(exp_done, 1)

            def head_piece(i, piece):
                name, s, k = piece
                if name == "values":
                    act.wait_ge(z_ready, i * UNITS + s - 2)
                    copy(z_hi[:, (s - 3) % 2, :], bank_z[(s - 3) % 2][:, 0:SEQ]).then_inc(zhi_done, 1)
                elif name == "turn":
                    act.wait_ge(t_ready, i * UNITS + s - 1)
                    copy(pt_hi[:, s % 2, 1:4, :], bank_t[:, 0:3 * P].rearrange("p (a c) -> p a c", a=3))\
                        .then_inc(t_hi, 1)
                elif name == "scores":
                    exps(i, s)
                elif name == "ughi":
                    act.wait_ge(loaded_prep, 16 * (i + 1))
                    copy(ug_hi[:, i, :], prep[:, 0:UG_PIECE]).then_inc(ug_hi_done, 1)
                elif name == "tile":
                    half, n, number = tile_at(s, k)
                    proj_part(half, n, i * TPP + number)

            def first_hi(b):
                act.wait_ge(lnt_ready, b + 1)
                copy(xt_hi[:, :, tokens(b)], two((bank_s + bank_z)[b][:, :])).then_inc(lnt_hi, 1)

            first_hi(0)
            first_hi(1)
            act.wait_ge(loaded_ident, 16)
            act.wait_ge(loaded_const, 16 * N_CONST)
            copy(ident_b[:, :], ident[:, :])
            copy(had_p[:, :], prob[:, 0, 0:P])
            copy(had_n[:, :], prob[:, 0, P:2 * P])
            copy(mask_b[:, :], prob[:, 0, 2 * P:3 * P]).then_inc(consts_ready, 1)
            for n in range(CH):
                proj_part(0, n, n)
                if n == 3:
                    first_hi(2)
                    first_hi(3)
            act.wait_ge(cam_arg, 1)
            nc.scalar.activation(cam[:, 1:2], cam[:, 0:1], ACT.Exp, scale=-1.0).then_inc(cam_exp, 1)
            for s in range(UNITS):
                for piece in pieces(s, prev=False):
                    head_piece(0, piece)
            with act.Fori(1, PAIRS - 1) as i:
                for s in range(UNITS):
                    for piece in pieces(s):
                        head_piece(i, piece)

            def first(e):
                act.wait_ge(rot_ready, ROT[e] + 1)
                return rot(ROT[e])

            for e in TAIL:
                stage, b, c = e
                if stage in HEAD_PIECES:
                    head_piece(PAIRS - 1, e)
                elif stage in ("ln1", "ln2", "had"):
                    copy(xt_hi[:, :, tokens(b)], two(first(e)[:, :])).then_inc(rot_hi, 1)
                elif stage == "ln3":
                    bank = first(e)
                    for k in range(KC):
                        a = copy(xt_hi[:, k, tokens(b)], bank[:, k * SEQ:(k + 1) * SEQ], scale=vec(V_SU + k))
                    a.then_inc(rot_hi, 1)
                elif stage in ("gu0", "gu1"):
                    if GU[e] == 0:
                        act.wait_ge(w_v, PAIRS + 1)
                    scale = vec(V_GS0 + c) if stage == "gu0" else wscale[:, C1 + c:C1 + c + 1]
                    nc.scalar.activation(gate_act[GU[e] % SLOTS], first(e)[:, 0:SEQ], ACT.Silu, scale=scale)\
                        .then_inc(rot_hi, 1)
                elif stage in ("hid0", "hid1"):
                    gu = "gu" + stage[3]
                    act.wait_ge(rot_free, ROT[gu, b, c] + 1)
                    copy(hidden(reg_hi, gu, b)[:, c, :], fused[GU[gu, b, c] % SLOTS]).then_inc(fuse_hi, 1)
                elif stage == "proj" and c < 2:
                    bank = first(e)
                    for n in range(2):
                        a = nc.scalar.activation(attn1(reg_hi, b)[c][:, n, :], bank[:, n * SEQ:(n + 1) * SEQ],
                                                 ACT.Identity, bias=vec(V_BQK + 2 * c + n))
                    a.then_inc(rot_hi, 1)
                elif stage == "vsplit":
                    act.wait_ge(rot_free, ROT["proj", b, 2] + 1)
                    copy(attn1(reg_hi, b)[2], v_sum).then_inc(v_hi_done, 1)
                elif stage in ("score", "score2"):
                    n = SOFT[e]
                    act.wait_ge(nbias_done, ALL_UNITS + n + 1)
                    for qt in range(2):
                        ts = slice(qt * SEQ, (qt + 1) * SEQ)
                        a = nc.scalar.activation(prob[:, n % 2, ts], bank_z[n % 2][:, ts], ACT.Exp, scale=SCALE1,
                                                 bias=nbias[:, UNITS + n, qt:qt + 1],
                                                 accum_out=rsum[:, UNITS + n, qt:qt + 1])
                    a.then_inc(exp_done, 1)
                elif stage in ("pturn", "pturn2"):
                    m = TURN[e]
                    act.wait_ge(t_ready, ALL_UNITS + m + 1)
                    copy(pt_hi[:, m % 2, :, :], bank_t[:, :].rearrange("p (a c) -> p a c", a=4)).then_inc(t_hi, 1)
                elif stage == "ctx":
                    nc.scalar.activation(cam_tanh, first(e)[:, 0:SEQ], ACT.Tanh, scale=vec(V_CAMG)).then_inc(rot_hi, 1)
                elif stage == "camq":
                    act.wait_ge(camq_sum, b + 1)
                    copy(attn1(reg_hi, b)[0][:, 0, :], cam_total).then_inc(camq_hi, 1)
                elif stage == "mix":
                    copy(z_hi[:, :, :], two(first(e)[:, :])).then_inc(rot_hi, 1)

        @block.vector
        def _(v):
            taken = [0]

            def step(ins):
                taken[0] += 1
                ins.then_inc(dve, 1)
                v.wait_ge(dve, taken[0])

            def lo(dst, src, hi):
                return nc.vector.tensor_tensor(dst, src, f32(hi), ALU.subtract)

            def ln_stats(t0, nt):
                sl = slice(t0, t0 + nt)
                for t in range(t0, t0 + nt):
                    a = nc.vector.bn_stats(stats[:, t, :], xres[:, t, :])
                step(a)
                for t in range(t0, t0 + nt):
                    a = nc.vector.bn_aggr(mv[:, t, :], stats[:, t, :])
                step(a)
                return ln_guess(t0, nt)

            def ln_guess(t0, nt):
                sl = slice(t0, t0 + nt)
                step(nc.vector.tensor_scalar(nwt[:, 0, sl], mv[:, sl, 1], EPS, None, ALU.add))
                return nc.vector.tensor_scalar(nwt[:, 1, sl].bitcast(I32), nwt[:, 0, sl].bitcast(I32), -0.5, 0x5F3759DF,
                                               ALU.mult, ALU.add)

            def ln_apply(tok, b):
                for t in range(2):
                    tile = 2 * b + t
                    a = nc.vector.tensor_scalar(tok[:, t, :], xres[:, tile, :], mv[:, tile, 0:1],
                                                nwt[:, 1, tile:tile + 1], ALU.subtract, ALU.mult)
                a.then_inc(ln_done, 1)

            def proj_part(half, n, number):
                v.wait_ge(proj_hi, number + 1)
                lo(proj_dst(False, half, n), proj_src(n), proj_dst(True, half, n)).then_inc(proj_split, 1)

            def maxima(i, j):
                v.wait_ge(s_ready, i * UNITS + j + 1)
                bank = bank_s[j % 2]
                nc.vector.reduce_max(rmax[:, j, 0:1], bank[:, 0:P], AX_X)
                nc.vector.reduce_max(rmax[:, j, 1:2], bank[:, SEQ:2 * SEQ], AX_X).then_inc(max_done, 1)
                v.wait_ge(max_done, i * UNITS + j + 1)
                nc.vector.tensor_scalar(nbias[:, j, :], rmax[:, j, :], -INV_SQRT_DH, None, ALU.mult)\
                    .then_inc(nbias_done, 1)

            def fp8_round(i, s):
                w = prep[:, UG_PIECE + WD_PIECE:PREP_COLS]
                bits, bits_w = q8_pow[:, :].bitcast(I32), w.bitcast(I32)

                def done(n):
                    v.wait_ge(q8_step, i * 7 + n)

                if s == 1:
                    v.wait_ge(loaded_prep, 16 * (i + 1))
                    nc.vector.tensor_scalar(bits, bits_w, 0x7F800000, None, ALU.bitwise_and).then_inc(q8_step, 1)
                    done(1)
                    nc.vector.tensor_scalar(q8_pow[:, :], q8_pow[:, :], FP8_MIN_NORMAL, ROUND_TO_4_BITS,
                                            ALU.max, ALU.mult).then_inc(q8_step, 1)
                elif s == 2:
                    done(2)
                    nc.vector.tensor_tensor(w, w, q8_pow[:, :], ALU.add).then_inc(q8_step, 1)
                elif s == 3:
                    done(3)
                    nc.vector.tensor_tensor(w, w, q8_pow[:, :], ALU.subtract).then_inc(q8_step, 1)
                elif s == 4:
                    done(4)
                    nc.vector.tensor_scalar(bits, bits_w, 0x7FFFFFFF, None, ALU.bitwise_and).then_inc(q8_step, 1)
                    done(5)
                    nc.vector.tensor_scalar(q8_pow[:, :], q8_pow[:, :], FP8_MAX, 3e38, ALU.is_gt, ALU.mult)\
                        .then_inc(q8_step, 1)
                elif s == 6:
                    done(6)
                    nc.vector.tensor_scalar(q8_pow[:, :], q8_pow[:, :], 3e38, 0.0, ALU.mult, ALU.mult)\
                        .then_inc(q8_step, 1)
                elif s == 7:
                    done(7)
                    nc.vector.tensor_tensor(q8[:, i, :], q8_pow[:, :], w, ALU.add).then_inc(prep_q8, 1)

            def wd_piece(i):
                signed = bfly[:, 0, :].rearrange("p (c m) -> p c m", c=C1)
                v.wait_ge(wdmm_ready, i + 1)
                nc.vector.tensor_tensor(signed, bank_o[:, 0:WD_PIECE].rearrange("p (c m) -> p c m", c=C1),
                                        vec(V_SUDP, C1).unsqueeze(2).broadcast_to([P, C1, DCOLS]), ALU.mult)\
                    .then_inc(o_added, 1)
                v.wait_ge(o_added, i * OPP + 2)
                nc.vector.tensor_copy(wd_hi[:, :, i, :], signed).then_inc(wd_done, 1)
                v.wait_ge(wd_done, 2 * i + 1)
                lo(wd_lo[:, :, i, :], signed, wd_hi[:, :, i, :]).then_inc(wd_done, 1)

            def head_piece(i, piece):
                name, s, k = piece
                if name == "values":
                    v.wait_ge(zhi_done, i * UNITS + s - 2)
                    lo(z_lo[:, (s - 3) % 2, :], bank_z[(s - 3) % 2][:, 0:SEQ], z_hi[:, (s - 3) % 2, :])\
                        .then_inc(z_split, 1)
                elif name == "turn":
                    v.wait_ge(t_hi, i * UNITS + s - 1)
                    lo(pt_lo[:, s % 2, 1:4, :], bank_t[:, 0:3 * P].rearrange("p (a c) -> p a c", a=3),
                       pt_hi[:, s % 2, 1:4, :]).then_inc(t_split, 1)
                elif name == "scores":
                    maxima(i, s)
                elif name == "out":
                    b = (s - 5) // 2 % BATCH
                    v.wait_ge(o_ready, i * BATCH + OUT_DONE[s])
                    nc.vector.tensor_tensor(xres[:, 2 * b:2 * b + 2, :], two(bank_o[:, :]),
                                            xres[:, 2 * b:2 * b + 2, :], ALU.add).then_inc(o_added, 1)
                elif name == "hwd":
                    wd_piece(i)
                elif name == "round":
                    fp8_round(i, s)
                elif name == "sums":
                    v.wait_ge(exp_done, i * UNITS + s + 1)
                    nc.vector.reciprocal(rinv[:, s, :], rsum[:, s, :]).then_inc(rinv_done, 1)
                elif name == "tile":
                    half, n, number = tile_at(s, k)
                    proj_part(half, n, i * TPP + number)

            def first_stats(b):
                v.wait_ge(loaded_x[b], 16)
                for t in (2 * b, 2 * b + 1):
                    a = nc.vector.bn_stats(stats[:, t, :], xres[:, t, :])
                if b % 2 == 1:
                    step(a)

            def first_guess(b):
                for t in range(2 * b, 2 * b + 4):
                    a = nc.vector.bn_aggr(mv[:, t, :], stats[:, t, :])
                step(a)
                step(ln_guess(2 * b, 4))

            def first_newton(b, steps):
                ve, y, tmp = (nwt[:, n, 2 * b:2 * b + 4] for n in range(3))
                for _ in range(steps):
                    step(nc.vector.tensor_tensor(tmp, y, y, ALU.mult))
                    step(nc.vector.scalar_tensor_tensor(out=tmp, in0=tmp, scalar=-0.5, in1=ve, op0=ALU.mult, op1=ALU.mult))
                    step(nc.vector.scalar_tensor_tensor(out=y, in0=tmp, scalar=1.5, in1=y, op0=ALU.add, op1=ALU.mult))

            def first_lo(b):
                v.wait_ge(lnt_hi, b + 1)
                lo(xt_lo[:, :, tokens(b)], two((bank_s + bank_z)[b][:, :]), xt_hi[:, :, tokens(b)])\
                    .then_inc(lnt_split, 1)

            first_stats(0)
            first_stats(1)
            first_guess(0)
            first_newton(0, 3)
            ln_apply(xn[:, 0], 0)
            ln_apply(xn[:, 1], 1)
            first_stats(2)
            first_lo(0)
            first_lo(1)
            first_stats(3)
            first_guess(2)
            first_newton(2, 1)
            proj_part(0, 0, 0)
            first_newton(2, 2)
            v.wait_ge(lnt_ready, 2)
            proj_part(0, 1, 1)
            ln_apply(xn[:, 0], 2)
            ln_apply(xn[:, 1], 3)
            proj_part(0, 2, 2)
            proj_part(0, 3, 3)
            first_lo(2)
            first_lo(3)
            v.wait_ge(loaded_const, 16 * N_CONST)
            nc.vector.scalar_tensor_tensor(out=cam[:, 0:1], in0=vec(V_W1), scalar=0.5, in1=vec(V_W0),
                                           op0=ALU.mult, op1=ALU.add).then_inc(cam_arg, 1)
            for n in range(4, CH):
                proj_part(0, n, n)
            for s in range(UNITS):
                for piece in pieces(s, prev=False):
                    head_piece(0, piece)
                if s == 5:
                    v.wait_ge(cam_exp, 1)
                    step(nc.vector.tensor_scalar(cam[:, 2:3], cam[:, 1:2], 1.0, None, ALU.add))
                    step(nc.vector.reciprocal(cam[:, 3:4], cam[:, 2:3]))
                    step(nc.vector.tensor_scalar(wscale[:, :], vec(V_WUP, 2 * C1), 1.0 / 16, None, ALU.mult))
            with v.Fori(1, PAIRS - 1) as i:
                for s in range(UNITS):
                    for piece in pieces(s):
                        head_piece(i, piece)

            def onto(e):
                stage, b, _ = e
                v.wait_ge(o_ready, PAIRS * BATCH + ONTO[e] + 1)
                res, got, tmp = xres[:, 2 * b:2 * b + 2, :], two(bank_o[:, :]), bfly[:, :, :]
                if stage == "down0":
                    a = nc.vector.tensor_tensor(tmp, got, row(R_DS, 2), ALU.mult)
                elif stage == "proj_out":
                    a = nc.vector.tensor_tensor(tmp, got, row(R_PB, 2), ALU.add)
                else:
                    if b >= 1:
                        v.wait_ge(x_final, b)
                    a = nc.vector.scalar_tensor_tensor(out=tmp, in0=got, scalar=1.0 / 32, in1=row(R_WDP, 2),
                                                       op0=ALU.mult, op1=ALU.mult)
                a.then_inc(o_added, 1)
                v.wait_ge(o_added, PAIRS * OPP + ONTO[e] + 1)
                nc.vector.tensor_tensor(res, tmp, res, ALU.add).then_inc(x_final if stage == "down1" else x_added, 1)

            def rest(e):
                v.wait_ge(rot_hi, HI[e] + 1)
                return rot(ROT[e])

            v.wait_ge(loaded_rows, 16)
            for e in TAIL:
                stage, b, c = e
                if stage in HEAD_PIECES:
                    head_piece(PAIRS - 1, e)
                elif stage in ("stats1", "stats2", "stats3"):
                    if stage == "stats1":
                        v.wait_ge(o_added, (PAIRS - 1) * OPP + OUT_USES[5 + 2 * b] + 1)
                    else:
                        v.wait_ge(x_added, ADDED["down0" if stage == "stats2" else "proj_out", b, 0] + 1)
                    ln_stats(2 * b, 2).then_inc(stats_done, 1)
                elif stage in ("norm1", "norm2", "norm3"):
                    v.wait_ge(root_done, ROOT["root" + stage[4], b, 0] + 1)
                    if e == ("norm1", 2, 0):
                        v.wait_ge(prep_pool, PAIRS)
                    ln_apply(normed[b], b)
                elif stage in ("ln1", "ln2", "had"):
                    lo(xt_lo[:, :, tokens(b)], two(rest(e)[:, :]), xt_hi[:, :, tokens(b)]).then_inc(rot_free, 1)
                elif stage == "ln3":
                    bank = rest(e)
                    for k in range(KC):
                        a = nc.vector.scalar_tensor_tensor(
                            out=xt_lo[:, k, tokens(b)], in0=bank[:, k * SEQ:(k + 1) * SEQ], scalar=vec(V_SU + k),
                            in1=f32(xt_hi[:, k, tokens(b)]), op0=ALU.mult, op1=ALU.subtract)
                    a.then_inc(rot_free, 1)
                elif stage in ("gu0", "gu1"):
                    g = GU[e]
                    if g >= SLOTS:
                        v.wait_ge(fuse_lo, g - SLOTS + 1)
                    scale = vec(V_US0 + c) if stage == "gu0" else wscale[:, c:c + 1]
                    nc.vector.scalar_tensor_tensor(out=fused[g % SLOTS], in0=rest(e)[:, SEQ:2 * SEQ], scalar=scale,
                                                   in1=gate_act[g % SLOTS], op0=ALU.mult, op1=ALU.mult)\
                        .then_inc(rot_free, 1)
                elif stage in ("down0", "proj_out", "down1"):
                    onto(e)
                elif stage == "proj" and c < 2:
                    bank, hi, low = rest(e), attn1(reg_hi, b)[c], attn1(reg_lo, b)[c]
                    for n in range(2):
                        a = nc.vector.scalar_tensor_tensor(
                            out=low[:, n, :], in0=bank[:, n * SEQ:(n + 1) * SEQ], scalar=vec(V_BQK + 2 * c + n),
                            in1=f32(hi[:, n, :]), op0=ALU.add, op1=ALU.subtract)
                    a.then_inc(rot_free, 1)
                elif stage == "proj":
                    v.wait_ge(rot_ready, ROT[e] + 1)
                    if b == 0:
                        v.wait_ge(w_o, PAIRS + 1)
                    else:
                        v.wait_ge(v_split, b)
                    nc.vector.tensor_tensor(v_sum, two(rot(ROT[e])[:, :]), row(R_VB, 2), ALU.add)\
                        .then_inc(rot_free, 1)
                elif stage == "vsplit":
                    v.wait_ge(v_hi_done, b + 1)
                    lo(attn1(reg_lo, b)[2], v_sum, attn1(reg_hi, b)[2]).then_inc(v_split, 1)
                elif stage in ("score", "score2"):
                    n = SOFT[e]
                    m = UNITS + n
                    v.wait_ge(s_ready, ALL_UNITS + n + 1)
                    nc.vector.reduce_max(rmax[:, m, :], two(bank_z[n % 2][:, :]), AX_X).then_inc(max_done, 1)
                    v.wait_ge(max_done, ALL_UNITS + n + 1)
                    nc.vector.tensor_scalar(nbias[:, m, :], rmax[:, m, :], -SCALE1, None, ALU.mult)\
                        .then_inc(nbias_done, 1)
                elif stage in ("sum", "sum2"):
                    n = SOFT["score" + stage[3:], b, 0]
                    v.wait_ge(exp_done, ALL_UNITS + n + 1)
                    nc.vector.reciprocal(rinv[:, UNITS + n, :], rsum[:, UNITS + n, :]).then_inc(rinv_done, 1)
                elif stage in ("pturn", "pturn2"):
                    m = TURN[e]
                    v.wait_ge(t_hi, ALL_UNITS + m + 1)
                    lo(pt_lo[:, m % 2, :, :], bank_t[:, :].rearrange("p (a c) -> p a c", a=4), pt_hi[:, m % 2, :, :])\
                        .then_inc(t_split, 1)
                elif stage == "ctx":
                    q0_hi, q0_lo = (attn1(r, b)[0][:, 0, :] for r in (reg_hi, reg_lo))
                    rest(e)
                    if b >= 1:
                        v.wait_ge(camq_split, b)
                    nc.vector.scalar_tensor_tensor(out=cam_total, in0=cam_tanh, scalar=cam[:, 3:4],
                                                   in1=f32(q0_hi), op0=ALU.mult, op1=ALU.add).then_inc(rot_free, 1)
                    v.wait_ge(rot_free, ROT[e] + 1)
                    nc.vector.tensor_tensor(cam_total, cam_total, f32(q0_lo), ALU.add).then_inc(camq_sum, 1)
                elif stage == "camq":
                    q0_hi, q0_lo = (attn1(r, b)[0][:, 0, :] for r in (reg_hi, reg_lo))
                    v.wait_ge(camq_hi, b + 1)
                    lo(q0_lo, cam_total, q0_hi).then_inc(camq_split, 1)
                elif stage == "mix":
                    lo(z_lo[:, :, :], two(rest(e)[:, :]), z_hi[:, :, :]).then_inc(rot_free, 1)

        @block.gpsimd
        def _(pool):
            def hi(dst, src):
                return nc.gpsimd.tensor_scalar(dst, src, 1.0, 1.0, ALU.mult, ALU.mult)

            def lo(dst, src, hi_part):
                return nc.gpsimd.tensor_tensor(dst, src, f32(hi_part), ALU.subtract)

            def raw_qkv(which):
                return qkv_raw[:, which * 2 * D:(which + 1) * 2 * D].rearrange("p (k m) -> p k m", k=KC)

            def raw_wo():
                return wo_raw[:, :].rearrange("p (h m) -> p h m", h=2)

            def wait(s, value):
                pool.wait_ge(s, value)
                pool.sem_inc(pool_went, 1)

            def butterfly(dst, src, d):
                s, t = (x.rearrange("p (g a x) -> p g a x", a=2, x=d * DCOLS) for x in (src, dst))
                nc.gpsimd.tensor_tensor(t[:, :, 0, :], s[:, :, 0, :], s[:, :, 1, :], ALU.add)
                return nc.gpsimd.tensor_tensor(t[:, :, 1, :], s[:, :, 0, :], s[:, :, 1, :], ALU.subtract)

            def head_piece(i, piece, prev=True):
                name, s, _ = piece

                def pstep(ins, n):
                    ins.then_inc(pool_step, 1)
                    wait(pool_step, i * 7 + n)

                def split_w(which, n):
                    if which == 0:
                        wait(loaded_qkv, 16 * (i + 1))
                    wait(proj_ready, i * TPP + CH + 2 * which + 2)
                    pstep(hi(wqkv_hi[:, which, :, :], raw_qkv(which)), n)
                    lo(wqkv_lo[:, which, :, :], raw_qkv(which), wqkv_hi[:, which, :, :])\
                        .then_inc((w_q, w_k, w_v)[which], 1)

                if name == "sums":
                    wait(rinv_done, i * UNITS + s + 1)
                    nc.gpsimd.tensor_scalar(probn[:, s % 2, 0:P], prob[:, s % 2, 0:P], rinv[:, s, 0:1], 1.0,
                                            ALU.mult, ALU.mult)
                    nc.gpsimd.tensor_scalar(probn[:, s % 2, P:3 * P], prob[:, s % 2, P:3 * P], rinv[:, s, 1:2], 1.0,
                                            ALU.mult, ALU.mult).then_inc(norm_done, 1)
                if name != "split":
                    return
                if s == 1:
                    split_w(0, 1)
                    wait(loaded_prep, 16 * (i + 1))
                    pstep(butterfly(bfly[:, 0, 0:WD_PIECE], prep[:, UG_PIECE:UG_PIECE + WD_PIECE], 1), 2)
                elif s == 2:
                    pstep(butterfly(bfly[:, 1, 0:WD_PIECE], bfly[:, 0, 0:WD_PIECE], 2), 3)
                    split_w(1, 4)
                elif s == 3:
                    if prev:
                        wait(o_ready, i * BATCH)
                        split_wo(i)
                    pstep(butterfly(bfly[:, 0, 0:WD_PIECE], bfly[:, 1, 0:WD_PIECE], 4), 5)
                elif s == 4:
                    split_w(2, 6)
                    pstep(hi(bf_hi[:, :], bfly[:, 0, 0:WD_PIECE]), 7)
                    lo(bf_lo[:, :], bfly[:, 0, 0:WD_PIECE], bf_hi[:, :]).then_inc(bf_ready, 1)
                elif s == 5:
                    wait(ug_hi_done, i + 1)
                    lo(ug_lo[:, i, :], prep[:, 0:UG_PIECE], ug_hi[:, i, :]).then_inc(prep_pool, 1)

            def split_wo(i):
                wait(loaded_wo, 16 * (i + 1))
                hi(wo_hi[:, :, :], raw_wo()).then_inc(wo_hi_done, 1)
                wait(wo_hi_done, i + 1)
                lo(wo_lo[:, :, :], raw_wo(), wo_hi[:, :, :]).then_inc(w_o, 1)

            for r in (pt_hi, pt_lo):
                a = nc.gpsimd.memset(f32(r[:, :, 0, :]), 0.0)
            a.then_inc(zeros_ready, 1)
            for which in range(3):
                pool.wait_ge(loaded_first[which], 16)
                hi(wqkv_hi[:, which, :, :], raw_qkv(which)).then_inc(pool_first, 1)
                pool.wait_ge(pool_first, which + 1)
                lo(wqkv_lo[:, which, :, :], raw_qkv(which), wqkv_hi[:, which, :, :])\
                    .then_inc((w_q, w_k, w_v)[which], 1)
            split_wo(0)
            for s in range(UNITS):
                for piece in pieces(s, prev=False):
                    head_piece(0, piece, prev=False)
            with pool.Fori(1, PAIRS - 1) as i:
                for s in range(UNITS):
                    for piece in pieces(s):
                        head_piece(i, piece)

            steps = 0
            for e in TAIL:
                stage, b, c = e
                if stage in HEAD_PIECES:
                    head_piece(PAIRS - 1, e)
                elif stage == "wosplit":
                    pool.wait_ge(o_ready, PAIRS * BATCH)
                    split_wo(PAIRS)
                elif stage in ("root1", "root2", "root3"):
                    n = STATS["stats" + stage[4], b, 0]
                    ve, y, tmp = (nwt[:, k, 2 * b:2 * b + 2] for k in range(3))
                    pool.wait_ge(stats_done, n + 1)
                    for k in range(3):
                        for ins in (lambda: nc.gpsimd.tensor_tensor(tmp, y, y, ALU.mult),
                                    lambda: nc.gpsimd.tensor_tensor(tmp, tmp, ve, ALU.mult),
                                    lambda: nc.gpsimd.tensor_scalar(tmp, tmp, -0.5, 1.5, ALU.mult, ALU.add)):
                            ins().then_inc(newton, 1)
                            steps += 1
                            pool.wait_ge(newton, steps)
                        a = nc.gpsimd.tensor_tensor(y, y, tmp, ALU.mult)
                        if k < 2:
                            a.then_inc(newton, 1)
                            steps += 1
                            pool.wait_ge(newton, steps)
                    a.then_inc(root_done, 1)
                elif stage in ("sum", "sum2"):
                    n = SOFT["score" + stage[3:], b, 0]
                    pool.wait_ge(rinv_done, ALL_UNITS + n + 1)
                    for qt in range(2):
                        ts = slice(qt * SEQ, (qt + 1) * SEQ)
                        a = nc.gpsimd.tensor_scalar(probn[:, n % 2, ts], prob[:, n % 2, ts],
                                                    rinv[:, UNITS + n, qt:qt + 1], 1.0, ALU.mult, ALU.mult)
                    a.then_inc(norm_done, 1)
                elif stage in ("hid0", "hid1"):
                    gu = "gu" + stage[3]
                    g = GU[gu, b, c]
                    pool.wait_ge(fuse_hi, g + 1)
                    lo(hidden(reg_lo, gu, b)[:, c, :], fused[g % SLOTS], hidden(reg_hi, gu, b)[:, c, :])\
                        .then_inc(fuse_lo, 1)


def kernel(L0_attn_x, L0_attn_W_K, L0_attn_W_Q, L0_attn_W_V, L0_attn_W_O, L0_ffn_gate_w, L0_ffn_up_w, L0_ffn_down_w,
           L0_ffn_gate_scale, L0_ffn_up_scale, L0_ffn_down_scale, L1_attn_c_attn_w, L1_attn_c_attn_b,
           L1_attn_c_proj_w, L1_attn_c_proj_b, L1_attn_cam_gate, L1_attn_cam_w0, L1_attn_cam_w1, L1_ffn_SU_ug,
           L1_ffn_SU_dp, L1_ffn_Wscale_ug, L1_ffn_Wscale_dp, L1_ffn_W_up, L1_ffn_W_gate, L1_ffn_W_down):
    args_by_name = dict(locals())
    import numpy as np
    import concourse.bacc as bacc
    from concourse import mybir as mb
    from concourse.bass_utils import run_bass_kernel_spmd

    a = {k: np.asarray(x) for k, x in args_by_name.items()}

    def chunks(w):
        return w.reshape(-1, P, w.shape[-1]).transpose(1, 0, 2)

    def pair_qkv(w):
        w = w.reshape(PAIRS, 2 * DH, KC, P).transpose(0, 3, 2, 1)
        return w.reshape(PAIRS, P, -1)

    wo = a["L0_attn_W_O"].T.reshape(PAIRS, 2, P, D).transpose(0, 2, 1, 3).reshape(PAIRS, P, -1)
    pairs = np.concatenate([pair_qkv(a["L0_attn_W_Q"]), pair_qkv(a["L0_attn_W_K"]), pair_qkv(a["L0_attn_W_V"]), wo], -1)
    c_attn = chunks(a["L1_attn_c_attn_w"]).reshape(P, KC, 3, D).transpose(0, 2, 1, 3).reshape(P, -1)
    c_proj = chunks(a["L1_attn_c_proj_w"]).reshape(P, -1)
    pairs = np.concatenate([pairs, np.concatenate([c_attn, c_proj], -1)[None]], 0)

    up, gate = (chunks(a["L1_ffn_W_" + n].T).reshape(P, KC, C1, P) for n in ("up", "gate"))
    ug = np.stack([gate, up], 3).reshape(P, PAIRS, UG_PIECE).transpose(1, 0, 2)
    wd = chunks(a["L1_ffn_W_down"].T).reshape(P, C1, PAIRS, DCOLS).transpose(2, 0, 1, 3).reshape(PAIRS, P, -1)
    q8 = np.concatenate([chunks(a["L0_ffn_" + n]).reshape(P, -1) for n in ("gate_w", "up_w", "down_w")], -1)
    q8 = q8.reshape(P, PAIRS, Q8_PIECE).transpose(1, 0, 2)
    prep = np.concatenate([ug, wd, q8], -1)

    had = np.ones((1, 1), np.float32)
    while len(had) < P:
        had = np.block([[had, had], [had, -had]])
    mask = np.where(np.arange(P)[None, :] > np.arange(P)[:, None], np.float32(MASKED), np.float32(0))
    mats = np.concatenate([np.eye(P, dtype=np.float32), had, -had, mask], 1).astype(np.float32)

    def cols(x):
        return x.reshape(-1, P).T

    vecs = np.concatenate(
        [cols(a["L1_attn_c_attn_b"][:2 * D]), cols(a["L1_ffn_SU_ug"]), cols(a["L1_ffn_SU_dp"]),
         cols(a["L0_ffn_gate_scale"]), cols(a["L0_ffn_up_scale"]), cols(a["L1_ffn_Wscale_ug"]),
         cols(a["L1_attn_cam_gate"]), np.repeat(a["L1_attn_cam_w0"][None], P, 0),
         np.repeat(a["L1_attn_cam_w1"][None], P, 0)], 1)
    rows = np.stack([a["L0_ffn_down_scale"], a["L1_attn_c_attn_b"][2 * D:], a["L1_attn_c_proj_b"],
                     a["L1_ffn_Wscale_dp"]], 0)
    rows = np.repeat(rows[None], P, 0)

    arrays = {n: np.ascontiguousarray(x) for n, x in (
        ("x", a["L0_attn_x"]), ("pairs", pairs), ("prep", prep), ("mats", mats), ("vecs", vecs), ("rows", rows))}
    nc = bacc.Bacc("TRN2", target_bir_lowering=False, num_devices=1)
    args = [nc.dram_tensor(f"in_{n}", x.shape, mb.dt.from_np(x.dtype), kind="ExternalInput").ap()
            for n, x in arrays.items()]
    out = nc.dram_tensor("out", (BATCH, SEQ, D), mb.dt.float32, kind="ExternalOutput").ap()
    build_program(nc, *args, out)
    r = run_bass_kernel_spmd(nc, [{f"in_{n}": x for n, x in arrays.items()}], core_ids=[0])
    return r.results[0]["out"]
```
